# Optimizing a Trainium2 kernel written in Bass

```python
import numpy as np
import jax
import jax.numpy as jnp

def _softmax(x, axis=-1):
    return jax.nn.softmax(x, axis=axis)

def _gelu(x):
    return jax.nn.gelu(x, approximate=True)

def _silu(x):
    return jax.nn.silu(x)

def _sigmoid(x):
    return jax.nn.sigmoid(x)

def _layernorm(x, axis=-1, eps=1e-05):
    m = jnp.mean(x, axis=axis, keepdims=True)
    v = jnp.var(x, axis=axis, keepdims=True)
    return (x - m) / jnp.sqrt(v + eps)

def _scatter_add(tgt, idx, src, axis=0):
    return tgt.at[idx].add(src)

def _segment_sum(src, seg, n):
    return jax.ops.segment_sum(src, seg, n)
kernel_name = 'mk_perceiver_d1_seqx_r4_71f5f1'

def setup_inputs(seed: int=0):
    np.random.seed(seed)
    _w = jnp.asarray

    def _rec_inputs():
        import jax
        import jax.numpy as jnp
        _rk = jax.random.key(seed)
        x = -0.0005146 + 1 * jax.random.normal(jax.random.fold_in(_rk, 1), (8, 64, 1024), jnp.float32)
        _lenS = 64 - jax.random.randint(jax.random.fold_in(_rk, 7), (8,), 0, max(1, 64 // 4) + 1, jnp.int32)
        _lenS2 = 1024 - jax.random.randint(jax.random.fold_in(_rk, 8), (8,), 0, max(1, 1024 // 4) + 1, jnp.int32)
        _ctx_4096P = jax.random.normal(jax.random.fold_in(_rk, 11), (8, 16, 1024), jnp.float32)
        _ctx_4096c = jax.random.dirichlet(jax.random.fold_in(_rk, 511), 0.3 * jnp.ones((16,), jnp.float32), (8, 1024))
        _ctx_4096t = jnp.einsum('bsk,bkd->bsd', _ctx_4096c, _ctx_4096P)
        _ctx_4096t = _ctx_4096t * jax.lax.rsqrt(jnp.mean(jnp.square(_ctx_4096t)) + 1e-12) * 0.953939
        ctx_4096 = -0.0142356 + 1.00583 * (_ctx_4096t + 0.3 * jax.random.normal(jax.random.fold_in(_rk, 611), (8, 1024, 1024), jnp.float32))
        return (x, ctx_4096)
    x, ctx_4096 = _rec_inputs()

    def _L0_xattn_setup():
        import jax, jax.numpy as jnp
        import numpy as np
        K = 10
        NUM_BITS = 10
        M_METHODS = 4

        def _quantize(coords, num_bits=NUM_BITS):
            cmin = coords.min(axis=1, keepdims=True)
            cmax = coords.max(axis=1, keepdims=True)
            scale = (2 ** num_bits - 1) / (cmax - cmin + 1e-06)
            q = jnp.floor((coords - cmin) * scale)
            return jnp.clip(q, 0, 2 ** num_bits - 1).astype(jnp.int32)

        def _morton_key(q):
            x, y, z = (q[..., 0], q[..., 1], q[..., 2])
            key = jnp.zeros(x.shape, dtype=jnp.int32)
            for b in range(NUM_BITS):
                key = key | (x >> b & 1) << 3 * b + 2 | (y >> b & 1) << 3 * b + 1 | (z >> b & 1) << 3 * b
            return key

        def _hilbert_key(q, num_bits=NUM_BITS):
            n = 3
            X = [q[..., i] for i in range(n)]
            M = 1 << num_bits - 1
            Q = M
            while Q > 1:
                P = Q - 1
                for i in range(n):
                    cond = X[i] & Q > 0
                    t = (X[0] ^ X[i]) & P
                    new_X0 = jnp.where(cond, X[0] ^ P, X[0] ^ t)
                    if i != 0:
                        X[i] = jnp.where(cond, X[i], X[i] ^ t)
                    X[0] = new_X0
                Q >>= 1
            for i in range(1, n):
                X[i] = X[i] ^ X[i - 1]
            t = jnp.zeros_like(X[0])
            Q = M
            while Q > 1:
                t = jnp.where(X[n - 1] & Q > 0, t ^ Q - 1, t)
                Q >>= 1
            X = [xi ^ t for xi in X]
            key = jnp.zeros(X[0].shape, dtype=jnp.int32)
            for b in range(num_bits - 1, -1, -1):
                for i in range(n):
                    key = key << 1 | X[i] >> b & 1
            return key

        def _sorted_indices(coords_bn3):
            q = _quantize(coords_bn3)
            qt = q[..., jnp.array([1, 0, 2])]
            keys = [_morton_key(q), _morton_key(qt), _hilbert_key(q), _hilbert_key(qt)]
            return [jnp.argsort(kk, axis=1) for kk in keys]

        def _window_inds(sorted_idx, k=K):
            B, N = sorted_idx.shape
            i = jnp.arange(N)
            start = jnp.maximum(0, i - k // 2)
            end = jnp.minimum(N, i + k // 2 + 1)
            pos = jnp.minimum(start[:, None] + jnp.arange(k)[None, :], (end - 1)[:, None])
            return jnp.take(sorted_idx, pos, axis=1)

        def _get_graph_features(feats, inds_list, perm, W_lin, b_lin, k=K):
            B, N, C = feats.shape
            center = feats[:, :, None, :]
            gather = jax.vmap(lambda f, idx: f[idx])
            per_method = []
            for inds in inds_list:
                neigh = gather(feats, inds)
                gf = jnp.concatenate([jnp.broadcast_to(center, (B, N, k, C)), neigh - center], axis=-1)
                per_method.append(gf)
            allf = jnp.stack(per_method, axis=-1)
            allf = allf[..., perm]
            total = 2 * C * M_METHODS
            x = allf.reshape(B * N, k, total)
            x16 = x.astype(jnp.float16).astype(jnp.float32)
            headdim = min(64, total)
            nheads = total // headdim
            qh = x16.reshape(B * N, k, nheads, headdim)
            scores = jnp.einsum('bihd,bjhd->bhij', qh, qh) / np.float32(np.sqrt(headdim))
            attn = jax.nn.softmax(scores, axis=-1)
            out = jnp.einsum('bhij,bjhd->bihd', attn, qh).reshape(B * N, k, total)
            fused = out @ W_lin.T + b_lin
            return fused.reshape(B, N, k, 128)

        def _instance_norm(x, axes):
            mu = x.mean(axis=axes, keepdims=True)
            var = x.var(axis=axes, keepdims=True)
            return (x - mu) / jnp.sqrt(var + 1e-05)

        def _lrelu(x):
            return jnp.where(x > 0, x, 0.2 * x)
        key = jax.random.key(seed)
        ks = jax.random.split(key, 8)
        B, N, C = (2, 1024, 64)
        tot = M_METHODS * 2 * C
        s = 0.02
        return {'coords': jax.random.normal(ks[0], (B, 3, N), jnp.float32), 'feats': jax.random.normal(ks[1], (B, C, N), jnp.float32), 'W_lin1': jax.random.normal(ks[2], (128, tot), jnp.float32) * s, 'b_lin1': jnp.zeros((128,), jnp.float32), 'W_lin2': jax.random.normal(ks[3], (128, tot), jnp.float32) * s, 'b_lin2': jnp.zeros((128,), jnp.float32), 'W_conv1': jax.random.normal(ks[4], (C, 2 * C), jnp.float32) * s, 'W_conv2': jax.random.normal(ks[5], (2 * C, 2 * C), jnp.float32) * s, 'W_conv3': jax.random.normal(ks[6], (C, 4 * C), jnp.float32) * s}
    _L0_xattn_all = _L0_xattn_setup()
    _L0_xattn_in = {k: v for k, v in _L0_xattn_all.items() if k in ('W_lin1', 'b_lin1', 'W_lin2', 'b_lin2', 'W_conv1', 'W_conv2', 'W_conv3')}
    del _L0_xattn_all

    def _L0_attn_setup():
        import jax, jax.numpy as jnp
        import numpy as np
        import math
        B, S, H = (1, 512, 1024)
        NH, NKV, HD = (32, 8, 128)
        GS = 128
        WBITS = 4
        ZERO = float(2 ** (WBITS - 1))
        THETA = 10000.0

        def _dequant_matmul(x, qw, scales):
            w = (qw.astype(jnp.float32) - ZERO) * jnp.repeat(scales, GS, axis=0)
            return x @ w

        def _rope_tables(seq_len, dtype):
            inv_freq = 1.0 / THETA ** (jnp.arange(0, HD, 2, dtype=jnp.float32) / HD)
            freqs = jnp.arange(seq_len, dtype=jnp.float32)[:, None] * inv_freq
            emb = jnp.concatenate([freqs, freqs], axis=-1)
            return (jnp.cos(emb).astype(dtype), jnp.sin(emb).astype(dtype))

        def _rotate_half(x):
            x1, x2 = jnp.split(x, 2, axis=-1)
            return jnp.concatenate([-x2, x1], axis=-1)

        def _apply_rope(x, cos, sin):
            return x * cos[None, None] + _rotate_half(x) * sin[None, None]
        key = jax.random.key(seed)
        ks = jax.random.split(key, 9)
        small = lambda k, shp: jax.random.uniform(k, shp, jnp.float32) * 0.01 + 0.001
        return {'hidden_states': jax.random.normal(ks[0], (B, S, H), jnp.float32), 'scales_q': small(ks[1], (H // GS, NH * HD)), 'scales_k': small(ks[2], (H // GS, NKV * HD)), 'scales_v': small(ks[3], (H // GS, NKV * HD)), 'scales_o': small(ks[4], (NH * HD // GS, H)), 'qw_q': jax.random.randint(ks[5], (H, NH * HD), 0, 2 ** WBITS, jnp.int32), 'qw_k': jax.random.randint(ks[6], (H, NKV * HD), 0, 2 ** WBITS, jnp.int32), 'qw_v': jax.random.randint(ks[7], (H, NKV * HD), 0, 2 ** WBITS, jnp.int32), 'qw_o': jax.random.randint(ks[8], (NH * HD, H), 0, 2 ** WBITS, jnp.int32)}
    _L0_attn_all = _L0_attn_setup()
    _L0_attn_in = {k: v for k, v in _L0_attn_all.items() if k in ('scales_q', 'scales_k', 'scales_v', 'scales_o', 'qw_q', 'qw_k', 'qw_v', 'qw_o')}
    del _L0_attn_all

    def _L0_ffn_setup():
        import jax, jax.numpy as jnp
        import numpy as np
        NUM_EXPERTS = 8
        RANK = 32
        ALPHA = 16.0
        TOP_K = 2
        TEMPERATURE = 1.0
        GAMMA = 0.5
        SOFT_TOPK_TEMP = 0.5
        N_GRAM = 2
        EPS = 1e-06
        key = jax.random.key(seed)
        ks = jax.random.split(key, 6)
        d_in, d_out = (1024, 1024)
        Bsz, T = (4, 512)
        x = jax.random.normal(ks[0], (Bsz, T, d_in), dtype=jnp.float32)
        W = jax.random.normal(ks[1], (d_out, d_in), dtype=jnp.float32) / np.sqrt(d_in)
        b = jax.random.normal(ks[2], (d_out,), dtype=jnp.float32) * 0.01
        A = jax.random.normal(ks[3], (d_in, RANK), dtype=jnp.float32) / np.sqrt(d_in)
        Bmat = jax.random.normal(ks[4], (RANK, d_out), dtype=jnp.float32) * 0.01
        LiMEs = jax.random.normal(ks[5], (NUM_EXPERTS, RANK), dtype=jnp.float32) * 0.1
        return {'x': x, 'W': W, 'b': b, 'A': A, 'Bmat': Bmat, 'LiMEs': LiMEs}
    _L0_ffn_all = _L0_ffn_setup()
    _L0_ffn_in = {k: v for k, v in _L0_ffn_all.items() if k in ('W', 'b', 'A', 'Bmat', 'LiMEs')}
    del _L0_ffn_all
    return {'x': x, 'ctx_4096': ctx_4096, 'L0_xattn_W_lin1': _L0_xattn_in['W_lin1'], 'L0_xattn_b_lin1': _L0_xattn_in['b_lin1'], 'L0_xattn_W_lin2': _L0_xattn_in['W_lin2'], 'L0_xattn_b_lin2': _L0_xattn_in['b_lin2'], 'L0_xattn_W_conv1': _L0_xattn_in['W_conv1'], 'L0_xattn_W_conv2': _L0_xattn_in['W_conv2'], 'L0_xattn_W_conv3': _L0_xattn_in['W_conv3'], 'L0_attn_scales_q': _L0_attn_in['scales_q'], 'L0_attn_scales_k': _L0_attn_in['scales_k'], 'L0_attn_scales_v': _L0_attn_in['scales_v'], 'L0_attn_scales_o': _L0_attn_in['scales_o'], 'L0_attn_qw_q': _L0_attn_in['qw_q'], 'L0_attn_qw_k': _L0_attn_in['qw_k'], 'L0_attn_qw_v': _L0_attn_in['qw_v'], 'L0_attn_qw_o': _L0_attn_in['qw_o'], 'L0_ffn_W': _L0_ffn_in['W'], 'L0_ffn_b': _L0_ffn_in['b'], 'L0_ffn_A': _L0_ffn_in['A'], 'L0_ffn_Bmat': _L0_ffn_in['Bmat'], 'L0_ffn_LiMEs': _L0_ffn_in['LiMEs']}

def reference(x, ctx_4096, L0_xattn_W_lin1, L0_xattn_b_lin1, L0_xattn_W_lin2, L0_xattn_b_lin2, L0_xattn_W_conv1, L0_xattn_W_conv2, L0_xattn_W_conv3, L0_attn_scales_q, L0_attn_scales_k, L0_attn_scales_v, L0_attn_scales_o, L0_attn_qw_q, L0_attn_qw_k, L0_attn_qw_v, L0_attn_qw_o, L0_ffn_W, L0_ffn_b, L0_ffn_A, L0_ffn_Bmat, L0_ffn_LiMEs):
    import jax
    import jax.numpy as jnp

    def _L0_xattn_ref(coords, feats, W_lin1, b_lin1, W_lin2, b_lin2, W_conv1, W_conv2, W_conv3):
        import jax, jax.numpy as jnp
        import numpy as np
        K = 10
        NUM_BITS = 10
        M_METHODS = 4

        def _quantize(coords, num_bits=NUM_BITS):
            cmin = coords.min(axis=1, keepdims=True)
            cmax = coords.max(axis=1, keepdims=True)
            scale = (2 ** num_bits - 1) / (cmax - cmin + 1e-06)
            q = jnp.floor((coords - cmin) * scale)
            return jnp.clip(q, 0, 2 ** num_bits - 1).astype(jnp.int32)

        def _morton_key(q):
            x, y, z = (q[..., 0], q[..., 1], q[..., 2])
            key = jnp.zeros(x.shape, dtype=jnp.int32)
            for b in range(NUM_BITS):
                key = key | (x >> b & 1) << 3 * b + 2 | (y >> b & 1) << 3 * b + 1 | (z >> b & 1) << 3 * b
            return key

        def _hilbert_key(q, num_bits=NUM_BITS):
            n = 3
            X = [q[..., i] for i in range(n)]
            M = 1 << num_bits - 1
            Q = M
            while Q > 1:
                P = Q - 1
                for i in range(n):
                    cond = X[i] & Q > 0
                    t = (X[0] ^ X[i]) & P
                    new_X0 = jnp.where(cond, X[0] ^ P, X[0] ^ t)
                    if i != 0:
                        X[i] = jnp.where(cond, X[i], X[i] ^ t)
                    X[0] = new_X0
                Q >>= 1
            for i in range(1, n):
                X[i] = X[i] ^ X[i - 1]
            t = jnp.zeros_like(X[0])
            Q = M
            while Q > 1:
                t = jnp.where(X[n - 1] & Q > 0, t ^ Q - 1, t)
                Q >>= 1
            X = [xi ^ t for xi in X]
            key = jnp.zeros(X[0].shape, dtype=jnp.int32)
            for b in range(num_bits - 1, -1, -1):
                for i in range(n):
                    key = key << 1 | X[i] >> b & 1
            return key

        def _sorted_indices(coords_bn3):
            q = _quantize(coords_bn3)
            qt = q[..., jnp.array([1, 0, 2])]
            keys = [_morton_key(q), _morton_key(qt), _hilbert_key(q), _hilbert_key(qt)]
            return [jnp.argsort(kk, axis=1) for kk in keys]

        def _window_inds(sorted_idx, k=K):
            B, N = sorted_idx.shape
            i = jnp.arange(N)
            start = jnp.maximum(0, i - k // 2)
            end = jnp.minimum(N, i + k // 2 + 1)
            pos = jnp.minimum(start[:, None] + jnp.arange(k)[None, :], (end - 1)[:, None])
            return jnp.take(sorted_idx, pos, axis=1)

        def _get_graph_features(feats, inds_list, perm, W_lin, b_lin, k=K):
            B, N, C = feats.shape
            center = feats[:, :, None, :]
            gather = jax.vmap(lambda f, idx: f[idx])
            per_method = []
            for inds in inds_list:
                neigh = gather(feats, inds)
                gf = jnp.concatenate([jnp.broadcast_to(center, (B, N, k, C)), neigh - center], axis=-1)
                per_method.append(gf)
            allf = jnp.stack(per_method, axis=-1)
            allf = allf[..., perm]
            total = 2 * C * M_METHODS
            x = allf.reshape(B * N, k, total)
            x16 = x.astype(jnp.float16).astype(jnp.float32)
            headdim = min(64, total)
            nheads = total // headdim
            qh = x16.reshape(B * N, k, nheads, headdim)
            scores = jnp.einsum('bihd,bjhd->bhij', qh, qh) / np.float32(np.sqrt(headdim))
            attn = jax.nn.softmax(scores, axis=-1)
            out = jnp.einsum('bhij,bjhd->bihd', attn, qh).reshape(B * N, k, total)
            fused = out @ W_lin.T + b_lin
            return fused.reshape(B, N, k, 128)

        def _instance_norm(x, axes):
            mu = x.mean(axis=axes, keepdims=True)
            var = x.var(axis=axes, keepdims=True)
            return (x - mu) / jnp.sqrt(var + 1e-05)

        def _lrelu(x):
            return jnp.where(x > 0, x, 0.2 * x)
        inds_sorted = _sorted_indices(coords.transpose(0, 2, 1))
        inds_list = [_window_inds(s) for s in inds_sorted]
        perm1 = jnp.array([2, 0, 3, 1])
        perm2 = jnp.array([1, 3, 0, 2])
        f0 = feats.transpose(0, 2, 1)
        g1 = _get_graph_features(f0, inds_list, perm1, W_lin1, b_lin1)
        h1 = jnp.einsum('oc,bnkc->bonk', W_conv1, g1)
        h1 = _lrelu(_instance_norm(h1, (2, 3)))
        feats1 = h1.max(axis=-1)
        g2 = _get_graph_features(feats1.transpose(0, 2, 1), inds_list, perm2, W_lin2, b_lin2)
        h2 = jnp.einsum('oc,bnkc->bonk', W_conv2, g2)
        h2 = _lrelu(_instance_norm(h2, (2, 3)))
        feats2 = h2.max(axis=-1)
        f3 = jnp.concatenate([feats, feats1, feats2], axis=1)
        h3 = jnp.einsum('oc,bcn->bon', W_conv3, f3)
        return _lrelu(_instance_norm(h3, (2,)))

    def _L0_attn_ref(hidden_states, scales_q, scales_k, scales_v, scales_o, qw_q, qw_k, qw_v, qw_o):
        import jax, jax.numpy as jnp
        import numpy as np
        import math
        B, S, H = (1, 512, 1024)
        NH, NKV, HD = (32, 8, 128)
        GS = 128
        WBITS = 4
        ZERO = float(2 ** (WBITS - 1))
        THETA = 10000.0

        def _dequant_matmul(x, qw, scales):
            w = (qw.astype(jnp.float32) - ZERO) * jnp.repeat(scales, GS, axis=0)
            return x @ w

        def _rope_tables(seq_len, dtype):
            inv_freq = 1.0 / THETA ** (jnp.arange(0, HD, 2, dtype=jnp.float32) / HD)
            freqs = jnp.arange(seq_len, dtype=jnp.float32)[:, None] * inv_freq
            emb = jnp.concatenate([freqs, freqs], axis=-1)
            return (jnp.cos(emb).astype(dtype), jnp.sin(emb).astype(dtype))

        def _rotate_half(x):
            x1, x2 = jnp.split(x, 2, axis=-1)
            return jnp.concatenate([-x2, x1], axis=-1)

        def _apply_rope(x, cos, sin):
            return x * cos[None, None] + _rotate_half(x) * sin[None, None]
        b, s, _ = hidden_states.shape
        q = _dequant_matmul(hidden_states, qw_q, scales_q).reshape(b, s, NH, HD).transpose(0, 2, 1, 3)
        k = _dequant_matmul(hidden_states, qw_k, scales_k).reshape(b, s, NKV, HD).transpose(0, 2, 1, 3)
        v = _dequant_matmul(hidden_states, qw_v, scales_v).reshape(b, s, NKV, HD).transpose(0, 2, 1, 3)
        cos, sin = _rope_tables(s, hidden_states.dtype)
        q = _apply_rope(q, cos, sin)
        k = _apply_rope(k, cos, sin)
        rep = NH // NKV
        k = jnp.repeat(k, rep, axis=1)
        v = jnp.repeat(v, rep, axis=1)
        scores = jnp.einsum('bhqd,bhkd->bhqk', q, k) / math.sqrt(HD)
        causal = jnp.tril(jnp.ones((s, s), dtype=bool))
        scores = jnp.where(causal[None, None], scores, jnp.finfo(scores.dtype).min)
        attn = jax.nn.softmax(scores.astype(jnp.float32), axis=-1).astype(q.dtype)
        ctx = jnp.einsum('bhqk,bhkd->bhqd', attn, v)
        ctx = ctx.transpose(0, 2, 1, 3).reshape(b, s, NH * HD)
        return _dequant_matmul(ctx, qw_o, scales_o)

    def _L0_ffn_ref(x, W, b, A, Bmat, LiMEs):
        import jax, jax.numpy as jnp
        import numpy as np
        NUM_EXPERTS = 8
        RANK = 32
        ALPHA = 16.0
        TOP_K = 2
        TEMPERATURE = 1.0
        GAMMA = 0.5
        SOFT_TOPK_TEMP = 0.5
        N_GRAM = 2
        EPS = 1e-06
        Bsz, T, d_in = x.shape
        E = LiMEs.shape[0]
        scaling = ALPHA / RANK
        H = jnp.einsum('btd,od->bto', x, W) + b
        z = jnp.einsum('btd,dr->btr', x, A)
        anchors = jnp.arange(N_GRAM - 1, T, N_GRAM)
        H_slice = H[:, anchors, :E]
        delta_slice = jnp.einsum('bar,er->bae', z[:, anchors], LiMEs)
        H_scale = jnp.maximum(jnp.max(jnp.abs(H_slice)), EPS)
        d_scale = jnp.maximum(jnp.max(jnp.abs(delta_slice)), EPS)
        logits = ((1.0 - GAMMA) * (H_slice / H_scale) + GAMMA * (delta_slice / d_scale)) / TEMPERATURE
        probs = jax.nn.softmax(logits, axis=-1)
        topk_vals, _ = jax.lax.top_k(probs, TOP_K)
        thresh = topk_vals[..., -1:]
        mask = jax.nn.sigmoid((probs - thresh) / SOFT_TOPK_TEMP)
        weights = probs * mask
        weights = weights / (jnp.sum(weights, axis=-1, keepdims=True) + 1e-09)
        weights_full = jnp.repeat(weights, N_GRAM, axis=1)
        p_mix = jnp.einsum('bte,er->btr', weights_full, LiMEs)
        delta = jnp.einsum('btr,ro->bto', z * p_mix, Bmat) * scaling
        return H + delta
    x = x + _L0_xattn_ref(ctx_4096, _layernorm(x, axis=-1), L0_xattn_W_lin1, L0_xattn_b_lin1, L0_xattn_W_lin2, L0_xattn_b_lin2, L0_xattn_W_conv1, L0_xattn_W_conv2, L0_xattn_W_conv3)
    x = x + _L0_attn_ref(_layernorm(x, axis=-1), L0_attn_scales_q, L0_attn_scales_k, L0_attn_scales_v, L0_attn_scales_o, L0_attn_qw_q, L0_attn_qw_k, L0_attn_qw_v, L0_attn_qw_o)
    x = x + _L0_ffn_ref(_layernorm(x, axis=-1), L0_ffn_W, L0_ffn_b, L0_ffn_A, L0_ffn_Bmat, L0_ffn_LiMEs)
    return x

_drawn_inputs = setup_inputs


def setup_inputs(seed=0):
    import zlib

    import numpy as np

    out = dict(_drawn_inputs(seed))
    spreads = {'L0_xattn_b_lin1': (0.0, 0.8), 'L0_xattn_b_lin2': (0.0, 0.8)}
    factors = {'L0_ffn_b': 8.0, 'L0_ffn_A': 8.0, 'L0_ffn_Bmat': 8.0, 'L0_ffn_LiMEs': 8.0}
    for name, (base, spread) in spreads.items():
        noise = np.random.default_rng([zlib.crc32(name.encode()), seed]).standard_normal(out[name].shape)
        drawn = base * np.exp(spread * noise) if base else spread * noise
        out[name] = jnp.asarray(drawn.astype(out[name].dtype))
    for name, factor in factors.items():
        out[name] = (out[name] * factor).astype(out[name].dtype)
    return out
```

```python
from contextlib import ExitStack

import numpy as np
import concourse.bass as bass
from concourse import mybir

ALU = mybir.AluOpType
ACT = mybir.ActivationFunctionType
AX = mybir.AxisListType
F32, F16, BF16, I32 = mybir.dt.float32, mybir.dt.float16, mybir.dt.bfloat16, mybir.dt.int32
NP_BF16 = mybir.dt.np(BF16)

P = 128
B, C, N = 8, 64, 1024
M = 4
KNN = 10
NB = N // P
EPS = 1e-5
WSCALE = 256.0


class Kernel:

    def __init__(self, nc, given):
        self.nc, self.given = nc, given
        self.stage, self.sems = 0, []
        self.d_quant = nc.dram_tensor("d_quant", (3 * B, N), I32).ap()
        self.d_key = nc.dram_tensor("d_key", (2, B, M, N), F32).ap()
        self.d_feats = nc.dram_tensor("d_feats", (B, C, N), F32).ap()
        self.d_f = nc.dram_tensor("d_f", (B, C, N), F32).ap()
        self.d_g = nc.dram_tensor("d_g", (B, 8, M, 16, N), F16).ap()
        self.d_x1 = nc.dram_tensor("d_x1", (B * C, N), F32).ap()


class Counted:

    def __init__(self, eng, sem, start=0):
        self.eng, self.sem, self.start, self.n = eng, sem, start, 0

    def inc(self, ins):
        self.n += 1
        ins.then_inc(self.sem, 1)

    def then(self, ins):
        self.inc(ins)
        self.eng.wait_ge(self.sem, self.start + self.n)


def placing(k, ctx):
    k.stage += 1
    nc, tag = k.nc, f"_{k.stage}"

    def sb(name, shape, dt=F32):
        return ctx.enter_context(nc.sbuf_tensor(name + tag, shape, dt))

    def ps(name, shape, dt=F32):
        return ctx.enter_context(nc.psum_tensor(name + tag, shape, dt))

    def sem(name):
        k.sems.append(nc.alloc_semaphore(name + tag))
        return k.sems[-1]

    return sb, ps, sem


def curve_keys(k):
    nc = k.nc
    with ExitStack() as ctx:
        sb, ps, sem = placing(k, ctx)
        NQ = 3 * B
        xs = sb("xs", [C, B, N], F32)
        xstat = sb("xstat", [C, B, 2, 6], F32)
        xmv = sb("xmv", [C, B, 2], F32)
        xstd = sb("xstd", [C, B], F32)
        xrstd = sb("xrstd", [C, B], F32)
        co = sb("co", [NQ, N], F32)
        cq = sb("cq", [NQ, N], F32)
        cfl = sb("cfl", [NQ, N], F32)
        cint = sb("cint", [NQ, N], I32)
        col = sb("col", [NQ, 16], F32)
        coli = col[:, :].bitcast(I32)
        X = sb("X", [P, 3, M, 64], I32)
        T = sb("T", [P, 3, M, 64], I32)
        mask = sb("mask", [P, 2, 64], I32)
        flip = sb("flip", [P, 2, 64], I32)
        point = sb("point", [P, 64], I32)
        key = sb("key", [P, 2, M, 64], I32)
        keyf = sb("keyf", [P, 2, M, 64], F32)
        epsc = sb("epsc", [P, 1], F32)

        s_x = sem("s_x")
        s_co = sem("s_co")
        s_chain = sem("s_chain")
        s_var = sem("s_var")
        s_std = sem("s_std")
        s_eps = sem("s_eps")
        s_cint = sem("s_cint")
        s_qout = sem("s_qout")
        s_qin = sem("s_qin")
        s_point = sem("s_point")
        s_keyf = sem("s_keyf")
        s_kout = sem("s_kout")
        s_f = sem("s_f")
        s_fout = sem("s_fout")

        with nc.Block() as block:
            @block.sync
            def _(sp):
                sp.dma_start(co[:, :], k.given["coords"].rearrange("b a n -> (b a) n")).then_inc(s_co, 16)
                sp.dma_start(xs[:, :, :], k.given["x"].rearrange("b c n -> c b n")).then_inc(s_x, 16)
                sp.wait_ge(s_cint, 1)
                sp.dma_start(k.d_quant, cint[:, :]).then_inc(s_qout, 16)
                sp.wait_ge(s_qout, 16)
                for b in range(B):
                    for a in range(3):
                        sp.dma_start(X[16 * b:16 * b + 16, a, 0, :],
                                     k.d_quant[3 * b + a].rearrange("(g e) -> g e", e=64)).then_inc(s_qin, 16)
                sp.wait_ge(s_keyf, 1)
                for b in range(B):
                    for h in range(2):
                        sp.dma_start(k.d_key[h, b].rearrange("m (g e) -> g m e", e=64),
                                     keyf[16 * b:16 * b + 16, h, :, :]).then_inc(s_kout, 16)
                sp.wait_ge(s_kout, 16 * 2 * B)

            @block.gpsimd
            def _(pool):
                pool.iota(point[:, :], pattern=[[1, 64]], base=0, channel_multiplier=64).then_inc(s_point, 1)
                pool.memset(epsc[:, :], EPS).then_inc(s_eps, 1)

            @block.scalar
            def _(act):
                act.wait_ge(s_var, 1)
                act.wait_ge(s_eps, 1)
                act.activation(xstd[:, :], xmv[:, :, 1], ACT.Sqrt, bias=epsc[0:C, :]).then_inc(s_std, 1)
                for h in range(2):
                    act.wait_ge(s_f, 4 * h + 4)
                    act.dma_start(k.d_feats[4 * h:4 * h + 4].rearrange("b c n -> c b n"),
                                  k.F[0:C, 4 * h:4 * h + 4, :]).then_inc(s_fout, 16)
                act.wait_ge(s_fout, 32)

            @block.vector
            def _(v):
                ch = Counted(v, s_chain)

                def ts(out, a, s1, s2, o1, o2=ALU.bypass):
                    ch.then(v.tensor_scalar(out, a, s1, s2, o1, o2) if s2 is not None
                            else v.tensor_scalar(out, a, s1, None, o1))

                def tt(out, a, b_, op):
                    ch.then(v.tensor_tensor(out, a, b_, op))

                v.wait_ge(s_co, 16)
                ch.then(v.tensor_reduce(col[:, 0:1], co[:, :], AX.X, ALU.min))
                ch.then(v.tensor_reduce(col[:, 1:2], co[:, :], AX.X, ALU.max))
                tt(col[:, 2:3], col[:, 1:2], col[:, 0:1], ALU.subtract)
                ts(col[:, 3:4], col[:, 2:3], 1e-6, None, ALU.add)
                ch.then(v.reciprocal(col[:, 4:5], col[:, 3:4]))
                ts(col[:, 5:6], col[:, 4:5], 1023.0, None, ALU.mult)
                for src, hi, lo in ((3, 6, 7), (5, 8, 9)):
                    ts(coli[:, hi:hi + 1], coli[:, src:src + 1], -4096, None, ALU.bitwise_and)
                    tt(col[:, lo:lo + 1], col[:, src:src + 1], col[:, hi:hi + 1], ALU.subtract)
                tt(col[:, 10:11], col[:, 6:7], col[:, 8:9], ALU.mult)
                ts(col[:, 11:12], col[:, 10:11], -1.0, 1023.0, ALU.mult, ALU.add)
                for a, b_ in ((6, 9), (7, 8), (7, 9)):
                    tt(col[:, 10:11], col[:, a:a + 1], col[:, b_:b_ + 1], ALU.mult)
                    tt(col[:, 11:12], col[:, 11:12], col[:, 10:11], ALU.subtract)
                tt(col[:, 10:11], col[:, 11:12], col[:, 4:5], ALU.mult)
                tt(col[:, 12:13], col[:, 5:6], col[:, 10:11], ALU.add)
                ts(cq[:, :], co[:, :], col[:, 0:1], col[:, 12:13], ALU.subtract, ALU.mult)
                ch.then(v.tensor_copy(cint[:, :], cq[:, :]))
                ch.then(v.tensor_copy(cfl[:, :], cint[:, :]))
                tt(cq[:, :], cfl[:, :], cq[:, :], ALU.is_gt)
                tt(cfl[:, :], cfl[:, :], cq[:, :], ALU.subtract)
                ts(cfl[:, :], cfl[:, :], 0.0, 1023.0, ALU.max, ALU.min)
                ch.then(v.tensor_copy(cint[:, :], cfl[:, :]))
                v.tensor_copy(col[:, 13:14], col[:, 12:13]).then_inc(s_cint, 1)

                v.wait_ge(s_x, 16)
                for b in range(B):
                    for h in range(2):
                        ch.inc(v.bn_stats(xstat[:, b, h, :], xs[:, b, 512 * h:512 * h + 512]))
                v.wait_ge(s_chain, ch.n)
                for b in range(B):
                    ch.inc(v.bn_aggr(xmv[:, b, :], xstat[:, b, :, :]))
                v.wait_ge(s_chain, ch.n)
                v.tensor_copy(col[:, 14:15], col[:, 13:14]).then_inc(s_var, 1)

                v.wait_ge(s_qin, 16 * 3 * B)
                for a, b_ in ((0, 1), (1, 0), (2, 2)):
                    ch.inc(v.tensor_copy(X[:, b_, 1, :], X[:, a, 0, :]))
                for a in range(3):
                    ch.inc(v.tensor_copy(X[:, a, 2, :], X[:, a, 0, :]))
                for a, b_ in ((0, 1), (1, 0), (2, 2)):
                    ch.inc(v.tensor_copy(X[:, b_, 3, :], X[:, a, 0, :]))
                v.wait_ge(s_chain, ch.n)

                H = [X[:, a, 2:4, :] for a in range(3)]
                t, u = mask[:, :, :], flip[:, :, :]
                for bit in range(9, 0, -1):
                    low = (1 << bit) - 1
                    ts(t, H[0], 31 - bit, 31, ALU.logical_shift_left, ALU.arith_shift_right)
                    ch.then(v.scalar_tensor_tensor(H[0], t, low, H[0], ALU.bitwise_and, ALU.bitwise_xor))
                    for a in (1, 2):
                        ts(t, H[a], 31 - bit, 31, ALU.logical_shift_left, ALU.arith_shift_right)
                        tt(u, H[0], H[a], ALU.bitwise_xor)
                        ch.then(v.scalar_tensor_tensor(H[0], t, low, H[0], ALU.bitwise_and, ALU.bitwise_xor))
                        ts(t, t, low, low, ALU.bitwise_and, ALU.bitwise_xor)
                        tt(u, u, t, ALU.bitwise_and)
                        tt(H[0], H[0], u, ALU.bitwise_xor)
                        tt(H[a], H[a], u, ALU.bitwise_xor)
                tt(H[1], H[1], H[0], ALU.bitwise_xor)
                tt(H[2], H[2], H[1], ALU.bitwise_xor)
                ts(u, H[2], 0, None, ALU.bitwise_and)
                for bit in range(9, 0, -1):
                    ts(t, H[2], 31 - bit, 31, ALU.logical_shift_left, ALU.arith_shift_right)
                    ch.then(v.scalar_tensor_tensor(u, t, (1 << bit) - 1, u, ALU.bitwise_and, ALU.bitwise_xor))
                for a in range(3):
                    ch.inc(v.tensor_tensor(H[a], H[a], u, ALU.bitwise_xor))
                v.wait_ge(s_chain, ch.n)

                Xf = X[:, :, :, :].rearrange("p a m e -> p (a m e)")
                Tf = T[:, :, :, :].rearrange("p a m e -> p (a m e)")
                for shift, keep in ((16, 0x030000FF), (8, 0x0300F00F), (4, 0x030C30C3), (2, 0x09249249)):
                    ch.then(v.scalar_tensor_tensor(Tf, Xf, shift, Xf, ALU.logical_shift_left, ALU.bitwise_or))
                    ts(Xf, Tf, keep, None, ALU.bitwise_and)
                S = [X[:, a, :, :] for a in range(3)]
                ch.then(v.scalar_tensor_tensor(T[:, 0, :, :], S[1], 1, S[2], ALU.logical_shift_left, ALU.bitwise_or))
                ch.then(v.scalar_tensor_tensor(T[:, 1, :, :], S[0], 2, T[:, 0, :, :],
                                               ALU.logical_shift_left, ALU.bitwise_or))
                K = T[:, 1, :, :]
                ts(key[:, 0, :, :], K, 6, None, ALU.logical_shift_right)
                ch.then(v.tensor_copy(keyf[:, 0, :, :], key[:, 0, :, :]))
                ts(key[:, 1, :, :], K, 63, 10, ALU.bitwise_and, ALU.logical_shift_left)
                v.wait_ge(s_point, 1)
                ts(point[:, :], point[:, :], N - 1, None, ALU.bitwise_and)
                for m in range(M):
                    ch.inc(v.tensor_tensor(key[:, 1, m, :], key[:, 1, m, :], point[:, :], ALU.bitwise_or))
                v.wait_ge(s_chain, ch.n)
                ch.inc(v.tensor_copy(keyf[:, 1, :, :], key[:, 1, :, :]))
                ts(keyf[:, 0, :, :], keyf[:, 0, :, :], 65536.0, None, ALU.mult)
                v.tensor_copy(col[:, 15:16], col[:, 14:15]).then_inc(s_keyf, 1)

                v.wait_ge(s_std, 1)
                ch.then(v.reciprocal(xrstd[:, :], xstd[:, :]))
                for b in range(B):
                    v.tensor_scalar(k.F[0:C, b, :], xs[:, b, :], xmv[:, b, 0:1], xrstd[:, b:b + 1],
                                    ALU.subtract, ALU.mult).then_inc(s_f, 1)


def curve_ranks(k):
    nc = k.nc
    R = B * M
    RING = 4
    with ExitStack() as ctx:
        sb, ps, sem = placing(k, ctx)
        rows = sb("rows", [R, 2, N], F32)
        own = sb("own", [P, 2, R, NB], F32)
        wide = sb("wide", [P, RING, 2, N], F32)
        cmp = sb("cmp", [P, 4, N], F32)
        total = sb("total", [P, R, NB], F32)
        psT = ps("psT", [P, 2, NB, R], F32)
        s_rows = sem("s_rows")
        s_t = sem("s_t")
        s_own = sem("s_own")
        s_wide = [sem(f"s_wide{i}") for i in range(RING)]
        s_cmp = sem("s_cmp")
        s_sign = sem("s_sign")
        s_tot = sem("s_tot")

        with nc.Block() as block:
            @block.sync
            def _(sp):
                sp.dma_start(rows[:, :, :], k.d_key.rearrange("h b m n -> (b m) h n")).then_inc(s_rows, 16)
                keyw = k.d_key.rearrange("h b m n -> (b m) h n")

                def load(r, i):
                    sp.dma_start(wide[:, i, :, :], bass.AP(
                        tensor=keyw.tensor, offset=keyw[bass.ds(r, 1), 0:1, 0:1].offset,
                                 ap=[[0, P], [R * N, 2], [1, N]])).then_inc(s_wide[i], 16)

                for i in range(RING):
                    load(i, i)
                with sp.Fori(0, R // RING - 1) as t:
                    for i in range(RING):
                        sp.wait_ge(s_cmp, (t * RING + i + 1) * NB)
                        load(t * RING + (RING + i), i)

            @block.tensor
            def _(pe):
                pe.wait_ge(s_rows, 16)
                for h in range(2):
                    for n in range(NB):
                        last = pe.transpose(psT[:, h, n, :], rows[:, h, n * P:(n + 1) * P], k.id32[0:R, 0:R])
                last.then_inc(s_t, 1)

            @block.vector
            def _(v):
                v.wait_ge(s_t, 1)
                v.tensor_copy(own[:, 0, :, :], psT[:, 0, :, :].rearrange("p n r -> p r n")).then_inc(s_own, 1)
                v.tensor_scalar(own[:, 1, :, :], psT[:, 1, :, :].rearrange("p n r -> p r n"), -1.0, None,
                                ALU.mult).then_inc(s_own, 1)
                v.wait_ge(s_own, 2)
                own0 = own[:, 0, :, :].rearrange("p r n -> p (r n)")

                def step(r, t, i, n, wait):
                    if wait is not None:
                        v.wait_ge(s_sign, wait)
                    v.scalar_tensor_tensor(cmp[:, n % 4, :], wide[:, i, 0, :], own0[:, bass.ds(r * NB + n, 1)],
                                           wide[:, i, 1, :], ALU.subtract, ALU.add).then_inc(s_cmp, 1)

                for i in range(RING):
                    v.wait_ge(s_wide[i], 16)
                    for n in range(NB):
                        at = i * NB + n
                        step(i, 0, i, n, at - 3 if at >= 4 else None)
                with v.Fori(1, R // RING) as t:
                    for i in range(RING):
                        v.wait_ge(s_wide[i], 16 * t + 16)
                        for n in range(NB):
                            step(t * RING + i, t, i, n, t * (RING * NB) + (i * NB + n - 3))
                v.wait_ge(s_tot, 1)
                v.tensor_scalar(k.rank[:, :, :], total[:, :, :], -0.5, (N - 1) / 2, ALU.mult, ALU.add)

            @block.scalar
            def _(act):
                act.wait_ge(s_own, 2)
                own1 = own[:, 1, :, :].rearrange("p r n -> p (r n)")
                tot = total[:, :, :].rearrange("p r n -> p (r n)")
                with act.Fori(0, R) as r:
                    for n in range(NB):
                        act.wait_ge(s_cmp, r * NB + (n + 1))
                        act.activation(cmp[:, n % 4, :], cmp[:, n % 4, :], ACT.Sign, bias=own1[:, bass.ds(r * NB + n, 1)],
                                       accum_out=tot[:, bass.ds(r * NB + n, 1)]).then_inc(s_sign, 1)
                act.wait_ge(s_sign, R * NB)
                act.copy(cmp[:, 0, 0:1], cmp[:, 0, 0:1]).then_inc(s_tot, 1)


def split_features(k, src, centre, wd, O):
    nc = k.nc
    with ExitStack() as ctx:
        sb, ps, sem = placing(k, ctx)
        hi = sb("hi", [C, 2, N], F16)
        lo = sb("lo", [C, 2, N], F16)
        both = sb("both", [C, 2, 2, N], F32)
        psF = [ps(f"psF{i}", [P, NB, P], F16) for i in range(2)]
        psC = [ps(f"psC{i}", [P, NB * O]) for i in range(2)]
        s_hi = sem("s_hi")
        s_lo = sem("s_lo")
        s_both = sem("s_both")
        s_dump = [sem("s_dump0"), sem("s_dump1")]
        s_turn = sem("s_turn")
        s_fT = sem("s_fT")
        s_c = sem("s_c")
        s_chi = sem("s_chi")
        s_clo = sem("s_clo")

        def part(b, h):
            return centre[:, b * NB:(b + 1) * NB, h, :]

        with nc.Block() as block:
            @block.scalar
            def _(act):
                for b in range(B):
                    if b >= 2:
                        act.wait_ge(s_turn, b - 1)
                        act.wait_ge(s_both, 2 * (b - 1))
                        act.wait_ge(s_lo, b - 1)
                    act.copy(hi[:, b % 2, :], src[0:C, b, :]).then_inc(s_hi, 1)
                    if b >= 1:
                        act.wait_ge(s_c, b)
                        act.copy(part(b - 1, 0), psC[(b - 1) % 2][:, :].rearrange("p (n o) -> p n o", o=O)
                                 ).then_inc(s_chi, 1)
                act.wait_ge(s_c, B)
                act.copy(part(B - 1, 0), psC[(B - 1) % 2][:, :].rearrange("p (n o) -> p n o", o=O)).then_inc(s_chi, 1)

            @block.vector
            def _(v):
                def rest(b):
                    v.wait_ge(s_chi, b + 1)
                    v.tensor_tensor(part(b, 1), psC[b % 2][:, :].rearrange("p (n o) -> p n o", o=O), part(b, 0),
                                    ALU.subtract).then_inc(s_clo, 1)

                for b in range(B):
                    v.wait_ge(s_hi, b + 1)
                    if b >= 2:
                        v.wait_ge(s_turn, b - 1)
                        v.wait_ge(s_both, 2 * (b - 1))
                    v.tensor_tensor(lo[:, b % 2, :], src[0:C, b, :], hi[:, b % 2, :],
                                    ALU.subtract).then_inc(s_lo, 1)
                    v.wait_ge(s_turn, b + 1)
                    v.tensor_copy(k.fT[:, b, :, :], psF[b % 2][:, :, :]).then_inc(s_fT, 1)
                    if b >= 1:
                        rest(b - 1)
                rest(B - 1)

            @block.gpsimd
            def _(pool):
                for b in range(B):
                    pool.wait_ge(s_lo, b + 1)
                    if b >= 2:
                        pool.wait_ge(s_dump[b % 2], 16 * (b // 2))
                        pool.wait_ge(s_c, b - 1)
                    pool.tensor_copy(both[:, b % 2, 0, :], hi[:, b % 2, :]).then_inc(s_both, 1)
                    pool.tensor_tensor(both[:, b % 2, 1, :], hi[:, b % 2, :], lo[:, b % 2, :],
                                       ALU.add).then_inc(s_both, 1)

            @block.sync
            def _(sp):
                for b in range(B):
                    sp.wait_ge(s_both, 2 * (b + 1))
                    sp.dma_start(k.d_f[b], both[:, b % 2, 1, :]).then_inc(s_dump[b % 2], 16)
                for u in range(2):
                    sp.wait_ge(s_dump[u], 16 * (B // 2))

            @block.tensor
            def _(pe):
                for b in range(B):
                    pe.wait_ge(s_lo, b + 1)
                    if b >= 2:
                        pe.wait_ge(s_fT, b - 1)
                    for n in range(NB):
                        for h, part in enumerate((hi, lo)):
                            last = pe.transpose(psF[b % 2][:, n, C * h:C * h + C], part[:, b % 2, n * P:(n + 1) * P],
                                                k.id16[0:C, 0:C])
                    last.then_inc(s_turn, 1)
                    pe.wait_ge(s_both, 2 * (b + 1))
                    if b >= 2:
                        pe.wait_ge(s_clo, b - 1)
                    for n in range(NB):
                        for h in range(2):
                            last = pe.matmul(psC[b % 2][:, n * O:(n + 1) * O], both[:, b % 2, h, n * P:(n + 1) * P],
                                             wd[:, h, :], start=(h == 0), stop=(h == 1))
                    last.then_inc(s_c, 1)


def gather(k):
    nc = k.nc
    with ExitStack() as ctx:
        sb, ps, sem = placing(k, ctx)
        hot = sb("hot", [P, 8, N], F16)
        out = sb("out", [P, M, N], F16)
        psG = [ps(f"psGa{i}", [P, N], F32) for i in range(2)]
        s_hot = sem("s_hot")
        s_sent = [sem(f"s_sent{m}") for m in range(M)]
        s_freehot = sem("s_freehot")
        s_freeps = sem("s_freeps")
        rank = k.rank[:, :, :].rearrange("p r n -> p (r n)")

        with nc.Block() as block:
            @block.vector
            def _(v):
                with v.Fori(0, B) as b:
                    for j in range(M * NB):
                        v.wait_ge(s_freehot, b * (M * NB) + (j + 1))
                        v.tensor_scalar(hot[:, j % 8, :], k.ramp[:, :], rank[:, bass.ds(b * (M * NB) + j, 1)], None,
                                        ALU.is_equal).then_inc(s_hot, 1)

            @block.tensor
            def _(pe):
                pe.sem_inc(s_freehot, 8)
                fT = k.fT[:, :, :, :].rearrange("p b n c -> p (b n c)")
                with pe.Fori(0, B) as b:
                    for m in range(M):
                        pe.wait_ge(s_freeps, b * M + (m + 1))
                        for n in range(NB):
                            pe.wait_ge(s_hot, b * (M * NB) + (m * NB + n + 1))
                            for h in range(2):
                                last = pe.matmul(psG[m % 2][:, 512 * h:512 * h + 512],
                                                 fT[:, bass.ds(b * (NB * P) + n * P, P)],
                                                 hot[:, (m * NB + n) % 8, 512 * h:512 * h + 512],
                                                 start=(n == 0), stop=(n == NB - 1))
                            last.then_inc(s_freehot, 1)

            @block.scalar
            def _(act):
                act.sem_inc(s_freeps, 2)
                with act.Fori(0, B) as b:
                    for m in range(M):
                        act.wait_ge(s_freehot, b * (M * NB) + ((m + 1) * NB + 8))
                        act.wait_ge(s_sent[m], b * 16 + 16)
                        act.copy(out[:, m, :], psG[m % 2][:, :]).then_inc(s_freeps, 1)
                        act.wait_ge(s_freeps, b * M + (m + 3))
                        act.dma_start(k.d_g[bass.ds(b, 1), :, m, :, :].rearrange("o q c n -> (o q) c n"),
                                      out[:, m, :]).then_inc(s_sent[m], 16)
                for m in range(M):
                    act.wait_ge(s_sent[m], 16 * B + 16)

            @block.sync
            def _(sp):
                for m in range(M):
                    sp.sem_inc(s_sent[m], 16)


def combine_weights(k, layers):
    nc = k.nc
    with ExitStack() as ctx:
        sb, ps, sem = placing(k, ctx)
        s_w, s_comb, s_hi = sem("s_w"), sem("s_comb"), sem("s_hi")
        lin, win, conv, bias, psN, psD = [], [], [], [], [], []
        for i, (_, _, _, _, O, _, _, _) in enumerate(layers):
            lin.append(sb(f"lin{i}", [P, 2 * C * M]))
            win.append(sb(f"win{i}", [P, 2, P]))
            conv.append(sb(f"conv{i}", [P, O]))
            bias.append(sb(f"bias{i}", [P, 1]))
            psN.append(ps(f"psN{i}", [P, 2, O]))
            psD.append(ps(f"psD{i}", [P, 2 * O + 1]))

        with nc.Block() as block:
            @block.sync
            def _(sp):
                for i, (w_lin, w_win, w_conv, b_lin, _, _, _, _) in enumerate(layers):
                    sp.dma_start(lin[i][:, :], w_lin).then_inc(s_w, 16)
                    sp.dma_start(win[i][:, :, :], w_win.rearrange("c (k r) -> c k r", k=2)).then_inc(s_w, 16)
                    sp.dma_start(conv[i][:, :], w_conv).then_inc(s_w, 16)
                    sp.dma_start(bias[i][:, :], b_lin).then_inc(s_w, 16)

            @block.tensor
            def _(pe):
                pe.wait_ge(s_w, 16 * 4 * len(layers))
                for i, (_, _, _, _, O, _, _, _) in enumerate(layers):
                    for c in range(2):
                        pe.matmul(psN[i][:, c, :], win[i][:, c, :], conv[i][:, :], start=True, stop=True)
                    by_curve = lin[i][:, :].rearrange("c (h r m) -> c h m r", h=2, m=M)
                    for h in range(2):
                        for m in range(M):
                            pe.matmul(psD[i][0:C, h * O:(h + 1) * O], by_curve[:, h, m, :], conv[i][:, :],
                                      start=(m == 0), stop=(m == M - 1))
                    pe.matmul(psD[i][0:O, 2 * O:2 * O + 1], conv[i][:, :], bias[i][:, :], start=True, stop=True
                              ).then_inc(s_comb, 1)

            @block.scalar
            def _(act):
                for i, (_, _, _, _, O, wn, wd, hb) in enumerate(layers):
                    act.wait_ge(s_comb, i + 1)
                    act.mul(wn[:, 0, :, :], psN[i][:, :, :], WSCALE).then_inc(s_hi, 1)
                    act.copy(hb[0:O, :], psD[i][0:O, 2 * O:2 * O + 1])
                    act.copy(wd[:, 0, :], psD[i][0:C, 0:O])
                    act.mul(wd[:, 1, :], psD[i][0:C, O:2 * O], -1.0)

            @block.vector
            def _(v):
                for i, (_, _, _, _, O, wn, wd, hb) in enumerate(layers):
                    v.wait_ge(s_hi, i + 1)
                    v.scalar_tensor_tensor(wn[:, 1, :, :], psN[i][:, :, :], WSCALE, wn[:, 0, :, :],
                                           ALU.mult, ALU.subtract)


G = 6
GP = 11
ROWS = GP * KNN
STEP = 64
WIN = 20
AW = 2 * (P + 2 * GP)
SPAN = STEP + 12
PAD = 5
GW = N + 16
STEPS = B * N // STEP
PER = N // STEP


def edge_layer(k, centre, wn, O, maxh, mv):
    nc = k.nc
    with ExitStack() as ctx:
        sb, ps, sem = placing(k, ctx)
        Gs = sb("Gs", [P, 2, 2, 2, GW], F16)
        none = sb("none", [P, 4], F32)
        fr = sb("fr", [P, 2, 2, N + 2], F32)
        sth = sb("sth", [P, 2, 2, 2, SPAN, 2], F16)
        stu = sb("stu", [P, 2, 2, SPAN], F32)
        d16 = sb("d16", [P, 2, 2, G * GP, KNN], F16)
        spread = sb("spread", [P, 2, STEP * KNN], F16)
        mkl = sb("mkl", [3 * GP, ROWS], BF16)
        mkr = sb("mkr", [3 * GP, 9, G * 4 * WIN], BF16)
        E = sb("E", [ROWS, 2, G * 2, WIN, 2], F32)
        top = sb("top", [ROWS, 2, G * 4], F32)
        tot = sb("tot", [ROWS, 2, G * 4], F32)
        inv = sb("inv", [ROWS, 2, G * 4], F32)
        A = sb("A", [ROWS, 2, 3, AW], F32)
        AT = sb("AT", [P, 2, G * ROWS], F32)
        GWs = sb("GWs", [P, 2, 3, O], F32)
        stat = sb("stat", [O, STEPS, 2, 6], F32)
        psS = [ps(f"psS{i}", [P, 512]) for i in range(2)]
        psW = ps("psW", [P, 512])
        psA = ps("psA", [P, 2, 512])
        psY = ps("psY", [P, 2, 512])

        s_w = sem("s_w")
        s_load = [sem("s_load0"), sem("s_load1")]
        s_zero = sem("s_zero")
        s_pool = sem("s_pool")
        s_S = sem("s_S")
        s_sth = sem("s_sth")
        s_dve = sem("s_dve")
        s_sub = sem("s_sub")
        s_exp = sem("s_exp")
        s_A = sem("s_A")
        s_T = sem("s_T")
        s_AT = sem("s_AT")
        s_W = sem("s_W")
        s_GW = sem("s_GW")
        s_Y = sem("s_Y")
        s_done = sem("s_done")
        NLOAD = 4 + 4

        PADS, EDGE, EACH = 1, 5, 3
        BATCH = PADS + EDGE + EACH * PER

        def staged(n):
            return n // PER * BATCH + n % PER * EACH + (PADS + EDGE + EACH)

        with nc.Block() as block:
            @block.sync
            def _(sp):
                sp.dma_start(spread[:, :, :], k.given["c_spread"]).then_inc(s_w, 16)
                sp.dma_start(mkl[:, :], k.given["c_mkl"]).then_inc(s_w, 16)
                sp.dma_start(mkr[:, :, :], k.given["c_mkr"]).then_inc(s_w, 16)
                def load(b, u):
                    for hl in range(2):
                        for c in range(2):
                            at = 4 * hl + 2 * c
                            sp.dma_start(Gs[:, u, hl, c, PAD:PAD + N],
                                         k.d_g[bass.ds(b, 1), at:at + 2].rearrange("o h m c n -> (o h m c) n")
                                         ).then_inc(s_load[u], 16)
                    flat = k.d_f.rearrange("b c n -> (b c) n")
                    for c in range(2):
                        for h in range(2):
                            at = flat[bass.ds(b * C + (32 * c + 16 * h), 16), :]
                            sp.dma_start(fr[64 * h:64 * h + 64, u, c, 0:N],
                                         bass.AP(tensor=at.tensor, offset=at.offset, ap=[[0, M], [N, 16], [1, N]])
                                         ).then_inc(s_load[u], 16)

                sp.wait_ge(s_zero, 4)
                for u in range(2):
                    load(u, u)
                with sp.Fori(1, B // 2) as t:
                    for u in range(2):
                        sp.wait_ge(s_sth, t * (4 * PER) + (u - 1) * (2 * PER))
                        sp.wait_ge(s_pool, t * (2 * BATCH) + (u - 1) * BATCH)
                        load(2 * t + u, u)

            @block.gpsimd
            def _(pool):
                pool.memset(Gs[:, :, :, :, 0:PAD], 0.0).then_inc(s_zero, 1)
                pool.memset(sth[:, :, :, :, :, :], 0.0).then_inc(s_zero, 1)
                pool.memset(none[:, :], 0.0).then_inc(s_zero, 1)
                pool.memset(fr[:, :, :, N:N + 2], 0.0).then_inc(s_zero, 1)
                pool.wait_ge(s_zero, 4)

                def stage(b, par, s, u, first):
                    n = b * PER + s
                    ch = Counted(pool, s_pool, b * BATCH + s * EACH + (PADS if first else PADS + EDGE))
                    w = s * STEP
                    at = bass.ds(w, SPAN)
                    ch.then(pool.tensor_tensor(stu[:, u, :, :], Gs[:, par, 0, :, at], Gs[:, par, 1, :, at], ALU.add))
                    pool.wait_ge(s_S, n + 1)
                    for c in range(2):
                        g = stu[:, u, c, :]
                        win = bass.AP(tensor=g.tensor, offset=g.offset, ap=[list(g.ap[0]), [1, G * GP], [1, KNN]])
                        ch.inc(pool.tensor_tensor(
                            d16[:, u, c, :, :], win,
                            fr[:, par, c, bass.ds(w, G * GP)].unsqueeze(2).to_broadcast([P, G * GP, KNN]),
                            ALU.subtract))
                    if first:
                        pool.wait_ge(s_pool, ch.start + ch.n)
                        for i in range(EDGE):
                            ch.inc(pool.tensor_tensor(
                                d16[:, u, :, i, 0:PAD - i],
                                stu[:, u, :, i + 2 * PAD:i + 2 * PAD + 1].to_broadcast([P, 2, PAD - i]),
                                fr[:, par, :, i:i + 1].to_broadcast([P, 2, PAD - i]), ALU.subtract))

                with pool.Fori(0, B // 2) as t:
                    for par in range(2):
                        b = 2 * t + par
                        pool.wait_ge(s_load[par], t * (16 * NLOAD) + 16 * NLOAD)
                        edge = Gs[:, par, :, :, :].rearrange("p q c n -> p (q c) n")
                        pool.tensor_tensor(edge[:, :, PAD + N:GW],
                                           edge[:, :, PAD + N - 1:PAD + N].to_broadcast([P, 4, GW - PAD - N]),
                                           none[:, :].unsqueeze(2).to_broadcast([P, 4, GW - PAD - N]),
                                           ALU.add).then_inc(s_pool, 1)
                        pool.wait_ge(s_pool, b * BATCH + PADS)
                        stage(b, par, 0, 0, True)
                        stage(b, par, 1, 1, False)
                        with pool.Fori(1, PER // 2) as q:
                            for u in range(2):
                                stage(b, par, 2 * q + u, u, False)

            @block.tensor
            def _(pe):
                pe.wait_ge(s_w, 16 * 3)
                pe.sem_inc(s_W, 2)
                pe.sem_inc(s_Y, 2)
                pe.sem_inc(s_S, 2)

                mk = mkr[:, :, :].rearrange("k v n -> k (v n)")
                cf = centre[:, :, :, :].rearrange("p b h o -> p (b h o)")
                NS = G * 4 * WIN

                def scores(n, u, first):
                    pe.wait_ge(s_pool, staged(n))
                    pe.wait_ge(s_sth, 2 * (n + 1))
                    if not first:
                        pe.wait_ge(s_sub, n - 1)
                    at = (n // 2) % (PER // 2) * NS + u * NS
                    pe.matmul(psS[u][0:ROWS, 0:NS], mkl[:, :], mk[:, bass.ds(at, NS)], start=True, stop=False)
                    for g in range(G):
                        for c in range(2):
                            for hl in range(2):
                                last = pe.matmul(psS[u][0:ROWS, 80 * g + 40 * c:80 * g + 40 * c + 40],
                                                 d16[:, u, c, GP * g:GP * g + GP, :],
                                                 sth[:, u, hl, c, GP * g:GP * g + WIN, :],
                                                 start=False, stop=(g == G - 1 and c == 1 and hl == 1))
                    last.then_inc(s_S, 1)

                def turn(n, u, first):
                    pe.wait_ge(s_A, n + 1)
                    if not first:
                        pe.wait_ge(s_AT, n)
                    for g in range(G):
                        last = pe.transpose(psA[:, g // 3, ROWS * (g % 3):ROWS * (g % 3) + ROWS],
                                            A[:, u, g // 2, P * (g % 2):P * (g % 2) + P], k.id32[0:ROWS, 0:ROWS])
                    last.then_inc(s_T, 1)

                def windows(n, u, first):
                    if not first:
                        pe.wait_ge(s_GW, n)
                    for w in range(3):
                        for c in range(2):
                            for q, (x, y) in enumerate(((0, 0), (0, 1), (1, 0))):
                                last = pe.matmul(psW[64 * c:64 * c + 64, O * w:O * w + O],
                                                 sth[:, u, x, c, 2 * GP * w:2 * GP * w + 32, :],
                                                 wn[:, y, c, :], start=(q == 0), stop=(q == 2))
                    last.then_inc(s_W, 1)

                def sums(n, u, first):
                    pe.wait_ge(s_AT, n + 1)
                    pe.wait_ge(s_GW, n + 1)
                    if not first:
                        pe.wait_ge(s_done, 4 * n)
                    for j, (p0, pn) in enumerate(((0, 4 * GP), (4 * GP, STEP - 4 * GP))):
                        for hl in range(2):
                            pe.matmul(psY[0:O, j, 0:pn * KNN], cf[:, bass.ds(n // 2 * (2 * O) + hl * O, O)],
                                      spread[:, u, p0 * KNN:(p0 + pn) * KNN], start=(hl == 0), stop=False)
                    for w in range(3):
                        cols = (2 * GP if w < 2 else STEP - 4 * GP) * KNN
                        at = 2 * ROWS * w if w < 2 else 0
                        last = pe.matmul(psY[0:O, w // 2, at:at + cols], GWs[:, u, w, :],
                                         AT[:, u, 2 * ROWS * w:2 * ROWS * w + cols], start=False, stop=(w > 0))
                    last.then_inc(s_Y, 1)

                scores(0, 0, True)
                windows(0, 0, True)
                scores(1, 1, True)
                turn(0, 0, True)
                windows(1, 1, False)
                scores(2, 0, False)
                sums(0, 0, True)
                with pe.Fori(1, STEPS // 2 - 1) as t:
                    for u in range(2):
                        n = 2 * t + u
                        turn(n - 1, 1 - u, False)
                        windows(n, u, False)
                        scores(n + 1, 1 - u, False)
                        sums(n - 1, 1 - u, False)
                turn(STEPS - 3, 1, False)
                windows(STEPS - 2, 0, False)
                scores(STEPS - 1, 1, False)
                sums(STEPS - 3, 1, False)
                turn(STEPS - 2, 0, False)
                windows(STEPS - 1, 1, False)
                sums(STEPS - 2, 0, False)
                turn(STEPS - 1, 1, False)
                sums(STEPS - 1, 1, False)

            @block.scalar
            def _(act):
                Gf = Gs[:, :, :, :, :].rearrange("p b q c n -> p (b q c) n")
                act.wait_ge(s_zero, 4)

                def windows(n, u):
                    act.wait_ge(s_W, n + 1)
                    act.wait_ge(s_pool, n // PER * BATCH + PADS)
                    for h in range(2):
                        r = slice(64 * h, 64 * h + 64)
                        act.copy(sth[r, u, :, :, :, h].rearrange("p q c n -> p (q c) n"),
                                 Gf[r, bass.ds(n // PER % 2 * 4, 4), bass.ds(n % PER * STEP, SPAN)]
                                 ).then_inc(s_sth, 1)

                def turned(n, u):
                    act.wait_ge(s_T, n + 1)
                    act.wait_ge(s_Y, n + 1)
                    act.copy(AT[:, u, :].rearrange("p (j n) -> p j n", j=2), psA[:, :, 0:3 * ROWS]).then_inc(s_AT, 1)

                def exps(n, u):
                    act.wait_ge(s_sub, n + 1)
                    act.activation(E[:, u, :, :], E[:, u, :, :], ACT.Exp, scale=0.125).then_inc(s_exp, 1)

                def evacuate(n, u):
                    act.wait_ge(s_W, n + 3)
                    act.wait_ge(s_Y, n + 1)
                    act.mul(GWs[:, u, :, :], psW[:, 0:3 * O].rearrange("p (w o) -> p w o", w=3), 1 / WSCALE
                            ).then_inc(s_GW, 1)

                windows(0, 0)
                windows(1, 1)
                exps(0, 0)
                evacuate(0, 0)
                windows(2, 0)
                turned(0, 0)
                exps(1, 1)
                evacuate(1, 1)
                windows(3, 1)
                with act.Fori(1, STEPS // 2 - 1) as t:
                    for u in range(2):
                        n = 2 * t + u
                        turned(n - 1, 1 - u)
                        exps(n, u)
                        evacuate(n, u)
                        windows(n + 2, u)
                for n in (STEPS - 2, STEPS - 1):
                    turned(n - 1, (n - 1) % 2)
                    exps(n, n % 2)
                    evacuate(n, n % 2)
                turned(STEPS - 1, 1)

            @block.vector
            def _(v):
                v.memset(A[:, :, :, :], 0.0).then_inc(s_dve, 1)
                v.wait_ge(s_dve, 1)
                EV = 3
                mh = maxh.rearrange("o b n -> o (b n)")

                def soften(n, u):
                    v.wait_ge(s_S, n + 3)
                    S = psS[u][0:ROWS, 0:G * 4 * WIN].rearrange("p (g n h) -> p g h n", n=WIN, h=2)
                    e = E[:, u, :, :, :].rearrange("p g n h -> p g h n")
                    m = top[:, u, :].rearrange("p (g h) -> p g h", h=2)
                    v.tensor_reduce(m, S, AX.X, ALU.max).then_inc(s_dve, 1)
                    v.wait_ge(s_dve, n * EV + 2)
                    v.tensor_tensor(e, S, m.unsqueeze(3).to_broadcast([ROWS, G * 2, 2, WIN]),
                                    ALU.subtract).then_inc(s_sub, 1)

                def collect(n):
                    v.wait_ge(s_Y, n + 3)
                    for j, (p0, pn) in enumerate(((0, 4 * GP), (4 * GP, STEP - 4 * GP))):
                        v.bn_stats(stat[:, :, j, :].rearrange("o n e -> o n e")[:, bass.ds(n, 1), :],
                                   psY[0:O, j, 0:pn * KNN]).then_inc(s_done, 1)
                        v.tensor_reduce(mh[:, bass.ds(n * STEP + p0, pn)],
                                        psY[0:O, j, 0:pn * KNN].rearrange("o (i a) -> o i a", a=KNN),
                                        AX.X, ALU.max).then_inc(s_done, 1)

                def weights(n, u, first):
                    v.wait_ge(s_exp, n + 1)
                    v.tensor_reduce(tot[:, u, :].rearrange("p (g h) -> p g h", h=2),
                                    E[:, u, :, :, :].rearrange("p g n h -> p g h n"), AX.X, ALU.add).then_inc(s_dve, 1)
                    v.wait_ge(s_dve, n * EV + 3)
                    v.reciprocal(inv[:, u, :], tot[:, u, :]).then_inc(s_dve, 1)
                    v.wait_ge(s_dve, n * EV + 4)
                    if not first:
                        v.wait_ge(s_T, n - 1)
                    a = A[:, u, :, :]
                    out = bass.AP(tensor=a.tensor, offset=a.offset,
                                  ap=[list(a.ap[0]), [AW // 2, G], [P // 2, 2], [1, 2 * WIN]])
                    r = inv[:, u, :]
                    r = bass.AP(tensor=r.tensor, offset=r.offset,
                                ap=[list(r.ap[0]), [2, G * 2], [0, WIN], [1, 2]])
                    v.tensor_tensor(out, E[:, u, :, :, :].rearrange("p g n h -> p (g n h)"), r,
                                    ALU.mult).then_inc(s_A, 1)

                soften(0, 0)
                weights(0, 0, True)
                soften(1, 1)
                weights(1, 1, True)
                with v.Fori(1, STEPS // 2) as t:
                    for u in range(2):
                        n = 2 * t + u
                        soften(n, u)
                        collect(n - 2)
                        weights(n, u, False)
                collect(STEPS - 2)
                collect(STEPS - 1)
                v.wait_ge(s_done, 4 * STEPS)
                for b in range(B):
                    v.bn_aggr(mv[0:O, b, :], stat[:, PER * b:PER * b + PER, :, :].rearrange("o n j e -> o (n j e)"))


def instance_norm(k, x, mv, hb, O):
    nc = k.nc
    with ExitStack() as ctx:
        sb, ps, sem = placing(k, ctx)
        var = sb("var", [P, B])
        std = sb("std", [P, B])
        r = sb("r", [P, B])
        r2 = sb("r2", [P, B])
        mean = sb("mean", [P, B])
        s_var = sem("s_var")
        s_std = sem("s_std")
        s_chain = sem("s_chain")
        with nc.Block() as block:
            @block.scalar
            def _(act):
                act.wait_ge(s_var, 1)
                act.activation(std[0:O, :], var[0:O, :], ACT.Sqrt).then_inc(s_std, 1)

            @block.vector
            def _(v):
                ch = Counted(v, s_chain)
                v.tensor_scalar(var[0:O, :], mv[0:O, :, 1], EPS, None, ALU.add).then_inc(s_var, 1)
                if hb is not None:
                    ch.then(v.tensor_scalar(mean[0:O, :], mv[0:O, :, 0], hb[0:O, :], None, ALU.add))
                v.wait_ge(s_std, 1)
                rsqrt(ch, v, r[0:O, :], r2[0:O, :], std[0:O, :], var[0:O, :])
                for b in range(B):
                    if hb is not None:
                        ch.inc(v.tensor_scalar(x[0:O, b, :], x[0:O, b, :], hb[0:O, :], mean[0:O, b:b + 1],
                                               ALU.add, ALU.subtract))
                    else:
                        ch.inc(v.tensor_scalar(x[0:O, b, :], x[0:O, b, :], mv[0:O, b, 0:1], None, ALU.subtract))
                v.wait_ge(s_chain, ch.n)
                for b in range(B):
                    ch.inc(v.scalar_tensor_tensor(x[0:O, b, :], x[0:O, b, :], 0.2, x[0:O, b, :], ALU.mult, ALU.max))
                v.wait_ge(s_chain, ch.n)
                for b in range(B):
                    v.tensor_scalar(x[0:O, b, :], x[0:O, b, :], r[0:O, b:b + 1], None, ALU.mult)


def rsqrt(ch, v, r, t, std, var):
    ch.then(v.reciprocal(r, std))
    ch.then(v.tensor_tensor(t, r, r, ALU.mult))
    ch.then(v.tensor_tensor(t, t, var, ALU.mult))
    ch.then(v.tensor_scalar(t, t, -0.5, 1.5, ALU.mult, ALU.add))
    ch.then(v.tensor_tensor(r, r, t, ALU.mult))


def neighbour_counts(i):
    start, end = max(0, i - KNN // 2), min(N, i + KNN // 2 + 1)
    pos = [min(start + a, end - 1) for a in range(KNN)]
    return {p: pos.count(p) for p in pos}


def split_bf16(a):
    parts = []
    for _ in range(3):
        part = a.astype(NP_BF16)
        parts.append(part)
        a = a - part.astype(np.float32)
    return parts


def window_masks():
    pick = np.kron(np.eye(GP, dtype=np.float32), np.ones((1, KNN), np.float32))
    bias = np.full((GP, 9, G, 2, WIN, 2), -2.0 ** 30, np.float32)
    for kind in range(9):
        s = 0 if kind == 0 else PER - 1 if kind == 8 else 1
        for g in range(G):
            for r in range(GP):
                i = s * STEP + GP * g + r
                count = neighbour_counts(i) if i < N else {p: 1 for p in range(i - 5, N)}
                for p, c in count.items():
                    bias[r, kind, g, :, p - (s * STEP + GP * g - PAD), :] = 8 * np.log(np.float32(c))
    bias = bias.reshape(GP, -1)
    return (np.concatenate(split_bf16(pick)[:1] * 3), np.concatenate(split_bf16(bias)).reshape(3 * GP, 9, -1))


def lin_layouts(w, perm):
    w = np.asarray(w)
    cols = [((64 + 32 * c + 16 * h + x) * M + perm.index(m)) for c in range(2) for h in range(2)
            for m in range(M) for x in range(16)]
    return np.ascontiguousarray(w), np.ascontiguousarray(w[:, cols])


def points_out(k):
    nc = k.nc
    with ExitStack() as ctx:
        sb, ps, sem = placing(k, ctx)
        w3 = sb("w3", [P, 2, C])
        x3 = sb("x3", [C, B, N])
        xin = sb("xin", [C, B, N])
        st = sb("st", [C, B, 2, 6])
        mv3 = sb("mv3", [C, B, 2])
        psH = [ps(f"psH{i}", [P, 2, 512]) for i in range(2)]
        s_w3 = sem("s_w3")
        s_xin = sem("s_xin")
        s_h = sem("s_h")
        s_ev = sem("s_ev")
        s_st = sem("s_st")
        with nc.Block() as block:
            @block.sync
            def _(sp):
                sp.dma_start(w3[:, :, :], k.given["w_conv3"].rearrange("(h p) o -> p h o", p=P)).then_inc(s_w3, 16)
                sp.dma_start(xin[:, :, :], k.given["x"].rearrange("b c n -> c b n")).then_inc(s_xin, 16)
                sp.wait_ge(s_xin, 16)

            @block.tensor
            def _(pe):
                pe.wait_ge(s_w3, 16)
                for b in range(B):
                    if b >= 2:
                        pe.wait_ge(s_ev, b - 1)
                    for h in range(2):
                        for c, src in enumerate((k.F, k.M2)):
                            last = pe.matmul(psH[b % 2][0:C, h, :], w3[:, c, :], src[:, b, 512 * h:512 * h + 512],
                                             start=(c == 0), stop=(c == 1))
                    last.then_inc(s_h, 1)

            @block.scalar
            def _(act):
                for b in range(B):
                    act.wait_ge(s_h, b + 1)
                    act.copy(x3[:, b, :].rearrange("c (h n) -> c h n", h=2), psH[b % 2][0:C, :, :]).then_inc(s_ev, 1)

            @block.vector
            def _(v):
                for b in range(B):
                    v.wait_ge(s_ev, b + 1)
                    for h in range(2):
                        v.bn_stats(st[:, b, h, :], x3[:, b, 512 * h:512 * h + 512]).then_inc(s_st, 1)
                v.wait_ge(s_st, 2 * B)
                for b in range(B):
                    v.bn_aggr(mv3[:, b, :], st[:, b, :, :])
        instance_norm(k, x3, mv3, None, C)
        s_add = sem("s_add")
        s_x1 = sem("s_x1")
        with nc.Block() as block:
            @block.vector
            def _(v):
                for b in range(B):
                    v.tensor_tensor(x3[:, b, :], x3[:, b, :], xin[:, b, :], ALU.add).then_inc(s_add, 1)

            @block.sync
            def _(sp):
                for b in range(B):
                    sp.wait_ge(s_add, b + 1)
                    sp.dma_start(k.d_x1[C * b:C * b + C, :], x3[:, b, :]).then_inc(s_x1, 16)
                sp.wait_ge(s_x1, 16 * B)


TOK = B * C
TB = TOK // P
KC = N // P


def token_norm(k, X, xh, xl, load):
    nc = k.nc
    with ExitStack() as ctx:
        sb, ps, sem = placing(k, ctx)
        xn = sb("xn", [P, TB, N])
        st = sb("st", [P, TB, 2, 6])
        mv = sb("mv", [P, TB, 2])
        var = sb("var", [P, TB])
        std = sb("std", [P, TB])
        r = sb("r", [P, TB])
        t = sb("t", [P, TB])
        psX = [ps(f"psX{i}", [P, 4, P]) for i in range(4)]
        s_x = sem("s_x")
        s_st = sem("s_st")
        s_var = sem("s_var")
        s_std = sem("s_std")
        s_chain = sem("s_chain")
        s_xn = sem("s_xn")
        s_T = sem("s_T")
        s_hi = sem("s_hi")
        s_lo = sem("s_lo")
        with nc.Block() as block:
            @block.sync
            def _(sp):
                if load:
                    sp.dma_start(X[:, :, :], k.d_x1.rearrange("(t p) n -> p t n", p=P)).then_inc(s_x, 16)

            @block.vector
            def _(v):
                ch = Counted(v, s_chain)
                if load:
                    v.wait_ge(s_x, 16)
                for b in range(TB):
                    for h in range(2):
                        v.bn_stats(st[:, b, h, :], X[:, b, 512 * h:512 * h + 512]).then_inc(s_st, 1)
                v.wait_ge(s_st, 2 * TB)
                for b in range(TB):
                    ch.inc(v.bn_aggr(mv[:, b, :], st[:, b, :, :]))
                v.wait_ge(s_chain, ch.n)
                v.tensor_scalar(var[:, :], mv[:, :, 1], EPS, None, ALU.add).then_inc(s_var, 1)
                v.wait_ge(s_std, 1)
                rsqrt(ch, v, r[:, :], t[:, :], std[:, :], var[:, :])
                for b in range(TB):
                    v.tensor_scalar(xn[:, b, :], X[:, b, :], mv[:, b, 0:1], r[:, b:b + 1],
                                    ALU.subtract, ALU.mult).then_inc(s_xn, 1)
                for c in range(KC):
                    v.wait_ge(s_hi, c + 1)
                    v.tensor_tensor(xl[:, c, :], psX[c % 4][:, :, :].rearrange("p t n -> p (t n)"), xh[:, c, :],
                                    ALU.subtract).then_inc(s_lo, 1)

            @block.scalar
            def _(act):
                act.wait_ge(s_var, 1)
                act.activation(std[:, :], var[:, :], ACT.Sqrt).then_inc(s_std, 1)
                for c in range(KC):
                    act.wait_ge(s_T, c + 1)
                    act.copy(xh[:, c, :], psX[c % 4][:, :, :].rearrange("p t n -> p (t n)")).then_inc(s_hi, 1)

            @block.tensor
            def _(pe):
                pe.wait_ge(s_xn, TB)
                for c in range(KC):
                    if c >= 4:
                        pe.wait_ge(s_lo, c - 3)
                    for b in range(TB):
                        last = pe.transpose(psX[c % 4][:, b, :], xn[:, b, c * P:(c + 1) * P], k.id32[:, :])
                    last.then_inc(s_T, 1)


NH, NKV, HD = 32, 8, 128
REP = NH // NKV
def split_scales(v, ch, dst, src, done):
    for p in range(3):
        for _ in range(p):
            ch.then(v.tensor_copy(dst[p], src[p]))
            ch.then(v.tensor_tensor(src[p], src[p], dst[p], ALU.subtract))
        last = v.tensor_copy(dst[p], src[p])
        if p < 2:
            ch.then(last)
    last.then_inc(done, 1)


def attention(k, xh, xl, ctxh, ctxl):
    nc = k.nc
    with ExitStack() as ctx:
        sb, ps, sem = placing(k, ctx)
        QC, KV = REP * HD, 2 * HD
        NBLK = 2 * KC
        ROT = 1 + REP
        qw = sb("qw", [P, 2, KC // 2, QC], I32)
        kvw = sb("kvw", [P, 2, KC // 2, KV], I32)
        sc = sb("sc", [96, NKV, QC + KV], BF16)
        with ExitStack() as scales:
            sb1, _, sem1 = placing(k, scales)
            raw = sb1("raw", [96, NH * HD // 4])
            s_pick = sem1("s_pick")
            s_raw = sem1("s_raw")
            s_zero = sem1("s_zero")
            s_sc = sem1("s_sc")
            s_chain = sem1("s_chain")
            with nc.Block() as block:
                @block.sync
                def _(sp):
                    sp.dma_start(k.pick[:, :, :], k.given["c_pick"]).then_inc(s_pick, 16)
                    parts = [k.given["sq"][:, 1024 * i:1024 * i + 1024] for i in range(4)] + [k.given["sk"], k.given["sv"]]
                    for i, src in enumerate(parts):
                        if i:
                            sp.wait_ge(s_sc, i)
                        for p in range(3):
                            sp.dma_start(raw[32 * p:32 * p + KC, :], src).then_inc(s_raw, 16)
                    sp.wait_ge(s_pick, 16)

                @block.gpsimd
                def _(pool):
                    pool.memset(sc[:, :, :], 0.0).then_inc(s_zero, 1)

                @block.vector
                def _(v):
                    v.wait_ge(s_zero, 1)
                    ch = Counted(v, s_chain)
                    for i in range(6):
                        v.wait_ge(s_raw, 16 * 3 * (i + 1))
                        g = 2 if i < 4 else NKV
                        src = [raw[32 * p:32 * p + KC, :].rearrange("r (g n) -> r g n", g=g) for p in range(3)]
                        if i < 4:
                            dst = [sc[32 * p:32 * p + KC, 2 * i:2 * i + 2, 0:QC] for p in range(3)]
                        else:
                            o = QC + HD * (i - 4)
                            dst = [sc[32 * p:32 * p + KC, :, o:o + HD] for p in range(3)]
                        split_scales(v, ch, dst, src, s_sc)

        wt = sb("wt", [P, 2, QC])
        wh = sb("wh", [P, 2, KC, QC + KV], F16)
        wl = sb("wl", [P, 2, KC, QC + KV], F16)
        cos = sb("cos", [P, C])
        sin = sb("sin", [P, C])
        rc = sb("rc", [P, 2, B, C])
        rs = sb("rs", [P, 2, B, C])
        kr = sb("kr", [P, B, C])
        qr = sb("qr", [P, B, REP, C])
        vT = sb("vT", [P, TOK])
        V = sb("V", [P, TB, HD])
        mask = sb("mask", [P, C], BF16)
        idb = sb("idb", [P, P], BF16)
        Pr = sb("Pr", [P, 2, B, C])
        top = sb("top", [P, 2, B])
        tot = sb("tot", [P, 2, B])
        inv = sb("inv", [P, 2, B])
        PT = sb("PT", [P, 2, TB, P])
        psB = [ps(f"psB{i}", [P, 512]) for i in range(2)]
        psP = [ps(f"psP{i}", [P, 512]) for i in range(2)]
        psS = ps("psS", [P, B, C])
        psT = ps("psT", [P, TB, P])
        psC = ps("psC", [P, 2, TB, 2, C])
        s_c = sem("s_c")
        s_wq = [sem("s_wq0"), sem("s_wq1")]
        s_bc = sem("s_bc")
        s_deq = sem("s_deq")
        s_hi = sem("s_hi")
        s_lo = sem("s_lo")
        s_pr = sem("s_pr")
        s_rope = sem("s_rope")
        s_qk = sem("s_qk")
        s_vT = sem("s_vT")
        s_tr = sem("s_tr")
        s_V = sem("s_V")
        s_S = sem("s_S")
        s_soft = sem("s_soft")
        s_sub = sem("s_sub")
        s_exp = sem("s_exp")
        s_prob = sem("s_prob")
        s_PT = sem("s_PT")
        s_ctx = sem("s_ctx")
        s_ch = sem("s_ch")
        s_cl = sem("s_cl")

        def block_of(j):
            half, r = divmod(j, KC)
            c = half * (KC // 2) + r % (KC // 2)
            return (c, 0, QC) if r < KC // 2 else (c, QC, KV)

        with nc.Block() as block:
            @block.sync
            def _(sp):
                def load(g, half):
                    c = slice(half * (KC // 2), (half + 1) * (KC // 2))
                    sp.dma_start(qw[:, half, :, :], k.given["qw_q"].rearrange("(c p) n -> p c n", p=P)
                                 [:, c, bass.ds(g * QC, QC)]).then_inc(s_wq[half], 16)
                    for i, w in enumerate((k.given["qw_k"], k.given["qw_v"])):
                        sp.dma_start(kvw[:, half, :, HD * i:HD * i + HD], w.rearrange("(c p) n -> p c n", p=P)
                                     [:, c, bass.ds(g * HD, HD)]).then_inc(s_wq[half], 16)

                for half in range(2):
                    load(0, half)
                for dst, src in ((cos, k.given["c_cos"]), (sin, k.given["c_sin"]), (mask, k.given["c_causal"]), (idb, k.given["c_idb"])):
                    sp.dma_start(dst[:, :], src).then_inc(s_c, 16)
                with sp.Fori(1, NKV) as g:
                    for half in range(2):
                        sp.wait_ge(s_deq, g * NBLK + (half - 1) * KC)
                        load(g, half)

            @block.tensor
            def _(pe):
                scf = sc[:, :, :].rearrange("r g n -> r (g n)")

                def spread(g, j, first=False):
                    if not first:
                        pe.wait_ge(s_deq, g * NBLK + (j - 1))
                    c, o, w = block_of(j)
                    pe.matmul(psB[j % 2][:, 0:w], k.pick[:, c, :], scf[:, bass.ds(g * (QC + KV) + o, w)],
                              start=True, stop=True).then_inc(s_bc, 1)

                def project(g, u, slot, first):
                    if slot == 0:
                        pe.wait_ge(s_lo, (g + 1) * NBLK)
                    if slot == 3:
                        pe.wait_ge(s_vT, g + 1)
                    elif not (first and slot < 2):
                        pe.wait_ge(s_rope, g * ROT + {0: -1, 1: 0, 2: 1, 4: 2, 5: 3}[slot])
                    o = {0: QC, 1: QC + HD}.get(slot, (slot - 2) * HD)
                    for c in range(KC):
                        for i, (w, x) in enumerate(((wh, xh), (wh, xl), (wl, xh))):
                            last = pe.matmul(psP[slot % 2][:, :], w[:, u, c, o:o + HD], x[:, c, :],
                                             start=(c == 0 and i == 0), stop=(c == KC - 1 and i == 2))
                    last.then_inc(s_pr, 1)

                def values(g, first):
                    pe.wait_ge(s_vT, g + 1)
                    if not first:
                        pe.wait_ge(s_PT, 2 * g)
                    for b in range(TB):
                        last = pe.transpose(psT[:, b, :], vT[:, b * P:(b + 1) * P], k.id32[:, :])
                    last.then_inc(s_tr, 1)

                def scores(g, h, first):
                    if first and h == 0:
                        pe.wait_ge(s_c, 64)
                    if h == 0:
                        pe.wait_ge(s_qk, (g + 1) * ROT)
                    if not (first and h == 0):
                        pe.wait_ge(s_sub, 2 * g + h)
                    pe.matmul(psS[:, :, :], idb[:, :], mask[:, :].unsqueeze(1).to_broadcast([P, B, C]),
                              start=True, stop=False)
                    for b in range(B):
                        last = pe.matmul(psS[:, b, :], qr[:, b, 2 * h:2 * h + 2, :], kr[:, b, :],
                                         start=False, stop=(b == B - 1))
                    last.then_inc(s_S, 1)

                def turn(g, h):
                    pe.wait_ge(s_prob, 2 * g + (h + 1))
                    if h == 0:
                        pe.wait_ge(s_V, g + 1)
                    else:
                        pe.wait_ge(s_PT, 2 * g + 1)
                    for b in range(TB):
                        last = pe.transpose(psT[:, b, :], Pr[:, h, 2 * b:2 * b + 2, :], k.id32[:, :])
                    last.then_inc(s_tr, 1)

                def context(g, h, first):
                    pe.wait_ge(s_PT, 2 * g + (h + 1))
                    if not (first and h == 0):
                        pe.wait_ge(s_cl, 2 * g + h)
                    for b in range(B):
                        r = slice(C * (b % 2), C * (b % 2) + C)
                        last = pe.matmul(psC[:, b % 2, b // 2, :, :], V[r, b // 2, :], PT[r, h, b // 2, :],
                                         start=True, stop=True)
                    last.then_inc(s_ctx, 1)

                def head(g, u, first, ahead):
                    j = iter(range(NBLK))

                    def some(n):
                        for _ in range(n if ahead else 0):
                            spread(g + 1, next(j))

                    for slot in range(2 + REP):
                        project(g, u, slot, first)
                        if slot == 2:
                            values(g, first)
                        some(2)
                    scores(g, 0, first)
                    some(1)
                    scores(g, 1, first)
                    some(1)
                    for h in range(2):
                        turn(g, h)
                        context(g, h, first)
                        some(1)

                for j in range(NBLK):
                    spread(0, j, j < 2)
                head(0, 0, True, True)
                with pe.Fori(0, (NKV - 2) // 2) as t:
                    head(2 * t + 1, 1, False, True)
                    head(2 * t + 2, 0, False, True)
                head(NKV - 1, 1, False, False)

            @block.vector
            def _(v):
                def dequant(g, j, first=False):
                    c, o, w = block_of(j)
                    half = j // KC
                    if j % KC == 0:
                        v.wait_ge(s_wq[half], g * 48 + 48)
                    v.wait_ge(s_bc, g * NBLK + (j + 1))
                    if not (first and j < 2):
                        v.wait_ge(s_lo, g * NBLK + (j - 1))
                    v.scalar_tensor_tensor(wt[:, j % 2, 0:w], (qw if o == 0 else kvw)[:, half, c % (KC // 2), :], 8.0,
                                           psB[j % 2][:, 0:w], ALU.subtract, ALU.mult).then_inc(s_deq, 1)

                def rotate(g, n, first):
                    slot = (0, 2, 3, 4, 5)[n]
                    v.wait_ge(s_pr, g * (2 + REP) + (slot + 1))
                    if not (first and n < 2):
                        v.wait_ge(s_qk, g * ROT + (n - 1))
                    x = psP[slot % 2][:, :].rearrange("p (b s) -> p b s", s=C)
                    cb = cos[:, :].unsqueeze(1).to_broadcast([P, B, C])
                    tb = sin[:, :].unsqueeze(1).to_broadcast([P, B, C])
                    H = HD // 2
                    v.tensor_tensor(rc[:, n % 2, :, :], x, cb, ALU.mult)
                    v.tensor_tensor(rs[0:H, n % 2, :, :], x[H:P], tb[H:P], ALU.mult)
                    v.tensor_tensor(rs[H:P, n % 2, :, :], x[0:H], tb[0:H], ALU.mult).then_inc(s_rope, 1)

                def soften(g, h):
                    v.wait_ge(s_S, 2 * g + (h + 1))
                    v.tensor_reduce(top[:, h, :], psS[:, :, :], AX.X, ALU.max).then_inc(s_soft, 1)
                    v.wait_ge(s_soft, 6 * g + (h + 1))
                    v.tensor_tensor(Pr[:, h, :, :], psS[:, :, :], top[:, h, :].unsqueeze(2).to_broadcast([P, B, C]),
                                    ALU.subtract).then_inc(s_sub, 1)

                def probabilities(g, h):
                    v.wait_ge(s_exp, 2 * g + (h + 1))
                    v.tensor_reduce(tot[:, h, :], Pr[:, h, :, :], AX.X, ALU.add).then_inc(s_soft, 1)
                    v.wait_ge(s_soft, 6 * g + (2 * h + 3))
                    v.reciprocal(inv[:, h, :], tot[:, h, :]).then_inc(s_soft, 1)
                    v.wait_ge(s_soft, 6 * g + (2 * h + 4))
                    v.tensor_tensor(Pr[:, h, :, :], Pr[:, h, :, :], inv[:, h, :].unsqueeze(2).to_broadcast([P, B, C]),
                                    ALU.mult).then_inc(s_prob, 1)

                def rest(g, h):
                    v.wait_ge(s_ch, 2 * g + (h + 1))
                    for r in range(2):
                        hi, lo = (c[:, bass.ds(g * REP + 2 * h, 2), :]
                                  .rearrange("p x (t r s) -> p r x t s", r=2, s=C)[:, r] for c in (ctxh, ctxl))
                        last = v.tensor_tensor(lo, psC[:, r, :, :, :].rearrange("p t x s -> p x t s"), hi,
                                               ALU.subtract)
                    last.then_inc(s_cl, 1)

                def head(g, first, ahead):
                    j = iter(range(NBLK))

                    def some(n):
                        for _ in range(n if ahead else 0):
                            dequant(g + 1, next(j))

                    for slot in range(2 + REP):
                        if slot != 1:
                            rotate(g, (0, None, 1, 2, 3, 4)[slot], first)
                        some(2)
                    soften(g, 0)
                    some(1)
                    soften(g, 1)
                    some(1)
                    probabilities(g, 0)
                    probabilities(g, 1)
                    for h in range(2):
                        rest(g, h)
                        some(1)

                for j in range(NBLK):
                    dequant(0, j, True)
                v.wait_ge(s_c, 64)
                head(0, True, True)
                with v.Fori(1, NKV - 1) as g:
                    head(g, False, True)
                head(NKV - 1, False, False)

            @block.scalar
            def _(act):
                def high(g, u, j):
                    c, o, w = block_of(j)
                    act.wait_ge(s_deq, g * NBLK + (j + 1))
                    act.copy(wh[:, u, c, o:o + w], wt[:, j % 2, 0:w]).then_inc(s_hi, 1)

                def head(g, u, ahead):
                    j = iter(range(NBLK))

                    def some(n):
                        for _ in range(n if ahead else 0):
                            high(g + 1, 1 - u, next(j))

                    some(2)
                    act.wait_ge(s_pr, g * (2 + REP) + 2)
                    act.mul(vT[:, :], psP[1][:, :], 1 / WSCALE).then_inc(s_vT, 1)
                    some(2)
                    act.wait_ge(s_tr, 3 * g + 1)
                    act.copy(V[:, :, :], psT[:, :, :]).then_inc(s_V, 1)
                    some(8)
                    for h in range(2):
                        act.wait_ge(s_sub, 2 * g + (h + 1))
                        act.activation(Pr[:, h, :, :], Pr[:, h, :, :], ACT.Exp, scale=float(HD) ** -0.5).then_inc(s_exp, 1)
                        some(1)
                    for h in range(2):
                        act.wait_ge(s_tr, 3 * g + (h + 2))
                        act.copy(PT[:, h, :, :], psT[:, :, :]).then_inc(s_PT, 1)
                        act.wait_ge(s_ctx, 2 * g + (h + 1))
                        for r in range(2):
                            hi = (ctxh[:, bass.ds(g * REP + 2 * h, 2), :]
                                  .rearrange("p x (t r s) -> p r x t s", r=2, s=C)[:, r])
                            last = act.copy(hi, psC[:, r, :, :, :].rearrange("p t x s -> p x t s"))
                        last.then_inc(s_ch, 1)
                        some(1)

                for j in range(NBLK):
                    high(0, 0, j)
                head(0, 0, True)
                with act.Fori(0, (NKV - 2) // 2) as t:
                    head(2 * t + 1, 1, True)
                    head(2 * t + 2, 0, True)
                head(NKV - 1, 1, False)

            @block.gpsimd
            def _(pool):
                def low(g, u, j):
                    c, o, w = block_of(j)
                    pool.wait_ge(s_hi, g * NBLK + (j + 1))
                    pool.tensor_tensor(wl[:, u, c, o:o + w], wt[:, j % 2, 0:w], wh[:, u, c, o:o + w],
                                       ALU.subtract).then_inc(s_lo, 1)

                def add(g, n, first):
                    if n == 0 and not first:
                        pool.wait_ge(s_S, 2 * g)
                    pool.wait_ge(s_rope, g * ROT + (n + 1))
                    pool.tensor_tensor(kr[:, :, :] if n == 0 else qr[:, :, n - 1, :], rc[:, n % 2, :, :],
                                       rs[:, n % 2, :, :], ALU.add).then_inc(s_qk, 1)

                def head(g, u, first, ahead):
                    j = iter(range(NBLK))

                    def some(n):
                        for _ in range(n if ahead else 0):
                            low(g + 1, 1 - u, next(j))

                    add(g, 0, first)
                    some(4)
                    for n in range(1, 1 + REP):
                        add(g, n, first)
                        some(2)
                    some(4)

                for j in range(NBLK):
                    low(0, 0, j)
                head(0, 0, True, True)
                with pool.Fori(0, (NKV - 2) // 2) as t:
                    head(2 * t + 1, 1, False, True)
                    head(2 * t + 2, 0, False, True)
                head(NKV - 1, 1, False, False)


def out_projection(k, X, ctxh, ctxl):
    nc = k.nc
    with ExitStack() as ctx:
        sb, ps, sem = placing(k, ctx)
        OCT, W, HALF = 8, 512, NH
        ow = sb("ow", [P, 2, OCT, W], I32)
        raw = sb("raw", [96, N])
        sc = sb("sc", [96, 3 * W], BF16)
        zero = sb("zero", [P, W], F16)
        wt = sb("wt", [P, 4, W])
        wh = sb("wh", [P, 4, W], F16)
        wl = sb("wl", [P, 4, W], F16)
        psB = [ps(f"psB{i}", [P, 512]) for i in range(2)]
        psO = [ps(f"psO{i}", [P, 512]) for i in range(TB)]
        s_raw = sem("s_raw")
        s_chain = sem("s_chain")
        s_sc = sem("s_sc")
        s_ow = [sem("s_ow0"), sem("s_ow1")]
        s_bc = sem("s_bc")
        s_deq = sem("s_deq")
        s_hi = sem("s_hi")
        s_lo = sem("s_lo")
        s_mm = sem("s_mm")
        s_half = sem("s_half")
        s_zero = sem("s_zero")
        s_xin = sem("s_xin")
        s_x = sem("s_x")

        AHEAD = 4

        def blocks(eng, each, begin=None, end=None):
            with eng.Fori(0, 2) as hf:
                if begin:
                    begin(hf)
                with eng.Fori(0, 2) as q:
                    for i in range(2 * OCT):
                        each(hf, q, i, hf * HALF + q * (2 * OCT) + i)
                if end:
                    end(hf)

        with nc.Block() as block:
            @block.sync
            def _(sp):
                for p in range(3):
                    sp.dma_start(raw[32 * p:32 * p + NH, :], k.given["so"]).then_inc(s_raw, 16)
                sp.dma_start(X[:, :, :], k.d_x1.rearrange("(t p) n -> p t n", p=P)).then_inc(s_xin, 16)
                wo = k.given["qw_o"].rearrange("(h p) n -> p h n", p=P)
                for o in range(8):
                    if o >= 2:
                        sp.wait_ge(s_deq, OCT * (o - 1))
                    sp.dma_start(ow[:, o % 2, :, :], wo[:, o % 4 * OCT:o % 4 * OCT + OCT, o // 4 * W:o // 4 * W + W]
                                 ).then_inc(s_ow[o % 2], 16)

            @block.tensor
            def _(pe):
                pickf = k.pick[:, :, :].rearrange("r h n -> r (h n)")
                cf = [c[:, :, :].rearrange("p h n -> p (h n)") for c in (ctxh, ctxl)]
                pe.sem_inc(s_mm, AHEAD)

                def spread(i, h, col):
                    pe.matmul(psB[i % 2][:, :], pickf[:, bass.ds(h * P, P)], sc[:, bass.ds(col, W)],
                              start=True, stop=True).then_inc(s_bc, 1)

                def clear(start):
                    for b in range(TB):
                        mm = pe.matmul(psO[b][:, :], zero[:, 0:P], zero[:, :], start=start, stop=not start)
                    return mm

                def begin(hf):
                    pe.wait_ge(s_x, hf * TB + 1)
                    clear(True)

                def each(hf, q, i, J):
                    pe.wait_ge(s_deq, J + 1)
                    spread(i, (J + 2) % HALF, (J + 2) // HALF * W)
                    pe.wait_ge(s_lo, J + (AHEAD + 1))
                    h = q * (2 * OCT) + i
                    for b in range(TB):
                        hi, lo = (c[:, bass.ds(h * TOK + P * b, P)] for c in cf)
                        for x, w in ((hi, wh), (lo, wh), (hi, wl)):
                            mm = pe.matmul(psO[b][:, :], x, w[:, i % AHEAD, :], start=False, stop=False)
                    mm.then_inc(s_mm, 1)

                pe.wait_ge(s_zero, 1)
                pe.wait_ge(s_sc, 1)
                for J in range(2):
                    spread(J, J, 0)
                blocks(pe, each, begin, lambda hf: clear(False).then_inc(s_half, 1))

            @block.vector
            def _(v):
                ch = Counted(v, s_chain)
                v.sem_inc(s_x, 1)
                v.wait_ge(s_zero, 2)
                v.wait_ge(s_raw, 48)
                split_scales(v, ch, [sc[32 * p:32 * p + NH, 0:N] for p in range(3)],
                             [raw[32 * p:32 * p + NH, :] for p in range(3)], s_sc)

                def each(hf, q, i, J):
                    if i % OCT == 0:
                        v.wait_ge(s_ow[i // OCT], hf * 32 + q * 16 + 16)
                    v.wait_ge(s_bc, J + 1)
                    v.wait_ge(s_lo, J + 1)
                    v.scalar_tensor_tensor(wt[:, i % AHEAD, :], ow[:, i // OCT, i % OCT, :], 8.0, psB[i % 2][:, :],
                                           ALU.subtract, ALU.mult).then_inc(s_deq, 1)

                def end(hf):
                    v.wait_ge(s_half, hf + 1)
                    for b in range(TB):
                        x = X[:, b, bass.ds(hf * W, W)]
                        v.scalar_tensor_tensor(x, psO[b][:, :], 1 / WSCALE, x, ALU.mult, ALU.add).then_inc(s_x, 1)

                v.wait_ge(s_xin, 16)
                blocks(v, each, end=end)

            @block.scalar
            def _(act):
                def each(hf, q, i, J):
                    act.wait_ge(s_deq, J + 1)
                    act.wait_ge(s_mm, J + 1)
                    act.copy(wh[:, i % AHEAD, :], wt[:, i % AHEAD, :]).then_inc(s_hi, 1)

                blocks(act, each)

            @block.gpsimd
            def _(pool):
                pool.memset(zero[:, :], 0.0).then_inc(s_zero, 1)
                pool.memset(sc[:, :], 0.0).then_inc(s_zero, 1)
                pool.sem_inc(s_lo, AHEAD)

                def each(hf, q, i, J):
                    pool.wait_ge(s_hi, J + 1)
                    pool.tensor_tensor(wl[:, i % AHEAD, :], wt[:, i % AHEAD, :], wh[:, i % AHEAD, :],
                                       ALU.subtract).then_inc(s_lo, 1)

                blocks(pool, each)


NE, RANK = 8, 32


def feed_forward(k, X, xh, xl):
    nc = k.nc
    with ExitStack() as ctx:
        sb, ps, sem = placing(k, ctx)
        WA = N + RANK
        w = sb("w", [P, 2, WA])
        wh = sb("wh", [P, KC, WA], F16)
        wl = sb("wl", [P, KC, WA], F16)
        bias = sb("bias", [P, N])
        bm = sb("bm", [RANK, N])
        lim = sb("lim", [NE, RANK])
        limT = sb("limT", [RANK, NE])
        odd = sb("odd", [P, 1])
        H = sb("H", [P, TB, N])
        zT = sb("zT", [RANK, TOK])
        zp = sb("zp", [RANK, TOK])
        lg = sb("lg", [P, 2, TB, NE])
        e = sb("e", [P, TB, NE])
        g = sb("g", [P, TB, NE])
        best = sb("best", [P, TB, NE])
        one = sb("one", [P, 16])
        mx = sb("mx", [P, 2])
        mxa = sb("mxa", [P, 2])
        gT = sb("gT", [NE, TOK])
        psH = [ps(f"psH{i}", [P, 512]) for i in range(4)]
        psZ = ps("psZ", [RANK, TOK])
        psD = ps("psD", [P, TB, NE])
        psG = ps("psG", [NE, TOK])
        s_c = sem("s_c")
        s_w = [sem("s_w0"), sem("s_w1")]
        s_hi = sem("s_hi")
        s_lo = sem("s_lo")
        s_z = sem("s_z")
        s_zT = sem("s_zT")
        s_h = sem("s_h")
        s_H = sem("s_H")
        s_d = sem("s_d")
        s_mx = sem("s_mx")
        s_all = sem("s_all")
        s_act = sem("s_act")
        s_need = sem("s_need")
        s_chain = sem("s_chain")
        s_g = sem("s_g")
        s_gT = sem("s_gT")
        s_gc = sem("s_gc")
        s_p = sem("s_p")
        s_zp = sem("s_zp")
        s_dl = sem("s_dl")
        s_y = sem("s_y")
        s_out = sem("s_out")
        tiles = [(b, h) for h in range(2) for b in range(TB)]

        with nc.Block() as block:
            @block.sync
            def _(sp):
                sp.dma_start(bias[:, :], k.given["ffn_b"].partition_broadcast(P)).then_inc(s_c, 16)
                sp.dma_start(bm[:, :], k.given["ffn_Bmat"]).then_inc(s_c, 16)
                sp.dma_start(lim[:, :], k.given["ffn_lim"]).then_inc(s_c, 16)
                sp.dma_start(limT[:, :], k.given["ffn_limT"]).then_inc(s_c, 16)
                sp.dma_start(odd[:, :], k.given["c_odd"]).then_inc(s_c, 16)
                for c in range(KC):
                    if c >= 2:
                        sp.wait_ge(s_lo, c - 1)
                    sp.dma_start(w[:, c % 2, 0:N], k.given["ffn_WT"][c * P:(c + 1) * P, :]).then_inc(s_w[c % 2], 16)
                    sp.dma_start(w[:, c % 2, N:WA], k.given["ffn_A"][c * P:(c + 1) * P, :]).then_inc(s_w[c % 2], 16)
                for i, (b, h) in enumerate(tiles):
                    sp.wait_ge(s_y, i + 1)
                    sp.dma_start(k.given["out"][b * P:(b + 1) * P, 512 * h:512 * h + 512], X[:, b, 512 * h:512 * h + 512]
                                 ).then_inc(s_out, 16)
                sp.wait_ge(s_out, 16 * len(tiles))

            @block.scalar
            def _(act):
                for c in range(KC):
                    act.wait_ge(s_w[c % 2], 32 * (c // 2 + 1))
                    act.mul(wh[:, c, :], w[:, c % 2, :], WSCALE).then_inc(s_hi, 1)
                act.wait_ge(s_z, 1)
                act.mul(zT[:, :], psZ[:, :], 1 / WSCALE).then_inc(s_zT, 1)
                act.wait_ge(s_need, 1)
                act.activation(e[:, :, :], e[:, :, :], ACT.Exp).then_inc(s_act, 1)
                act.wait_ge(s_need, 2)
                act.activation(g[:, :, :], g[:, :, :], ACT.Sigmoid, scale=2.0).then_inc(s_act, 1)

            @block.gpsimd
            def _(pool):
                pool.wait_ge(s_mx, 1)
                pool.partition_all_reduce(mxa[:, :], mx[:, :], P, bass.bass_isa.ReduceOp.max).then_inc(s_all, 1)

            @block.tensor
            def _(pe):
                trio = ((xh, wh), (xl, wh), (xh, wl))
                pe.wait_ge(s_lo, KC)
                for c in range(KC):
                    for q, (x, ww) in enumerate(trio):
                        last = pe.matmul(psZ[:, :], ww[:, c, N:WA], x[:, c, :],
                                         start=(c == 0 and q == 0), stop=(c == KC - 1 and q == 2))
                last.then_inc(s_z, 1)
                for i, (b, h) in enumerate(tiles):
                    if i >= 4:
                        pe.wait_ge(s_H, i - 3)
                    for c in range(KC):
                        for q, (x, ww) in enumerate(trio):
                            last = pe.matmul(psH[i % 4][:, :], x[:, c, b * P:(b + 1) * P],
                                             ww[:, c, 512 * h:512 * h + 512],
                                             start=(c == 0 and q == 0), stop=(c == KC - 1 and q == 2))
                    last.then_inc(s_h, 1)
                    if i == 0:
                        pe.wait_ge(s_zT, 1)
                        pe.wait_ge(s_c, 16 * 5)
                        for t in range(TB):
                            last = pe.matmul(psD[:, t, :], zT[:, t * P:(t + 1) * P], limT[:, :], start=True, stop=True)
                        last.then_inc(s_d, 1)
                pe.wait_ge(s_g, 1)
                for t in range(TB):
                    last = pe.transpose(psG[:, t * P:(t + 1) * P], g[:, t, :], k.id32[:, :])
                last.then_inc(s_gT, 1)
                pe.wait_ge(s_gc, 1)
                pe.matmul(psZ[:, :], lim[:, :], gT[:, :], start=True, stop=True).then_inc(s_p, 1)
                pe.wait_ge(s_zp, 1)
                pe.wait_ge(s_H, len(tiles))
                for i, (b, h) in enumerate(tiles):
                    if i >= 4:
                        pe.wait_ge(s_y, i - 3)
                    pe.matmul(psH[i % 4][:, :], zp[:, b * P:(b + 1) * P], bm[:, 512 * h:512 * h + 512],
                              start=True, stop=True).then_inc(s_dl, 1)

            @block.vector
            def _(v):
                ch = Counted(v, s_chain)
                for c in range(KC):
                    v.wait_ge(s_hi, c + 1)
                    v.scalar_tensor_tensor(wl[:, c, :], w[:, c % 2, :], WSCALE, wh[:, c, :],
                                           ALU.mult, ALU.subtract).then_inc(s_lo, 1)
                v.wait_ge(s_c, 16 * 5)

                def hidden(i):
                    b, h = tiles[i]
                    v.wait_ge(s_h, i + 1)
                    v.scalar_tensor_tensor(H[:, b, 512 * h:512 * h + 512], psH[i % 4][:, :], 1 / WSCALE,
                                           bias[:, 512 * h:512 * h + 512], ALU.mult, ALU.add).then_inc(s_H, 1)

                for i in range(TB):
                    hidden(i)
                v.wait_ge(s_H, TB)
                v.wait_ge(s_d, 1)
                ch.inc(v.tensor_copy(lg[:, 0, :, :], H[:, :, 0:NE]))
                ch.then(v.tensor_copy(lg[:, 1, :, :], psD[:, :, :]))
                ch.then(v.tensor_reduce(one[:, 0:2], lg[:, :, :, :].rearrange("p h t e -> p h (t e)"), AX.X, ALU.max,
                                        apply_absolute_value=True))
                v.tensor_scalar(mx[:, :], one[:, 0:2], odd[:, :], None, ALU.mult).then_inc(s_mx, 1)
                v.wait_ge(s_all, 1)
                ch.then(v.tensor_scalar(one[:, 2:4], mxa[:, :], 1e-6, None, ALU.max))
                ch.then(v.reciprocal(one[:, 4:6], one[:, 2:4]))
                ch.then(v.tensor_scalar(e[:, :, :], lg[:, 0, :, :], one[:, 4:5], 0.5, ALU.mult, ALU.mult))
                ch.then(v.tensor_scalar(g[:, :, :], lg[:, 1, :, :], one[:, 5:6], 0.5, ALU.mult, ALU.mult))
                ch.then(v.tensor_tensor(e[:, :, :], e[:, :, :], g[:, :, :], ALU.add))
                ch.then(v.tensor_reduce(one[:, 6:10], e[:, :, :], AX.X, ALU.max))
                v.tensor_tensor(e[:, :, :], e[:, :, :], one[:, 6:10].unsqueeze(2).to_broadcast([P, TB, NE]),
                                ALU.subtract).then_inc(s_need, 1)
                v.wait_ge(s_act, 1)
                ch.then(v.tensor_reduce(one[:, 6:10], e[:, :, :], AX.X, ALU.add))
                ch.then(v.reciprocal(one[:, 10:14], one[:, 6:10]))
                ch.then(v.tensor_tensor(e[:, :, :], e[:, :, :], one[:, 10:14].unsqueeze(2).to_broadcast([P, TB, NE]),
                                        ALU.mult))
                for t in range(TB):
                    ch.inc(v.max(best[:, t, :], e[:, t, :]))
                v.wait_ge(s_chain, ch.n)
                v.tensor_tensor(g[:, :, :], e[:, :, :], best[:, :, 1:2].to_broadcast([P, TB, NE]),
                                ALU.subtract).then_inc(s_need, 1)
                v.wait_ge(s_act, 2)
                ch.then(v.tensor_tensor(g[:, :, :], e[:, :, :], g[:, :, :], ALU.mult))
                ch.then(v.tensor_reduce(one[:, 6:10], g[:, :, :], AX.X, ALU.add))
                ch.then(v.tensor_scalar(one[:, 6:10], one[:, 6:10], 1e-9, None, ALU.add))
                ch.then(v.reciprocal(one[:, 10:14], one[:, 6:10]))
                v.tensor_tensor(g[:, :, :], g[:, :, :], one[:, 10:14].unsqueeze(2).to_broadcast([P, TB, NE]),
                                ALU.mult).then_inc(s_g, 1)
                v.wait_ge(s_gT, 1)
                pairs = psG[:, :].rearrange("e (t o) -> e t o", o=2)[:, :, 1:2]
                v.tensor_copy(gT[:, :].rearrange("e (t o) -> e t o", o=2), pairs.to_broadcast([NE, TOK // 2, 2])
                              ).then_inc(s_gc, 1)
                v.wait_ge(s_p, 1)
                ch.then(v.tensor_tensor(zp[:, :], zT[:, :], psZ[:, :], ALU.mult))
                v.tensor_scalar(zp[:, :], zp[:, :], 0.5, None, ALU.mult).then_inc(s_zp, 1)
                for i in range(TB, 2 * TB):
                    hidden(i)
                v.wait_ge(s_H, 2 * TB)
                for b, h in tiles:
                    x = X[:, b, 512 * h:512 * h + 512]
                    ch.inc(v.tensor_tensor(x, x, H[:, b, 512 * h:512 * h + 512], ALU.add))
                v.wait_ge(s_chain, ch.n)
                for i, (b, h) in enumerate(tiles):
                    v.wait_ge(s_dl, i + 1)
                    x = X[:, b, 512 * h:512 * h + 512]
                    v.tensor_tensor(x, x, psH[i % 4][:, :], ALU.add).then_inc(s_y, 1)


def constants(k):
    with k.nc.semaphore("s_const") as s_const, k.nc.Block() as block:
        @block.sync
        def _(sp):
            pairs = ((k.id32, k.given["c_id32"]), (k.id16, k.given["c_id16"]), (k.ramp, k.given["c_ramp"]))
            for dst, src in pairs:
                sp.dma_start(dst[:, :], src).then_inc(s_const, 16)
            sp.wait_ge(s_const, 16 * len(pairs))


def copy_features(k):
    with k.nc.semaphore("s_cf") as s_cf, k.nc.Block() as block:
        @block.sync
        def _(sp):
            sp.dma_start(k.F[C:P, :, :], k.M2[0:C, :, :]).then_inc(s_cf, 16)
            sp.wait_ge(s_cf, 16)


def build(nc, given):
    k = Kernel(nc, given)
    with ExitStack() as ctx:
        sb, ps, sem = placing(k, ctx)
        k.id32 = sb("id32", [P, P])
        k.id16 = sb("id16", [P, P], F16)
        with ExitStack() as first:
            sb, ps, sem = placing(k, first)
            k.ramp = sb("ramp", [P, N], F16)
            k.F = sb("F", [P, B, N])
            k.M2 = sb("M2", [P, B, N])
            k.rank = sb("rank", [P, B * M, NB])
            mv = sb("mv", [P, B, 2])
            outputs = (C, 2 * C)
            wn = [sb(f"wn{i}", [P, 2, 2, O], F16) for i, O in enumerate(outputs)]
            wd = [sb(f"wd{i}", [C, 2, O]) for i, O in enumerate(outputs)]
            hb = [sb(f"hb{i}", [P, 1]) for i in range(2)]
            constants(k)
            combine_weights(k, [(given[f"lin{i + 1}"], given[f"win{i + 1}"], given[f"w_conv{i + 1}"],
                                 given[f"b_lin{i + 1}"], O, wn[i], wd[i], hb[i]) for i, O in enumerate(outputs)])
            curve_keys(k)
            curve_ranks(k)
            for i, (O, src) in enumerate(zip(outputs, (k.F, k.M2))):
                with ExitStack() as layer:
                    sb, ps, sem = placing(k, layer)
                    centre = sb("centre", [P, B * NB, 2, O], F16)
                    with ExitStack() as turned:
                        sb, ps, sem = placing(k, turned)
                        k.fT = sb("fT", [P, B, NB, P], F16)
                        split_features(k, src, centre, wd[i], O)
                        gather(k)
                    edge_layer(k, centre, wn[i], O, k.M2[0:O, :, :], mv)
                instance_norm(k, k.M2, mv, hb[i], O)
                if i == 0:
                    copy_features(k)
            points_out(k)
        nc.clear_and_free_semaphores(k.sems)
        nc.all_engine_barrier()
        with ExitStack() as second:
            sb, ps, sem = placing(k, second)
            xh = sb("xh", [P, KC, TOK], F16)
            xl = sb("xl", [P, KC, TOK], F16)
            with ExitStack() as rows:
                sb1, _, _ = placing(k, rows)
                token_norm(k, sb1("X", [P, TB, N]), xh, xl, True)
            k.pick = sb("pick", [96, 32, P], BF16)
            ctxh = sb("ctxh", [P, NH, TOK], F16)
            ctxl = sb("ctxl", [P, NH, TOK], F16)
            attention(k, xh, xl, ctxh, ctxl)
            X = sb("X", [P, TB, N])
            out_projection(k, X, ctxh, ctxl)
            token_norm(k, X, xh, xl, False)
            feed_forward(k, X, xh, xl)


def rope_tables():
    inv = 1.0 / np.float32(10000.0) ** (np.arange(0, HD, 2, dtype=np.float32) / np.float32(HD))
    angle = np.arange(C, dtype=np.float32)[:, None] * inv.astype(np.float32)
    cos, sin = np.cos(angle).T.astype(np.float32), np.sin(angle).T.astype(np.float32)
    scale = np.float32(1 / WSCALE)
    return np.concatenate([cos, cos]) * scale, np.concatenate([sin, -sin]) * scale


def kernel(**inputs):
    import concourse.bacc as bacc
    from concourse.bass_utils import run_bass_kernel_spmd

    a = {n: np.asarray(v) for n, v in inputs.items()}
    pick = np.zeros((96, 32, P), np.float32)
    for r in range(96):
        pick[r, r % 32] = WSCALE
    q, s = np.meshgrid(np.arange(P) % C, np.arange(C), indexing="ij")
    mkl, mkr = window_masks()
    cos, sin = rope_tables()
    arrays = {
        "x": a["x"], "coords": a["ctx_4096"][:, 0:3, :],
        "sq": a["L0_attn_scales_q"], "sk": a["L0_attn_scales_k"], "sv": a["L0_attn_scales_v"],
        "so": a["L0_attn_scales_o"], "qw_q": a["L0_attn_qw_q"], "qw_k": a["L0_attn_qw_k"],
        "qw_v": a["L0_attn_qw_v"], "qw_o": a["L0_attn_qw_o"],
        "ffn_WT": a["L0_ffn_W"].T, "ffn_b": a["L0_ffn_b"], "ffn_A": a["L0_ffn_A"], "ffn_Bmat": a["L0_ffn_Bmat"],
        "ffn_lim": a["L0_ffn_LiMEs"], "ffn_limT": a["L0_ffn_LiMEs"].T,
        "w_conv1": a["L0_xattn_W_conv1"].T, "w_conv2": a["L0_xattn_W_conv2"].T, "w_conv3": a["L0_xattn_W_conv3"].T,
        "b_lin1": a["L0_xattn_b_lin1"][:, None], "b_lin2": a["L0_xattn_b_lin2"][:, None],
        "c_id32": np.eye(P, dtype=np.float32), "c_id16": np.eye(P, dtype=np.float16),
        "c_idb": np.eye(P, dtype=np.float32).astype(NP_BF16),
        "c_ramp": np.tile(np.arange(N, dtype=np.float16), (P, 1)),
        "c_pick": pick.astype(NP_BF16), "c_mkl": mkl, "c_mkr": mkr, "c_cos": cos, "c_sin": sin,
        "c_causal": np.where(s > q, -2.0 ** 30, 0.0).astype(np.float32).astype(NP_BF16),
        "c_spread": np.ascontiguousarray(np.kron(np.eye(P, dtype=np.float16), np.ones((1, KNN), np.float16))
                                         .reshape(P, 2, STEP * KNN)),
        "c_odd": (np.arange(P, dtype=np.float32) % 2)[:, None],
    }
    for layer, perm in ((1, [2, 0, 3, 1]), (2, [1, 3, 0, 2])):
        plain, ordered = lin_layouts(a[f"L0_xattn_W_lin{layer}"], perm)
        arrays[f"lin{layer}"], arrays[f"win{layer}"] = plain, ordered
    nc = bacc.Bacc("TRN2", target_bir_lowering=False, num_devices=1)
    arrays = {f"in_{n}": np.ascontiguousarray(v) for n, v in arrays.items()}
    t = {n[3:]: nc.dram_tensor(n, v.shape, mybir.dt.from_np(v.dtype), kind="ExternalInput").ap()
         for n, v in arrays.items()}
    t["out"] = nc.dram_tensor("out", (TOK, N), F32, kind="ExternalOutput").ap()
    build(nc, t)
    got = run_bass_kernel_spmd(nc, [arrays], core_ids=[0])
    return got.results[0]["out"].reshape(B, C, N)
```

```python
from contextlib import ExitStack

import numpy as np
import concourse.bass as bass
from concourse import mybir

ALU = mybir.AluOpType
ACT = mybir.ActivationFunctionType
AX = mybir.AxisListType
F32, F16, BF16, I32 = mybir.dt.float32, mybir.dt.float16, mybir.dt.bfloat16, mybir.dt.int32
NP_BF16 = mybir.dt.np(BF16)

P = 128
B, C, N = 8, 64, 1024
M = 4
KNN = 10
NB = N // P
EPS = 1e-5
WSCALE = 256.0


class Kernel:

    def __init__(self, nc, given):
        self.nc, self.given = nc, given
        self.stage, self.sems = 0, []
        self.d_quant = nc.dram_tensor("d_quant", (3 * B, N), I32).ap()
        self.d_key = nc.dram_tensor("d_key", (2, B, M, N), F32).ap()
        self.d_f = nc.dram_tensor("d_f", (B, C, N), F32).ap()
        self.d_g = nc.dram_tensor("d_g", (B, 8, M, 16, N), F16).ap()
        self.d_x1 = nc.dram_tensor("d_x1", (B * C, N), F32).ap()


class Counted:

    def __init__(self, eng, sem, start=0):
        self.eng, self.sem, self.start, self.n = eng, sem, start, 0

    def inc(self, ins):
        self.n += 1
        ins.then_inc(self.sem, 1)

    def then(self, ins):
        self.inc(ins)
        self.eng.wait_ge(self.sem, self.start + self.n)


def placing(k, ctx):
    k.stage += 1
    nc, tag = k.nc, f"_{k.stage}"

    def sb(name, shape, dt=F32):
        return ctx.enter_context(nc.sbuf_tensor(name + tag, shape, dt))

    def ps(name, shape, dt=F32):
        return ctx.enter_context(nc.psum_tensor(name + tag, shape, dt))

    def sem(name):
        k.sems.append(nc.alloc_semaphore(name + tag))
        return k.sems[-1]

    return sb, ps, sem


def curve_keys(k):
    nc = k.nc
    with ExitStack() as ctx:
        sb, ps, sem = placing(k, ctx)
        NQ = 3 * B
        xs = sb("xs", [C, B, N], F32)
        xstat = sb("xstat", [C, B, 2, 6], F32)
        xmv = sb("xmv", [C, B, 2], F32)
        xstd = sb("xstd", [C, B], F32)
        xrstd = sb("xrstd", [C, B], F32)
        co = sb("co", [NQ, N], F32)
        cq = sb("cq", [NQ, N], F32)
        cfl = sb("cfl", [NQ, N], F32)
        cint = sb("cint", [NQ, N], I32)
        col = sb("col", [NQ, 16], F32)
        coli = col[:, :].bitcast(I32)
        X = sb("X", [P, 3, M, 64], I32)
        T = sb("T", [P, 3, M, 64], I32)
        mask = sb("mask", [P, 2, 64], I32)
        flip = sb("flip", [P, 2, 64], I32)
        point = sb("point", [P, 64], I32)
        key = sb("key", [P, 2, M, 64], I32)
        keyf = sb("keyf", [P, 2, M, 64], F32)
        epsc = sb("epsc", [P, 1], F32)

        s_x = sem("s_x")
        s_co = sem("s_co")
        s_chain = sem("s_chain")
        s_var = sem("s_var")
        s_std = sem("s_std")
        s_eps = sem("s_eps")
        s_cint = sem("s_cint")
        s_qout = sem("s_qout")
        s_qin = sem("s_qin")
        s_point = sem("s_point")
        s_keyf = sem("s_keyf")
        s_kout = sem("s_kout")
        s_rstd = sem("s_rstd")

        with nc.Block() as block:
            @block.sync
            def _(sp):
                sp.dma_start(co[:, :], k.given["coords"].rearrange("b a n -> (b a) n")).then_inc(s_co, 16)
                sp.dma_start(xs[:, :, :], k.given["x"].rearrange("b c n -> c b n")).then_inc(s_x, 16)
                sp.wait_ge(s_cint, 1)
                sp.dma_start(k.d_quant, cint[:, :]).then_inc(s_qout, 16)
                sp.wait_ge(s_qout, 16)
                for b in range(B):
                    for a in range(3):
                        sp.dma_start(X[16 * b:16 * b + 16, a, 0, :],
                                     k.d_quant[3 * b + a].rearrange("(g e) -> g e", e=64)).then_inc(s_qin, 16)
                sp.wait_ge(s_keyf, 1)
                for b in range(B):
                    for h in range(2):
                        sp.dma_start(k.d_key[h, b].rearrange("m (g e) -> g m e", e=64),
                                     keyf[16 * b:16 * b + 16, h, :, :]).then_inc(s_kout, 16)
                sp.wait_ge(s_kout, 16 * 2 * B)

            @block.gpsimd
            def _(pool):
                pool.iota(point[:, :], pattern=[[1, 64]], base=0, channel_multiplier=64).then_inc(s_point, 1)
                pool.memset(epsc[:, :], EPS).then_inc(s_eps, 1)
                pool.wait_ge(s_rstd, 1)
                for b in range(B):
                    pool.tensor_scalar(k.F[0:C, b, :], xs[:, b, :], xmv[:, b, 0:1], xrstd[:, b:b + 1],
                                       ALU.subtract, ALU.mult)

            @block.scalar
            def _(act):
                act.wait_ge(s_var, 1)
                act.wait_ge(s_eps, 1)
                act.activation(xstd[:, :], xmv[:, :, 1], ACT.Sqrt, bias=epsc[0:C, :]).then_inc(s_std, 1)

            @block.vector
            def _(v):
                ch = Counted(v, s_chain)

                def ts(out, a, s1, s2, o1, o2=ALU.bypass):
                    ch.then(v.tensor_scalar(out, a, s1, s2, o1, o2) if s2 is not None
                            else v.tensor_scalar(out, a, s1, None, o1))

                def tt(out, a, b_, op):
                    ch.then(v.tensor_tensor(out, a, b_, op))

                v.wait_ge(s_co, 16)
                ch.then(v.tensor_reduce(col[:, 0:1], co[:, :], AX.X, ALU.min))
                ch.then(v.tensor_reduce(col[:, 1:2], co[:, :], AX.X, ALU.max))
                tt(col[:, 2:3], col[:, 1:2], col[:, 0:1], ALU.subtract)
                ts(col[:, 3:4], col[:, 2:3], 1e-6, None, ALU.add)
                ch.then(v.reciprocal(col[:, 4:5], col[:, 3:4]))
                ts(col[:, 5:6], col[:, 4:5], 1023.0, None, ALU.mult)
                for src, hi, lo in ((3, 6, 7), (5, 8, 9)):
                    ts(coli[:, hi:hi + 1], coli[:, src:src + 1], -4096, None, ALU.bitwise_and)
                    tt(col[:, lo:lo + 1], col[:, src:src + 1], col[:, hi:hi + 1], ALU.subtract)
                tt(col[:, 10:11], col[:, 6:7], col[:, 8:9], ALU.mult)
                ts(col[:, 11:12], col[:, 10:11], -1.0, 1023.0, ALU.mult, ALU.add)
                for a, b_ in ((6, 9), (7, 8), (7, 9)):
                    tt(col[:, 10:11], col[:, a:a + 1], col[:, b_:b_ + 1], ALU.mult)
                    tt(col[:, 11:12], col[:, 11:12], col[:, 10:11], ALU.subtract)
                tt(col[:, 10:11], col[:, 11:12], col[:, 4:5], ALU.mult)
                tt(col[:, 12:13], col[:, 5:6], col[:, 10:11], ALU.add)
                ts(cq[:, :], co[:, :], col[:, 0:1], col[:, 12:13], ALU.subtract, ALU.mult)
                ch.then(v.tensor_copy(cint[:, :], cq[:, :]))
                ch.then(v.tensor_copy(cfl[:, :], cint[:, :]))
                tt(cq[:, :], cfl[:, :], cq[:, :], ALU.is_gt)
                tt(cfl[:, :], cfl[:, :], cq[:, :], ALU.subtract)
                ts(cfl[:, :], cfl[:, :], 0.0, 1023.0, ALU.max, ALU.min)
                ch.then(v.tensor_copy(cint[:, :], cfl[:, :]))
                v.tensor_copy(col[:, 13:14], col[:, 12:13]).then_inc(s_cint, 1)

                v.wait_ge(s_x, 16)
                for b in range(B):
                    for h in range(2):
                        ch.inc(v.bn_stats(xstat[:, b, h, :], xs[:, b, 512 * h:512 * h + 512]))
                v.wait_ge(s_chain, ch.n)
                for b in range(B):
                    ch.inc(v.bn_aggr(xmv[:, b, :], xstat[:, b, :, :]))
                v.wait_ge(s_chain, ch.n)
                v.tensor_copy(col[:, 14:15], col[:, 13:14]).then_inc(s_var, 1)

                v.wait_ge(s_std, 1)
                v.reciprocal(xrstd[:, :], xstd[:, :]).then_inc(s_rstd, 1)

                v.wait_ge(s_qin, 16 * 3 * B)
                for a, b_ in ((0, 1), (1, 0), (2, 2)):
                    ch.inc(v.tensor_copy(X[:, b_, 1, :], X[:, a, 0, :]))
                for a in range(3):
                    ch.inc(v.tensor_copy(X[:, a, 2, :], X[:, a, 0, :]))
                for a, b_ in ((0, 1), (1, 0), (2, 2)):
                    ch.inc(v.tensor_copy(X[:, b_, 3, :], X[:, a, 0, :]))
                v.wait_ge(s_chain, ch.n)

                H = [X[:, a, 2:4, :] for a in range(3)]
                t, u = mask[:, :, :], flip[:, :, :]
                for bit in range(9, 0, -1):
                    low = (1 << bit) - 1
                    ts(t, H[0], 31 - bit, 31, ALU.logical_shift_left, ALU.arith_shift_right)
                    ch.then(v.scalar_tensor_tensor(H[0], t, low, H[0], ALU.bitwise_and, ALU.bitwise_xor))
                    for a in (1, 2):
                        ts(t, H[a], 31 - bit, 31, ALU.logical_shift_left, ALU.arith_shift_right)
                        tt(u, H[0], H[a], ALU.bitwise_xor)
                        ch.then(v.scalar_tensor_tensor(H[0], t, low, H[0], ALU.bitwise_and, ALU.bitwise_xor))
                        ts(t, t, low, low, ALU.bitwise_and, ALU.bitwise_xor)
                        tt(u, u, t, ALU.bitwise_and)
                        tt(H[0], H[0], u, ALU.bitwise_xor)
                        tt(H[a], H[a], u, ALU.bitwise_xor)
                tt(H[1], H[1], H[0], ALU.bitwise_xor)
                tt(H[2], H[2], H[1], ALU.bitwise_xor)
                ts(u, H[2], 0, None, ALU.bitwise_and)
                for bit in range(9, 0, -1):
                    ts(t, H[2], 31 - bit, 31, ALU.logical_shift_left, ALU.arith_shift_right)
                    ch.then(v.scalar_tensor_tensor(u, t, (1 << bit) - 1, u, ALU.bitwise_and, ALU.bitwise_xor))
                for a in range(3):
                    ch.inc(v.tensor_tensor(H[a], H[a], u, ALU.bitwise_xor))
                v.wait_ge(s_chain, ch.n)

                Xf = X[:, :, :, :].rearrange("p a m e -> p (a m e)")
                Tf = T[:, :, :, :].rearrange("p a m e -> p (a m e)")
                for shift, keep in ((16, 0x030000FF), (8, 0x0300F00F), (4, 0x030C30C3), (2, 0x09249249)):
                    ch.then(v.scalar_tensor_tensor(Tf, Xf, shift, Xf, ALU.logical_shift_left, ALU.bitwise_or))
                    ts(Xf, Tf, keep, None, ALU.bitwise_and)
                S = [X[:, a, :, :] for a in range(3)]
                ch.then(v.scalar_tensor_tensor(T[:, 0, :, :], S[1], 1, S[2], ALU.logical_shift_left, ALU.bitwise_or))
                ch.then(v.scalar_tensor_tensor(T[:, 1, :, :], S[0], 2, T[:, 0, :, :],
                                               ALU.logical_shift_left, ALU.bitwise_or))
                K = T[:, 1, :, :]
                ts(key[:, 0, :, :], K, 6, None, ALU.logical_shift_right)
                ch.then(v.tensor_copy(keyf[:, 0, :, :], key[:, 0, :, :]))
                ts(key[:, 1, :, :], K, 63, 10, ALU.bitwise_and, ALU.logical_shift_left)
                v.wait_ge(s_point, 1)
                ts(point[:, :], point[:, :], N - 1, None, ALU.bitwise_and)
                for m in range(M):
                    ch.inc(v.tensor_tensor(key[:, 1, m, :], key[:, 1, m, :], point[:, :], ALU.bitwise_or))
                v.wait_ge(s_chain, ch.n)
                ch.inc(v.tensor_copy(keyf[:, 1, :, :], key[:, 1, :, :]))
                ts(keyf[:, 0, :, :], keyf[:, 0, :, :], 65536.0, None, ALU.mult)
                v.tensor_copy(col[:, 15:16], col[:, 14:15]).then_inc(s_keyf, 1)


def curve_ranks(k):
    nc = k.nc
    R = B * M
    RING = 4
    with ExitStack() as ctx:
        sb, ps, sem = placing(k, ctx)
        rows = sb("rows", [R, 2, N], F32)
        own = sb("own", [P, 2, R, NB], F32)
        wide = sb("wide", [P, RING, 2, N], F32)
        cmp = sb("cmp", [P, 4, N], F32)
        sign = sb("sign", [P, 2, NB, N], BF16)
        ones = sb("ones", [P, 1], BF16)
        total = sb("total", [P, R, NB], F32)
        psT = ps("psT", [P, 2, NB, R], F32)
        psL = ps("psL", [P, R, NB], F32)
        s_rows = sem("s_rows")
        s_t = sem("s_t")
        s_own = sem("s_own")
        s_wide = [sem(f"s_wide{i}") for i in range(RING)]
        s_cmp = sem("s_cmp")
        s_sign = sem("s_sign")
        s_ones = sem("s_ones")
        s_later = sem("s_later")
        s_tot = sem("s_tot")

        with nc.Block() as block:
            @block.sync
            def _(sp):
                keyw = k.d_key.rearrange("h b m n -> (b m) h n")
                sp.dma_start(rows[:, :, :], keyw).then_inc(s_rows, 16)

                def load(r, i):
                    at = keyw[bass.ds(r, 1), 0:1, 0:1]
                    sp.dma_start(wide[:, i, :, :], bass.AP(tensor=at.tensor, offset=at.offset,
                                                           ap=[[0, P], [R * N, 2], [1, N]])).then_inc(s_wide[i], 16)

                for i in range(RING):
                    load(i, i)
                with sp.Fori(0, R // RING - 1) as t:
                    for i in range(RING):
                        sp.wait_ge(s_cmp, (t * RING + i + 1) * NB)
                        load(t * RING + (RING + i), i)

            @block.gpsimd
            def _(pool):
                pool.memset(ones[:, :], 1.0).then_inc(s_ones, 1)

            @block.tensor
            def _(pe):
                pe.wait_ge(s_rows, 16)
                for h in range(2):
                    for n in range(NB):
                        last = pe.transpose(psT[:, h, n, :], rows[:, h, n * P:(n + 1) * P], k.id32[0:R, 0:R])
                last.then_inc(s_t, 1)
                pe.wait_ge(s_ones, 1)
                pe.sem_inc(s_later, 2)
                later = psL[:, :, :].rearrange("p r n -> p (r n)")
                with pe.Fori(0, R // 2) as t:
                    for u in range(2):
                        r = 2 * t + u
                        pe.wait_ge(s_sign, (r + 1) * NB)
                        for q in range(1, NB):
                            for n in range(q):
                                last = pe.matmul(later[:, bass.ds(r * NB + q, 1)], sign[:, u, n, q * P:(q + 1) * P],
                                                 ones[:, :], start=(n == 0), stop=(n == q - 1))
                        last.then_inc(s_later, 1)

            @block.vector
            def _(v):
                v.wait_ge(s_t, 1)
                v.tensor_copy(own[:, 0, :, :], psT[:, 0, :, :].rearrange("p n r -> p r n")).then_inc(s_own, 1)
                v.tensor_scalar(own[:, 1, :, :], psT[:, 1, :, :].rearrange("p n r -> p r n"), -1.0, None,
                                ALU.mult).then_inc(s_own, 1)
                v.wait_ge(s_own, 2)
                own0 = own[:, 0, :, :].rearrange("p r n -> p (r n)")

                def compare(r, i, n, wait):
                    if wait is not None:
                        v.wait_ge(s_sign, wait)
                    v.scalar_tensor_tensor(cmp[:, n % 4, n * P:N], wide[:, i, 0, n * P:N],
                                           own0[:, bass.ds(r * NB + n, 1)], wide[:, i, 1, n * P:N],
                                           ALU.subtract, ALU.add).then_inc(s_cmp, 1)

                for i in range(RING):
                    v.wait_ge(s_wide[i], 16)
                    for n in range(NB):
                        at = i * NB + n
                        compare(i, i, n, at - 3 if at >= 4 else None)
                with v.Fori(1, R // RING) as t:
                    for i in range(RING):
                        v.wait_ge(s_wide[i], 16 * t + 16)
                        for n in range(NB):
                            compare(t * RING + i, i, n, t * (RING * NB) + (i * NB + n - 3))
                v.wait_ge(s_sign, R * NB)
                v.wait_ge(s_later, R + 2)
                v.tensor_tensor(total[:, :, 1:NB], total[:, :, 1:NB], psL[:, :, 1:NB], ALU.subtract
                                ).then_inc(s_tot, 1)
                v.wait_ge(s_tot, 1)
                v.tensor_scalar(k.rank[:, :, :], total[:, :, :], -0.5, (N - 1) / 2, ALU.mult, ALU.add)

            @block.scalar
            def _(act):
                act.wait_ge(s_own, 2)
                own1 = own[:, 1, :, :].rearrange("p r n -> p (r n)")
                tot = total[:, :, :].rearrange("p r n -> p (r n)")
                with act.Fori(0, R // 2) as t:
                    for u in range(2):
                        r = 2 * t + u
                        act.wait_ge(s_later, r + 1)
                        for n in range(NB):
                            act.wait_ge(s_cmp, r * NB + (n + 1))
                            act.activation(sign[:, u, n, n * P:N], cmp[:, n % 4, n * P:N], ACT.Sign,
                                           bias=own1[:, bass.ds(r * NB + n, 1)],
                                           accum_out=tot[:, bass.ds(r * NB + n, 1)]).then_inc(s_sign, 1)


def split_features(k, src, centre, wd, O):
    nc = k.nc
    with ExitStack() as ctx:
        sb, ps, sem = placing(k, ctx)
        hi = sb("hi", [C, B, N], F16)
        lo = sb("lo", [C, B, N], F16)
        both = sb("both", [C, 2, N], F32)
        psF = [ps(f"psF{i}", [P, NB, P], F16) for i in range(2)]
        psC = [ps(f"psC{i}", [P, NB * O]) for i in range(2)]
        s_hi = sem("s_hi")
        s_lo = sem("s_lo")
        s_both = sem("s_both")
        s_dump = [sem("s_dump0"), sem("s_dump1")]
        s_turn = sem("s_turn")
        s_fT = sem("s_fT")
        s_c = sem("s_c")
        s_chi = sem("s_chi")
        s_clo = sem("s_clo")

        def part(b, h):
            return centre[:, b * NB:(b + 1) * NB, h, :]

        def sums(b):
            return psC[b % 2][:, :].rearrange("p (n o) -> p n o", o=O)

        with nc.Block() as block:
            @block.scalar
            def _(act):
                def high(b):
                    act.wait_ge(s_c, b + 1)
                    act.mul(part(b, 0), sums(b), 1 / WSCALE).then_inc(s_chi, 1)

                for b in range(B):
                    act.copy(hi[:, b, :], src[0:C, b, :]).then_inc(s_hi, 1)
                    if b >= 2:
                        high(b - 2)
                for b in range(B - 2, B):
                    high(b)

            @block.vector
            def _(v):
                def turned(b):
                    v.wait_ge(s_turn, b + 1)
                    v.tensor_copy(k.fT[:, b, :, :], psF[b % 2][:, :, :]).then_inc(s_fT, 1)

                def rest(b):
                    v.wait_ge(s_chi, b + 1)
                    v.scalar_tensor_tensor(part(b, 1), sums(b), 1 / WSCALE, part(b, 0), ALU.mult, ALU.subtract
                                           ).then_inc(s_clo, 1)

                for b in range(B):
                    v.wait_ge(s_hi, b + 1)
                    v.tensor_tensor(lo[:, b, :], src[0:C, b, :], hi[:, b, :], ALU.subtract).then_inc(s_lo, 1)
                    if b >= 1:
                        turned(b - 1)
                    if b >= 2:
                        rest(b - 2)
                turned(B - 1)
                for b in range(B - 2, B):
                    rest(b)

            @block.gpsimd
            def _(pool):
                for b in range(B):
                    pool.wait_ge(s_lo, b + 1)
                    if b >= 2:
                        pool.wait_ge(s_dump[b % 2], 16 * (b // 2))
                    pool.tensor_tensor(both[:, b % 2, :], hi[:, b, :], lo[:, b, :], ALU.add).then_inc(s_both, 1)

            @block.sync
            def _(sp):
                for b in range(B):
                    sp.wait_ge(s_both, b + 1)
                    sp.dma_start(k.d_f[b], both[:, b % 2, :]).then_inc(s_dump[b % 2], 16)
                for u in range(2):
                    sp.wait_ge(s_dump[u], 16 * (B // 2))

            @block.tensor
            def _(pe):
                for b in range(B):
                    pe.wait_ge(s_lo, b + 1)
                    if b >= 2:
                        pe.wait_ge(s_fT, b - 1)
                    for n in range(NB):
                        for h, x in enumerate((hi, lo)):
                            last = pe.transpose(psF[b % 2][:, n, C * h:C * h + C], x[:, b, n * P:(n + 1) * P],
                                                k.id16[0:C, 0:C])
                    last.then_inc(s_turn, 1)
                    if b >= 2:
                        pe.wait_ge(s_clo, b - 1)
                    for n in range(NB):
                        for q, x in enumerate((hi, hi, lo)):
                            last = pe.matmul(psC[b % 2][:, n * O:(n + 1) * O], x[:, b, n * P:(n + 1) * P],
                                             wd[:, q, :], start=(q == 0), stop=(q == 2))
                    last.then_inc(s_c, 1)


def gather(k):
    nc = k.nc
    with ExitStack() as ctx:
        sb, ps, sem = placing(k, ctx)
        hot = sb("hot", [P, 8, N], F16)
        out = sb("out", [P, M, N], F16)
        psG = [ps(f"psGa{i}", [P, N], F32) for i in range(2)]
        s_hot = sem("s_hot")
        s_sent = [sem(f"s_sent{m}") for m in range(M)]
        s_freehot = sem("s_freehot")
        s_freeps = sem("s_freeps")
        rank = k.rank[:, :, :].rearrange("p r n -> p (r n)")

        with nc.Block() as block:
            @block.vector
            def _(v):
                with v.Fori(0, B) as b:
                    for j in range(M * NB):
                        v.wait_ge(s_freehot, b * (M * NB) + (j + 1))
                        v.tensor_scalar(hot[:, j % 8, :], k.ramp[:, :], rank[:, bass.ds(b * (M * NB) + j, 1)], None,
                                        ALU.is_equal).then_inc(s_hot, 1)

            @block.tensor
            def _(pe):
                pe.sem_inc(s_freehot, 8)
                fT = k.fT[:, :, :, :].rearrange("p b n c -> p (b n c)")
                with pe.Fori(0, B) as b:
                    for m in range(M):
                        pe.wait_ge(s_freeps, b * M + (m + 1))
                        for n in range(NB):
                            pe.wait_ge(s_hot, b * (M * NB) + (m * NB + n + 1))
                            for h in range(2):
                                last = pe.matmul(psG[m % 2][:, 512 * h:512 * h + 512],
                                                 fT[:, bass.ds(b * (NB * P) + n * P, P)],
                                                 hot[:, (m * NB + n) % 8, 512 * h:512 * h + 512],
                                                 start=(n == 0), stop=(n == NB - 1))
                            last.then_inc(s_freehot, 1)

            @block.scalar
            def _(act):
                act.sem_inc(s_freeps, 2)
                with act.Fori(0, B) as b:
                    for m in range(M):
                        act.wait_ge(s_freehot, b * (M * NB) + ((m + 1) * NB + 8))
                        act.wait_ge(s_sent[m], b * 16 + 16)
                        act.copy(out[:, m, :], psG[m % 2][:, :]).then_inc(s_freeps, 1)
                        act.wait_ge(s_freeps, b * M + (m + 3))
                        act.dma_start(k.d_g[bass.ds(b, 1), :, m, :, :].rearrange("o q c n -> (o q) c n"),
                                      out[:, m, :]).then_inc(s_sent[m], 16)
                for m in range(M):
                    act.wait_ge(s_sent[m], 16 * B + 16)

            @block.sync
            def _(sp):
                for m in range(M):
                    sp.sem_inc(s_sent[m], 16)


def combine_weights(k, layers):
    nc = k.nc
    with ExitStack() as ctx:
        sb, ps, sem = placing(k, ctx)
        s_w, s_comb, s_hi, s_both = sem("s_w"), sem("s_comb"), sem("s_hi"), sem("s_both")
        lin, win, conv, bias, near, both, psN, psD = [], [], [], [], [], [], [], []
        for i, (_, _, _, _, O, _, _, _) in enumerate(layers):
            lin.append(sb(f"lin{i}", [P, 2 * C * M]))
            win.append(sb(f"win{i}", [P, 2, P]))
            conv.append(sb(f"conv{i}", [P, O]))
            bias.append(sb(f"bias{i}", [P, 1]))
            psN.append(ps(f"psN{i}", [P, 2, O]))
            psD.append(ps(f"psD{i}", [P, 2 * O + 1]))
            near.append(sb(f"near{i}", [C, O]))
            both.append(sb(f"both{i}", [C, O]))

        with nc.Block() as block:
            @block.sync
            def _(sp):
                for i, (w_lin, w_win, w_conv, b_lin, _, _, _, _) in enumerate(layers):
                    sp.dma_start(lin[i][:, :], w_lin).then_inc(s_w, 16)
                    sp.dma_start(win[i][:, :, :], w_win.rearrange("c (k r) -> c k r", k=2)).then_inc(s_w, 16)
                    sp.dma_start(conv[i][:, :], w_conv).then_inc(s_w, 16)
                    sp.dma_start(bias[i][:, :], b_lin).then_inc(s_w, 16)

            @block.tensor
            def _(pe):
                pe.wait_ge(s_w, 16 * 4 * len(layers))
                for i, (_, _, _, _, O, _, _, _) in enumerate(layers):
                    for c in range(2):
                        pe.matmul(psN[i][:, c, :], win[i][:, c, :], conv[i][:, :], start=True, stop=True)
                    by_curve = lin[i][:, :].rearrange("c (h r m) -> c h m r", h=2, m=M)
                    for h in range(2):
                        for m in range(M):
                            pe.matmul(psD[i][0:C, h * O:(h + 1) * O], by_curve[:, h, m, :], conv[i][:, :],
                                      start=(m == 0), stop=(m == M - 1))
                    pe.matmul(psD[i][0:O, 2 * O:2 * O + 1], conv[i][:, :], bias[i][:, :], start=True, stop=True
                              ).then_inc(s_comb, 1)

            @block.scalar
            def _(act):
                for i, (_, _, _, _, O, wn, wd, hb) in enumerate(layers):
                    act.wait_ge(s_comb, i + 1)
                    act.mul(wn[:, 0, :, :], psN[i][:, :, :], WSCALE).then_inc(s_hi, 1)
                    act.copy(hb[0:O, :], psD[i][0:O, 2 * O:2 * O + 1])
                    act.mul(near[i][:, :], psD[i][0:C, O:2 * O], -WSCALE).then_inc(s_hi, 1)
                    act.wait_ge(s_hi, 3 * i + 2)
                    act.copy(wd[:, 2, :], near[i][:, :])
                    act.wait_ge(s_both, i + 1)
                    act.copy(wd[:, 0, :], both[i][:, :]).then_inc(s_hi, 1)

            @block.vector
            def _(v):
                for i, (_, _, _, _, O, wn, wd, hb) in enumerate(layers):
                    v.wait_ge(s_hi, 3 * i + 2)
                    v.scalar_tensor_tensor(both[i][:, :], psD[i][0:C, 0:O], WSCALE, near[i][:, :], ALU.mult, ALU.add
                                           ).then_inc(s_both, 1)
                    v.scalar_tensor_tensor(wn[:, 1, :, :], psN[i][:, :, :], WSCALE, wn[:, 0, :, :],
                                           ALU.mult, ALU.subtract)
                    v.wait_ge(s_hi, 3 * i + 3)
                    v.wait_ge(s_both, i + 1)
                    v.tensor_tensor(wd[:, 1, :], both[i][:, :], wd[:, 0, :], ALU.subtract)


G = 6
GP = 11
ROWS = GP * KNN
STEP = 64
WIN = 20
AW = 2 * (P + 2 * GP)
SPAN = STEP + 12
PAD = 5
GW = N + 16
STEPS = B * N // STEP
PER = N // STEP


def edge_layer(k, centre, wn, O, maxh, mv):
    nc = k.nc
    with ExitStack() as ctx:
        sb, ps, sem = placing(k, ctx)
        Gs = sb("Gs", [P, 2, 2, 2, GW], F16)
        none = sb("none", [P, 4], F32)
        fr = sb("fr", [P, 2, 2, N + 2], F32)
        sth = sb("sth", [P, 2, 2, 2, SPAN, 2], F16)
        stu = sb("stu", [P, 2, 2, SPAN], F32)
        d16 = sb("d16", [P, 2, 2, G * GP, KNN], F16)
        spread = sb("spread", [P, 2, STEP * KNN], F16)
        mkl = sb("mkl", [3 * GP, ROWS], BF16)
        mkr = sb("mkr", [3 * GP, 9, G * 4 * WIN], BF16)
        E = sb("E", [ROWS, 2, G * 2, WIN, 2], F32)
        top = sb("top", [ROWS, 2, G * 4], F32)
        tot = sb("tot", [ROWS, 2, G * 4], F32)
        inv = sb("inv", [ROWS, 2, G * 4], F32)
        A = sb("A", [ROWS, 2, 3, AW], F32)
        AT = sb("AT", [P, 2, G * ROWS], F32)
        GWs = sb("GWs", [P, 2, 3, O], F32)
        stat = sb("stat", [O, STEPS, 2, 6], F32)
        psS = [ps(f"psS{i}", [P, 512]) for i in range(2)]
        psW = ps("psW", [P, 512])
        psA = ps("psA", [P, 2, 512])
        psY = ps("psY", [P, 2, 512])

        s_w = sem("s_w")
        s_load = [sem("s_load0"), sem("s_load1")]
        s_zero = sem("s_zero")
        s_pool = sem("s_pool")
        s_S = sem("s_S")
        s_sth = sem("s_sth")
        s_dve = sem("s_dve")
        s_sub = sem("s_sub")
        s_exp = sem("s_exp")
        s_A = sem("s_A")
        s_T = sem("s_T")
        s_AT = sem("s_AT")
        s_W = sem("s_W")
        s_GW = sem("s_GW")
        s_Y = sem("s_Y")
        s_done = sem("s_done")
        NLOAD = 4 + 4

        PADS, EDGE, EACH = 1, 5, 3
        BATCH = PADS + EDGE + EACH * PER

        def staged(n):
            return n // PER * BATCH + n % PER * EACH + (PADS + EDGE + EACH)

        with nc.Block() as block:
            @block.sync
            def _(sp):
                sp.dma_start(spread[:, :, :], k.given["c_spread"]).then_inc(s_w, 16)
                sp.dma_start(mkl[:, :], k.given["c_mkl"]).then_inc(s_w, 16)
                sp.dma_start(mkr[:, :, :], k.given["c_mkr"]).then_inc(s_w, 16)
                def load(b, u):
                    for hl in range(2):
                        for c in range(2):
                            at = 4 * hl + 2 * c
                            sp.dma_start(Gs[:, u, hl, c, PAD:PAD + N],
                                         k.d_g[bass.ds(b, 1), at:at + 2].rearrange("o h m c n -> (o h m c) n")
                                         ).then_inc(s_load[u], 16)
                    flat = k.d_f.rearrange("b c n -> (b c) n")
                    for c in range(2):
                        for h in range(2):
                            at = flat[bass.ds(b * C + (32 * c + 16 * h), 16), :]
                            sp.dma_start(fr[64 * h:64 * h + 64, u, c, 0:N],
                                         bass.AP(tensor=at.tensor, offset=at.offset, ap=[[0, M], [N, 16], [1, N]])
                                         ).then_inc(s_load[u], 16)

                sp.wait_ge(s_zero, 4)
                for u in range(2):
                    load(u, u)
                with sp.Fori(1, B // 2) as t:
                    for u in range(2):
                        sp.wait_ge(s_sth, t * (4 * PER) + (u - 1) * (2 * PER))
                        sp.wait_ge(s_pool, t * (2 * BATCH) + (u - 1) * BATCH)
                        load(2 * t + u, u)

            @block.gpsimd
            def _(pool):
                pool.memset(Gs[:, :, :, :, 0:PAD], 0.0).then_inc(s_zero, 1)
                pool.memset(sth[:, :, :, :, :, :], 0.0).then_inc(s_zero, 1)
                pool.memset(none[:, :], 0.0).then_inc(s_zero, 1)
                pool.memset(fr[:, :, :, N:N + 2], 0.0).then_inc(s_zero, 1)
                pool.wait_ge(s_zero, 4)

                def stage(b, par, s, u, first):
                    n = b * PER + s
                    ch = Counted(pool, s_pool, b * BATCH + s * EACH + (PADS if first else PADS + EDGE))
                    w = s * STEP
                    at = bass.ds(w, SPAN)
                    ch.then(pool.tensor_tensor(stu[:, u, :, :], Gs[:, par, 0, :, at], Gs[:, par, 1, :, at], ALU.add))
                    pool.wait_ge(s_S, n + 1)
                    for c in range(2):
                        g = stu[:, u, c, :]
                        win = bass.AP(tensor=g.tensor, offset=g.offset, ap=[list(g.ap[0]), [1, G * GP], [1, KNN]])
                        ch.inc(pool.tensor_tensor(
                            d16[:, u, c, :, :], win,
                            fr[:, par, c, bass.ds(w, G * GP)].unsqueeze(2).to_broadcast([P, G * GP, KNN]),
                            ALU.subtract))
                    if first:
                        pool.wait_ge(s_pool, ch.start + ch.n)
                        for i in range(EDGE):
                            ch.inc(pool.tensor_tensor(
                                d16[:, u, :, i, 0:PAD - i],
                                stu[:, u, :, i + 2 * PAD:i + 2 * PAD + 1].to_broadcast([P, 2, PAD - i]),
                                fr[:, par, :, i:i + 1].to_broadcast([P, 2, PAD - i]), ALU.subtract))

                with pool.Fori(0, B // 2) as t:
                    for par in range(2):
                        b = 2 * t + par
                        pool.wait_ge(s_load[par], t * (16 * NLOAD) + 16 * NLOAD)
                        edge = Gs[:, par, :, :, :].rearrange("p q c n -> p (q c) n")
                        pool.tensor_tensor(edge[:, :, PAD + N:GW],
                                           edge[:, :, PAD + N - 1:PAD + N].to_broadcast([P, 4, GW - PAD - N]),
                                           none[:, :].unsqueeze(2).to_broadcast([P, 4, GW - PAD - N]),
                                           ALU.add).then_inc(s_pool, 1)
                        pool.wait_ge(s_pool, b * BATCH + PADS)
                        stage(b, par, 0, 0, True)
                        stage(b, par, 1, 1, False)
                        with pool.Fori(1, PER // 2) as q:
                            for u in range(2):
                                stage(b, par, 2 * q + u, u, False)

            @block.tensor
            def _(pe):
                pe.wait_ge(s_w, 16 * 3)
                pe.sem_inc(s_W, 2)
                pe.sem_inc(s_Y, 2)
                pe.sem_inc(s_S, 2)

                mk = mkr[:, :, :].rearrange("k v n -> k (v n)")
                cf = centre[:, :, :, :].rearrange("p b h o -> p (b h o)")
                NS = G * 4 * WIN

                def scores(n, u, first):
                    pe.wait_ge(s_pool, staged(n))
                    pe.wait_ge(s_sth, 2 * (n + 1))
                    if not first:
                        pe.wait_ge(s_sub, n - 1)
                    at = (n // 2) % (PER // 2) * NS + u * NS
                    pe.matmul(psS[u][0:ROWS, 0:NS], mkl[:, :], mk[:, bass.ds(at, NS)], start=True, stop=False)
                    for g in range(G):
                        for c in range(2):
                            for hl in range(2):
                                last = pe.matmul(psS[u][0:ROWS, 80 * g + 40 * c:80 * g + 40 * c + 40],
                                                 d16[:, u, c, GP * g:GP * g + GP, :],
                                                 sth[:, u, hl, c, GP * g:GP * g + WIN, :],
                                                 start=False, stop=(g == G - 1 and c == 1 and hl == 1))
                    last.then_inc(s_S, 1)

                def turn(n, u, first):
                    pe.wait_ge(s_A, n + 1)
                    if not first:
                        pe.wait_ge(s_AT, n)
                    for g in range(G):
                        last = pe.transpose(psA[:, g // 3, ROWS * (g % 3):ROWS * (g % 3) + ROWS],
                                            A[:, u, g // 2, P * (g % 2):P * (g % 2) + P], k.id32[0:ROWS, 0:ROWS])
                    last.then_inc(s_T, 1)

                def windows(n, u, first):
                    if not first:
                        pe.wait_ge(s_GW, n)
                    for w in range(3):
                        for c in range(2):
                            for q, (x, y) in enumerate(((0, 0), (0, 1), (1, 0))):
                                last = pe.matmul(psW[64 * c:64 * c + 64, O * w:O * w + O],
                                                 sth[:, u, x, c, 2 * GP * w:2 * GP * w + 32, :],
                                                 wn[:, y, c, :], start=(q == 0), stop=(q == 2))
                    last.then_inc(s_W, 1)

                def sums(n, u, first):
                    pe.wait_ge(s_AT, n + 1)
                    pe.wait_ge(s_GW, n + 1)
                    if not first:
                        pe.wait_ge(s_done, 4 * n)
                    for j, (p0, pn) in enumerate(((0, 4 * GP), (4 * GP, STEP - 4 * GP))):
                        for hl in range(2):
                            pe.matmul(psY[0:O, j, 0:pn * KNN], cf[:, bass.ds(n // 2 * (2 * O) + hl * O, O)],
                                      spread[:, u, p0 * KNN:(p0 + pn) * KNN], start=(hl == 0), stop=False)
                    for w in range(3):
                        cols = (2 * GP if w < 2 else STEP - 4 * GP) * KNN
                        at = 2 * ROWS * w if w < 2 else 0
                        last = pe.matmul(psY[0:O, w // 2, at:at + cols], GWs[:, u, w, :],
                                         AT[:, u, 2 * ROWS * w:2 * ROWS * w + cols], start=False, stop=(w > 0))
                    last.then_inc(s_Y, 1)

                scores(0, 0, True)
                windows(0, 0, True)
                scores(1, 1, True)
                turn(0, 0, True)
                windows(1, 1, False)
                scores(2, 0, False)
                sums(0, 0, True)
                with pe.Fori(1, STEPS // 2 - 1) as t:
                    for u in range(2):
                        n = 2 * t + u
                        turn(n - 1, 1 - u, False)
                        windows(n, u, False)
                        scores(n + 1, 1 - u, False)
                        sums(n - 1, 1 - u, False)
                turn(STEPS - 3, 1, False)
                windows(STEPS - 2, 0, False)
                scores(STEPS - 1, 1, False)
                sums(STEPS - 3, 1, False)
                turn(STEPS - 2, 0, False)
                windows(STEPS - 1, 1, False)
                sums(STEPS - 2, 0, False)
                turn(STEPS - 1, 1, False)
                sums(STEPS - 1, 1, False)

            @block.scalar
            def _(act):
                Gf = Gs[:, :, :, :, :].rearrange("p b q c n -> p (b q c) n")
                act.wait_ge(s_zero, 4)

                def windows(n, u):
                    act.wait_ge(s_W, n + 1)
                    act.wait_ge(s_pool, n // PER * BATCH + PADS)
                    for h in range(2):
                        r = slice(64 * h, 64 * h + 64)
                        act.copy(sth[r, u, :, :, :, h].rearrange("p q c n -> p (q c) n"),
                                 Gf[r, bass.ds(n // PER % 2 * 4, 4), bass.ds(n % PER * STEP, SPAN)]
                                 ).then_inc(s_sth, 1)

                def turned(n, u):
                    act.wait_ge(s_T, n + 1)
                    act.wait_ge(s_Y, n + 1)
                    act.copy(AT[:, u, :].rearrange("p (j n) -> p j n", j=2), psA[:, :, 0:3 * ROWS]).then_inc(s_AT, 1)

                def exps(n, u):
                    act.wait_ge(s_sub, n + 1)
                    act.activation(E[:, u, :, :], E[:, u, :, :], ACT.Exp, scale=0.125).then_inc(s_exp, 1)

                def evacuate(n, u):
                    act.wait_ge(s_W, n + 3)
                    act.wait_ge(s_Y, n + 1)
                    act.mul(GWs[:, u, :, :], psW[:, 0:3 * O].rearrange("p (w o) -> p w o", w=3), 1 / WSCALE
                            ).then_inc(s_GW, 1)

                windows(0, 0)
                windows(1, 1)
                exps(0, 0)
                evacuate(0, 0)
                windows(2, 0)
                turned(0, 0)
                exps(1, 1)
                evacuate(1, 1)
                windows(3, 1)
                with act.Fori(1, STEPS // 2 - 1) as t:
                    for u in range(2):
                        n = 2 * t + u
                        turned(n - 1, 1 - u)
                        exps(n, u)
                        evacuate(n, u)
                        windows(n + 2, u)
                for n in (STEPS - 2, STEPS - 1):
                    turned(n - 1, (n - 1) % 2)
                    exps(n, n % 2)
                    evacuate(n, n % 2)
                turned(STEPS - 1, 1)

            @block.vector
            def _(v):
                v.memset(A[:, :, :, :], 0.0).then_inc(s_dve, 1)
                v.wait_ge(s_dve, 1)
                EV = 3
                mh = maxh.rearrange("o b n -> o (b n)")

                def soften(n, u):
                    v.wait_ge(s_S, n + 3)
                    S = psS[u][0:ROWS, 0:G * 4 * WIN].rearrange("p (g n h) -> p g h n", n=WIN, h=2)
                    e = E[:, u, :, :, :].rearrange("p g n h -> p g h n")
                    m = top[:, u, :].rearrange("p (g h) -> p g h", h=2)
                    v.tensor_reduce(m, S, AX.X, ALU.max).then_inc(s_dve, 1)
                    v.wait_ge(s_dve, n * EV + 2)
                    v.tensor_tensor(e, S, m.unsqueeze(3).to_broadcast([ROWS, G * 2, 2, WIN]),
                                    ALU.subtract).then_inc(s_sub, 1)

                def collect(n):
                    v.wait_ge(s_Y, n + 3)
                    for j, (p0, pn) in enumerate(((0, 4 * GP), (4 * GP, STEP - 4 * GP))):
                        v.bn_stats(stat[:, :, j, :].rearrange("o n e -> o n e")[:, bass.ds(n, 1), :],
                                   psY[0:O, j, 0:pn * KNN]).then_inc(s_done, 1)
                        v.tensor_reduce(mh[:, bass.ds(n * STEP + p0, pn)],
                                        psY[0:O, j, 0:pn * KNN].rearrange("o (i a) -> o i a", a=KNN),
                                        AX.X, ALU.max).then_inc(s_done, 1)

                def weights(n, u, first):
                    v.wait_ge(s_exp, n + 1)
                    v.tensor_reduce(tot[:, u, :].rearrange("p (g h) -> p g h", h=2),
                                    E[:, u, :, :, :].rearrange("p g n h -> p g h n"), AX.X, ALU.add).then_inc(s_dve, 1)
                    v.wait_ge(s_dve, n * EV + 3)
                    v.reciprocal(inv[:, u, :], tot[:, u, :]).then_inc(s_dve, 1)
                    v.wait_ge(s_dve, n * EV + 4)
                    if not first:
                        v.wait_ge(s_T, n - 1)
                    a = A[:, u, :, :]
                    out = bass.AP(tensor=a.tensor, offset=a.offset,
                                  ap=[list(a.ap[0]), [AW // 2, G], [P // 2, 2], [1, 2 * WIN]])
                    r = inv[:, u, :]
                    r = bass.AP(tensor=r.tensor, offset=r.offset,
                                ap=[list(r.ap[0]), [2, G * 2], [0, WIN], [1, 2]])
                    v.tensor_tensor(out, E[:, u, :, :, :].rearrange("p g n h -> p (g n h)"), r,
                                    ALU.mult).then_inc(s_A, 1)

                soften(0, 0)
                weights(0, 0, True)
                soften(1, 1)
                weights(1, 1, True)
                with v.Fori(1, STEPS // 2) as t:
                    for u in range(2):
                        n = 2 * t + u
                        soften(n, u)
                        collect(n - 2)
                        weights(n, u, False)
                collect(STEPS - 2)
                collect(STEPS - 1)
                v.wait_ge(s_done, 4 * STEPS)
                for b in range(B):
                    v.bn_aggr(mv[0:O, b, :], stat[:, PER * b:PER * b + PER, :, :].rearrange("o n j e -> o (n j e)"))


def instance_norm(k, x, mv, hb, O):
    nc = k.nc
    with ExitStack() as ctx:
        sb, ps, sem = placing(k, ctx)
        var = sb("var", [P, B])
        std = sb("std", [P, B])
        r = sb("r", [P, B])
        r2 = sb("r2", [P, B])
        shift = sb("shift", [P, B])
        s_var = sem("s_var")
        s_std = sem("s_std")
        s_chain = sem("s_chain")
        with nc.Block() as block:
            @block.scalar
            def _(act):
                act.wait_ge(s_var, 1)
                act.activation(std[0:O, :], var[0:O, :], ACT.Sqrt).then_inc(s_std, 1)

            @block.vector
            def _(v):
                ch = Counted(v, s_chain)
                v.tensor_scalar(var[0:O, :], mv[0:O, :, 1], EPS, None, ALU.add).then_inc(s_var, 1)
                mean = mv[0:O, :, 0]
                if hb is not None:
                    ch.then(v.tensor_scalar(shift[0:O, :], mean, hb[0:O, :], hb[0:O, :], ALU.add, ALU.subtract))
                    mean = shift[0:O, :]
                v.wait_ge(s_std, 1)
                rsqrt(ch, v, r[0:O, :], r2[0:O, :], std[0:O, :], var[0:O, :])
                for b in range(B):
                    ch.inc(v.tensor_scalar(x[0:O, b, :], x[0:O, b, :], mean[:, b:b + 1], r[0:O, b:b + 1],
                                           ALU.subtract, ALU.mult))
                for b in range(B):
                    v.wait_ge(s_chain, ch.n - B + b + 1)
                    v.scalar_tensor_tensor(x[0:O, b, :], x[0:O, b, :], 0.2, x[0:O, b, :], ALU.mult, ALU.max)


def rsqrt(ch, v, r, t, std, var):
    ch.then(v.reciprocal(r, std))
    ch.then(v.tensor_tensor(t, r, r, ALU.mult))
    ch.then(v.tensor_tensor(t, t, var, ALU.mult))
    ch.then(v.tensor_scalar(t, t, -0.5, 1.5, ALU.mult, ALU.add))
    ch.then(v.tensor_tensor(r, r, t, ALU.mult))


def neighbour_counts(i):
    start, end = max(0, i - KNN // 2), min(N, i + KNN // 2 + 1)
    pos = [min(start + a, end - 1) for a in range(KNN)]
    return {p: pos.count(p) for p in pos}


def split_bf16(a):
    parts = []
    for _ in range(3):
        part = a.astype(NP_BF16)
        parts.append(part)
        a = a - part.astype(np.float32)
    return parts


def window_masks():
    pick = np.kron(np.eye(GP, dtype=np.float32), np.ones((1, KNN), np.float32))
    bias = np.full((GP, 9, G, 2, WIN, 2), -2.0 ** 30, np.float32)
    for kind in range(9):
        s = 0 if kind == 0 else PER - 1 if kind == 8 else 1
        for g in range(G):
            for r in range(GP):
                i = s * STEP + GP * g + r
                count = neighbour_counts(i) if i < N else {p: 1 for p in range(i - 5, N)}
                for p, c in count.items():
                    bias[r, kind, g, :, p - (s * STEP + GP * g - PAD), :] = 8 * np.log(np.float32(c))
    bias = bias.reshape(GP, -1)
    return (np.concatenate(split_bf16(pick)[:1] * 3), np.concatenate(split_bf16(bias)).reshape(3 * GP, 9, -1))


def lin_layouts(w, perm):
    w = np.asarray(w)
    cols = [((64 + 32 * c + 16 * h + x) * M + perm.index(m)) for c in range(2) for h in range(2)
            for m in range(M) for x in range(16)]
    return np.ascontiguousarray(w), np.ascontiguousarray(w[:, cols])


def points_out(k):
    nc = k.nc
    with ExitStack() as ctx:
        sb, ps, sem = placing(k, ctx)
        w3 = sb("w3", [P, 2, C])
        x3 = sb("x3", [C, B, N])
        xin = sb("xin", [C, B, N])
        st = sb("st", [C, B, 2, 6])
        mv3 = sb("mv3", [C, B, 2])
        psH = [ps(f"psH{i}", [P, 2, 512]) for i in range(2)]
        s_w3 = sem("s_w3")
        s_xin = sem("s_xin")
        s_h = sem("s_h")
        s_ev = sem("s_ev")
        s_st = sem("s_st")
        with nc.Block() as block:
            @block.sync
            def _(sp):
                sp.dma_start(w3[:, :, :], k.given["w_conv3"].rearrange("(h p) o -> p h o", p=P)).then_inc(s_w3, 16)
                sp.dma_start(xin[:, :, :], k.given["x"].rearrange("b c n -> c b n")).then_inc(s_xin, 16)
                sp.wait_ge(s_xin, 16)

            @block.tensor
            def _(pe):
                pe.wait_ge(s_w3, 16)
                for b in range(B):
                    if b >= 2:
                        pe.wait_ge(s_ev, b - 1)
                    for h in range(2):
                        for c, src in enumerate((k.F, k.M2)):
                            last = pe.matmul(psH[b % 2][0:C, h, :], w3[:, c, :], src[:, b, 512 * h:512 * h + 512],
                                             start=(c == 0), stop=(c == 1))
                    last.then_inc(s_h, 1)

            @block.scalar
            def _(act):
                for b in range(B):
                    act.wait_ge(s_h, b + 1)
                    act.copy(x3[:, b, :].rearrange("c (h n) -> c h n", h=2), psH[b % 2][0:C, :, :]).then_inc(s_ev, 1)

            @block.vector
            def _(v):
                for b in range(B):
                    v.wait_ge(s_ev, b + 1)
                    for h in range(2):
                        v.bn_stats(st[:, b, h, :], x3[:, b, 512 * h:512 * h + 512]).then_inc(s_st, 1)
                v.wait_ge(s_st, 2 * B)
                for b in range(B):
                    v.bn_aggr(mv3[:, b, :], st[:, b, :, :])
        instance_norm(k, x3, mv3, None, C)
        s_add = sem("s_add")
        s_x1 = sem("s_x1")
        with nc.Block() as block:
            @block.vector
            def _(v):
                for b in range(B):
                    v.tensor_tensor(x3[:, b, :], x3[:, b, :], xin[:, b, :], ALU.add).then_inc(s_add, 1)

            @block.sync
            def _(sp):
                for b in range(B):
                    sp.wait_ge(s_add, b + 1)
                    sp.dma_start(k.d_x1[C * b:C * b + C, :], x3[:, b, :]).then_inc(s_x1, 16)
                sp.wait_ge(s_x1, 16 * B)


TOK = B * C
TB = TOK // P
KC = N // P


def token_norm(k, X, xh, xl, load):
    nc = k.nc
    with ExitStack() as ctx:
        sb, ps, sem = placing(k, ctx)
        xn = sb("xn", [P, TB, N])
        st = sb("st", [P, TB, 2, 6])
        mv = sb("mv", [P, TB, 2])
        var = sb("var", [P, TB])
        std = sb("std", [P, TB])
        r = sb("r", [P, TB])
        t = sb("t", [P, TB])
        psX = [ps(f"psX{i}", [P, 4, P]) for i in range(4)]
        s_x = sem("s_x")
        s_st = sem("s_st")
        s_var = sem("s_var")
        s_std = sem("s_std")
        s_chain = sem("s_chain")
        s_xn = sem("s_xn")
        s_T = sem("s_T")
        s_hi = sem("s_hi")
        s_lo = sem("s_lo")
        with nc.Block() as block:
            @block.sync
            def _(sp):
                if load:
                    sp.dma_start(X[:, :, :], k.d_x1.rearrange("(t p) n -> p t n", p=P)).then_inc(s_x, 16)

            @block.vector
            def _(v):
                ch = Counted(v, s_chain)
                if load:
                    v.wait_ge(s_x, 16)
                for b in range(TB):
                    for h in range(2):
                        v.bn_stats(st[:, b, h, :], X[:, b, 512 * h:512 * h + 512]).then_inc(s_st, 1)
                v.wait_ge(s_st, 2 * TB)
                for b in range(TB):
                    ch.inc(v.bn_aggr(mv[:, b, :], st[:, b, :, :]))
                v.wait_ge(s_chain, ch.n)
                v.tensor_scalar(var[:, :], mv[:, :, 1], EPS, None, ALU.add).then_inc(s_var, 1)
                v.wait_ge(s_std, 1)
                rsqrt(ch, v, r[:, :], t[:, :], std[:, :], var[:, :])
                for b in range(TB):
                    v.tensor_scalar(xn[:, b, :], X[:, b, :], mv[:, b, 0:1], r[:, b:b + 1],
                                    ALU.subtract, ALU.mult).then_inc(s_xn, 1)
                for c in range(KC):
                    v.wait_ge(s_hi, c + 1)
                    v.tensor_tensor(xl[:, c, :], psX[c % 4][:, :, :].rearrange("p t n -> p (t n)"), xh[:, c, :],
                                    ALU.subtract).then_inc(s_lo, 1)

            @block.scalar
            def _(act):
                act.wait_ge(s_var, 1)
                act.activation(std[:, :], var[:, :], ACT.Sqrt).then_inc(s_std, 1)
                for c in range(KC):
                    act.wait_ge(s_T, c + 1)
                    act.copy(xh[:, c, :], psX[c % 4][:, :, :].rearrange("p t n -> p (t n)")).then_inc(s_hi, 1)

            @block.tensor
            def _(pe):
                pe.wait_ge(s_xn, TB)
                for c in range(KC):
                    if c >= 4:
                        pe.wait_ge(s_lo, c - 3)
                    for b in range(TB):
                        last = pe.transpose(psX[c % 4][:, b, :], xn[:, b, c * P:(c + 1) * P], k.id32[:, :])
                    last.then_inc(s_T, 1)


NH, NKV, HD = 32, 8, 128
REP = NH // NKV
def split_scales(v, ch, parts, raw):
    ch.then(v.tensor_copy(parts[0:96], raw[0:96]))
    ch.then(v.tensor_tensor(raw[0:96], raw[0:96], parts[0:96], ALU.subtract))
    ch.then(v.tensor_copy(parts[32:64], raw[32:64]))
    ch.then(v.tensor_copy(parts[64:96], raw[64:96]))
    ch.then(v.tensor_tensor(raw[64:96], raw[64:96], parts[64:96], ALU.subtract))
    return v.tensor_copy(parts[64:96], raw[64:96])


def attention(k, xh, xl, ctxh, ctxl):
    nc = k.nc
    with ExitStack() as ctx:
        sb, ps, sem = placing(k, ctx)
        QC, KV = REP * HD, 2 * HD
        NBLK = 2 * KC
        ROT = 1 + REP
        PAIRS = KC // 2
        qw = sb("qw", [P, 2, 2, QC], I32)
        kvw = sb("kvw", [P, 2, 2, KV], I32)
        SLAB = 1024
        pick = sb("pick", [96, 32, P], BF16)
        raw = sb("raw", [96, SLAB])
        sc = sb("sc", [96, 2, SLAB], BF16)
        wt = sb("wt", [P, 2, QC])
        wh = sb("wh", [P, 2, KC, QC + KV], F16)
        wl = sb("wl", [P, 2, KC, QC + KV], F16)
        cos = sb("cos", [P, C])
        sin = sb("sin", [P, C])
        rc = sb("rc", [P, 2, B, C])
        rs = sb("rs", [P, 2, B, C])
        kr = sb("kr", [P, 2, B, C])
        qr = sb("qr", [P, 2, B, REP, C])
        vT = sb("vT", [P, TOK])
        V = sb("V", [P, 2, TB, HD])
        mask = sb("mask", [P, C], BF16)
        idb = sb("idb", [P, P], BF16)
        Pr = sb("Pr", [P, 2, B, C])
        top = sb("top", [P, 2, B])
        tot = sb("tot", [P, 2, B])
        inv = sb("inv", [P, 2, B])
        PT = sb("PT", [P, 2, TB, P])
        psB = [ps(f"psB{i}", [P, 512]) for i in range(2)]
        psP = [ps(f"psP{i}", [P, 512]) for i in range(2)]
        psS = ps("psS", [P, B, C])
        psT = ps("psT", [P, TB, P])
        psC = ps("psC", [P, 2, TB, 2, C])
        s_c = sem("s_c")
        s_pick = sem("s_pick")
        s_raw = sem("s_raw")
        s_zero = sem("s_zero")
        s_chain = sem("s_chain")
        s_sc = sem("s_sc")
        s_wq = [sem("s_wq0"), sem("s_wq1")]
        s_bc = sem("s_bc")
        s_deq = sem("s_deq")
        s_hi = sem("s_hi")
        s_lo = sem("s_lo")
        s_pr = sem("s_pr")
        s_rope = sem("s_rope")
        s_qk = sem("s_qk")
        s_vT = sem("s_vT")
        s_tr = sem("s_tr")
        s_V = sem("s_V")
        s_S = sem("s_S")
        s_soft = sem("s_soft")
        s_sub = sem("s_sub")
        s_exp = sem("s_exp")
        s_prob = sem("s_prob")
        s_PT = sem("s_PT")
        s_ctx = sem("s_ctx")
        s_ch = sem("s_ch")
        s_cl = sem("s_cl")

        def block_of(j):
            pair, r = divmod(j, 4)
            return (2 * pair + r % 2, 0, QC) if r < 2 else (2 * pair + r % 2, QC, KV)

        with nc.Block() as block:
            @block.sync
            def _(sp):
                def load(g, pair):
                    c, u = slice(2 * pair, 2 * pair + 2), pair % 2
                    sp.dma_start(qw[:, u, :, :], k.given["qw_q"].rearrange("(c p) n -> p c n", p=P)
                                 [:, c, bass.ds(g * QC, QC)]).then_inc(s_wq[u], 16)
                    for i, w in enumerate((k.given["qw_k"], k.given["qw_v"])):
                        sp.dma_start(kvw[:, u, :, HD * i:HD * i + HD], w.rearrange("(c p) n -> p c n", p=P)
                                     [:, c, bass.ds(g * HD, HD)]).then_inc(s_wq[u], 16)

                def reload(g, pair):
                    sp.wait_ge(s_deq, g * NBLK + 4 * (pair - 1))
                    load(g, pair)

                def scales(slabs):
                    for p in range(3):
                        for i, src in enumerate(slabs):
                            at = 32 * p + KC * i
                            sp.dma_start(raw[at:at + KC, :], src).then_inc(s_raw, 16)

                sp.wait_ge(s_zero, 1)
                scales([k.given["sq"][:, SLAB * i:SLAB * i + SLAB] for i in range(4)])
                sp.dma_start(pick[:, :, :], k.given["c_pick"]).then_inc(s_pick, 16)
                for pair in range(2):
                    load(0, pair)
                sp.wait_ge(s_sc, 1)
                scales((k.given["sk"], k.given["sv"]))
                for dst, src in ((cos, "c_cos"), (sin, "c_sin"), (mask, "c_causal"), (idb, "c_idb")):
                    sp.dma_start(dst[:, :], k.given[src]).then_inc(s_c, 16)
                for pair in range(2, PAIRS):
                    reload(0, pair)
                with sp.Fori(1, NKV) as g:
                    for pair in range(PAIRS):
                        reload(g, pair)

            @block.tensor
            def _(pe):
                pickf = pick[:, :, :].rearrange("r c n -> r (c n)")

                def spread(g, j, first=False):
                    if not first:
                        pe.wait_ge(s_deq, g * NBLK + (j - 1))
                    c, o, w = block_of(j)
                    if o == 0:
                        last = pe.matmul(psB[j % 2][:, 0:w], pickf[:, bass.ds(g // 2 * (KC * P) + c * P, P)],
                                         sc[:, 0, bass.ds(g % 2 * QC, w)], start=True, stop=True)
                    else:
                        for i in range(2):
                            last = pe.matmul(psB[j % 2][:, HD * i:HD * i + HD], pick[:, KC * i + c, :],
                                             sc[:, 1, bass.ds(g * HD, HD)], start=True, stop=True)
                    last.then_inc(s_bc, 1)

                def project(g, u, slot, first, js):
                    js = list(js)
                    if slot == 0:
                        pe.wait_ge(s_lo, (g + 1) * NBLK)
                    if slot == 3:
                        pe.wait_ge(s_vT, g + 1)
                    elif not (first and slot < 2):
                        pe.wait_ge(s_rope, g * ROT + {0: -1, 1: 0, 2: 1, 4: 2, 5: 3}[slot])
                    o = {0: QC, 1: QC + HD}.get(slot, (slot - 2) * HD)
                    for c in range(KC):
                        for i, (w, x) in enumerate(((wh, xh), (wh, xl), (wl, xh))):
                            last = pe.matmul(psP[slot % 2][:, :], w[:, u, c, o:o + HD], x[:, c, :],
                                             start=(c == 0 and i == 0), stop=(c == KC - 1 and i == 2))
                        if c % 2 == 1 and js:
                            spread(g + 1, js.pop(0))
                    last.then_inc(s_pr, 1)

                def values(g, first):
                    pe.wait_ge(s_vT, g + 1)
                    if not first:
                        pe.wait_ge(s_PT, 2 * g)
                    for b in range(TB):
                        last = pe.transpose(psT[:, b, :], vT[:, b * P:(b + 1) * P], k.id32[:, :])
                    last.then_inc(s_tr, 1)

                def scores(g, u, h, first):
                    if first and h == 0:
                        pe.wait_ge(s_c, 64)
                    if h == 0:
                        pe.wait_ge(s_qk, (g + 1) * ROT)
                    if not (first and h == 0):
                        pe.wait_ge(s_sub, 2 * g + h)
                    pe.matmul(psS[:, :, :], idb[:, :], mask[:, :].unsqueeze(1).to_broadcast([P, B, C]),
                              start=True, stop=False)
                    for b in range(B):
                        last = pe.matmul(psS[:, b, :], qr[:, u, b, 2 * h:2 * h + 2, :], kr[:, u, b, :],
                                         start=False, stop=(b == B - 1))
                    last.then_inc(s_S, 1)

                def turn(g, h):
                    pe.wait_ge(s_prob, 2 * g + (h + 1))
                    if h == 0:
                        pe.wait_ge(s_V, g + 1)
                    else:
                        pe.wait_ge(s_PT, 2 * g + 1)
                    for b in range(TB):
                        last = pe.transpose(psT[:, b, :], Pr[:, h, 2 * b:2 * b + 2, :], k.id32[:, :])
                    last.then_inc(s_tr, 1)

                def context(g, u, h, first):
                    pe.wait_ge(s_PT, 2 * g + (h + 1))
                    if not (first and h == 0):
                        pe.wait_ge(s_cl, 2 * g + h)
                    for b in range(B):
                        r = slice(C * (b % 2), C * (b % 2) + C)
                        last = pe.matmul(psC[:, b % 2, b // 2, :, :], V[r, u, b // 2, :], PT[r, h, b // 2, :],
                                         start=True, stop=True)
                    last.then_inc(s_ctx, 1)

                def head(g, u, attend, ahead):
                    a, w, first = g - 1, 1 - u, attend == "first"
                    js = [range(a, b) if ahead else () for a, b in
                          ((0, 2), (2, 5), (5, 8), (8, 11), (11, 14), (14, 16))]
                    project(g, u, 0, not attend, js[0])
                    if attend:
                        scores(a, w, 0, first)
                    project(g, u, 1, not attend, js[1])
                    if attend:
                        scores(a, w, 1, first)
                    project(g, u, 2, not attend, js[2])
                    if attend:
                        turn(a, 0)
                    project(g, u, 3, not attend, js[3])
                    if attend:
                        context(a, w, 0, first)
                        turn(a, 1)
                    project(g, u, 4, not attend, js[4])
                    values(g, not attend)
                    if attend:
                        context(a, w, 1, first)
                    project(g, u, 5, not attend, js[5])

                pe.wait_ge(s_pick, 16)
                pe.wait_ge(s_sc, 2)
                for j in range(NBLK):
                    spread(0, j, j < 2)
                head(0, 0, None, True)
                head(1, 1, "first", True)
                with pe.Fori(1, NKV // 2 - 1) as t:
                    head(2 * t, 0, "later", True)
                    head(2 * t + 1, 1, "later", True)
                head(NKV - 2, 0, "later", True)
                head(NKV - 1, 1, "later", False)
                for h in range(2):
                    scores(NKV - 1, 1, h, False)
                for h in range(2):
                    turn(NKV - 1, h)
                    context(NKV - 1, 1, h, False)

            @block.vector
            def _(v):
                def dequant(g, j, first=False):
                    c, o, w = block_of(j)
                    pair = j // 4
                    if j % 4 == 0:
                        v.wait_ge(s_wq[pair % 2], g * 96 + (pair // 2 + 1) * 48)
                    v.wait_ge(s_bc, g * NBLK + (j + 1))
                    if not (first and j < 2):
                        v.wait_ge(s_lo, g * NBLK + (j - 1))
                    v.scalar_tensor_tensor(wt[:, j % 2, 0:w], (qw if o == 0 else kvw)[:, pair % 2, c % 2, :], 8.0,
                                           psB[j % 2][:, 0:w], ALU.subtract, ALU.mult).then_inc(s_deq, 1)

                def rotate(g, n, first):
                    slot = (0, 2, 3, 4, 5)[n]
                    v.wait_ge(s_pr, g * (2 + REP) + (slot + 1))
                    if not (first and n < 2):
                        v.wait_ge(s_qk, g * ROT + max(n - 1, 0))
                    x = psP[slot % 2][:, :].rearrange("p (b s) -> p b s", s=C)
                    cb = cos[:, :].unsqueeze(1).to_broadcast([P, B, C])
                    tb = sin[:, :].unsqueeze(1).to_broadcast([P, B, C])
                    H = HD // 2
                    v.tensor_tensor(rc[:, n % 2, :, :], x, cb, ALU.mult)
                    v.tensor_tensor(rs[0:H, n % 2, :, :], x[H:P], tb[H:P], ALU.mult)
                    v.tensor_tensor(rs[H:P, n % 2, :, :], x[0:H], tb[0:H], ALU.mult).then_inc(s_rope, 1)

                def soften(g, h):
                    v.wait_ge(s_S, 2 * g + (h + 1))
                    v.tensor_reduce(top[:, h, :], psS[:, :, :], AX.X, ALU.max).then_inc(s_soft, 1)
                    v.wait_ge(s_soft, 6 * g + (3 * h + 1))
                    v.tensor_tensor(Pr[:, h, :, :], psS[:, :, :], top[:, h, :].unsqueeze(2).to_broadcast([P, B, C]),
                                    ALU.subtract).then_inc(s_sub, 1)

                def probabilities(g, h):
                    v.wait_ge(s_exp, 2 * g + (h + 1))
                    v.tensor_reduce(tot[:, h, :], Pr[:, h, :, :], AX.X, ALU.add).then_inc(s_soft, 1)
                    v.wait_ge(s_soft, 6 * g + (3 * h + 2))
                    v.reciprocal(inv[:, h, :], tot[:, h, :]).then_inc(s_soft, 1)
                    v.wait_ge(s_soft, 6 * g + (3 * h + 3))
                    v.tensor_tensor(Pr[:, h, :, :], Pr[:, h, :, :], inv[:, h, :].unsqueeze(2).to_broadcast([P, B, C]),
                                    ALU.mult).then_inc(s_prob, 1)

                def rest(g, h):
                    v.wait_ge(s_ch, 2 * g + (h + 1))
                    for r in range(2):
                        hi, lo = (c[:, bass.ds(g * REP + 2 * h, 2), :]
                                  .rearrange("p x (t r s) -> p r x t s", r=2, s=C)[:, r] for c in (ctxh, ctxl))
                        last = v.tensor_tensor(lo, psC[:, r, :, :, :].rearrange("p t x s -> p x t s"), hi,
                                               ALU.subtract)
                    last.then_inc(s_cl, 1)

                def head(g, attend, ahead):
                    a, first = g - 1, not attend

                    def some(js):
                        for j in js if ahead else ():
                            dequant(g + 1, j)

                    rotate(g, 0, first)
                    if attend:
                        soften(a, 0)
                    some((0, 1, 2))
                    if attend:
                        probabilities(a, 0)
                    some((3, 4))
                    if attend:
                        soften(a, 1)
                    some((5,))
                    if attend:
                        probabilities(a, 1)
                    some((6, 7))
                    rotate(g, 1, first)
                    some((8, 9, 10))
                    rotate(g, 2, first)
                    some((11,))
                    if attend:
                        rest(a, 0)
                    some((12, 13))
                    rotate(g, 3, first)
                    if attend:
                        rest(a, 1)
                    some((14, 15))
                    rotate(g, 4, first)

                ch = Counted(v, s_chain)
                for i, loads in enumerate((12, 18)):
                    v.wait_ge(s_raw, 16 * loads)
                    split_scales(v, ch, sc[:, i, :], raw[:, :]).then_inc(s_sc, 1)
                for j in range(NBLK):
                    dequant(0, j, True)
                v.wait_ge(s_c, 64)
                head(0, False, True)
                with v.Fori(1, NKV - 1) as g:
                    head(g, True, True)
                head(NKV - 1, True, False)
                soften(NKV - 1, 0)
                probabilities(NKV - 1, 0)
                soften(NKV - 1, 1)
                probabilities(NKV - 1, 1)
                for h in range(2):
                    rest(NKV - 1, h)

            @block.scalar
            def _(act):
                def high(g, u, j):
                    c, o, w = block_of(j)
                    act.wait_ge(s_deq, g * NBLK + (j + 1))
                    act.copy(wh[:, u, c, o:o + w], wt[:, j % 2, 0:w]).then_inc(s_hi, 1)

                def exps(g, h):
                    act.wait_ge(s_sub, 2 * g + (h + 1))
                    act.activation(Pr[:, h, :, :], Pr[:, h, :, :], ACT.Exp, scale=float(HD) ** -0.5
                                   ).then_inc(s_exp, 1)

                def turned(g, h):
                    act.wait_ge(s_tr, 3 * g + (h + 2))
                    act.copy(PT[:, h, :, :], psT[:, :, :]).then_inc(s_PT, 1)

                def outputs(g, h):
                    act.wait_ge(s_ctx, 2 * g + (h + 1))
                    for r in range(2):
                        hi = (ctxh[:, bass.ds(g * REP + 2 * h, 2), :]
                              .rearrange("p x (t r s) -> p r x t s", r=2, s=C)[:, r])
                        last = act.copy(hi, psC[:, r, :, :, :].rearrange("p t x s -> p x t s"))
                    last.then_inc(s_ch, 1)

                def head(g, u, attend, ahead):
                    a = g - 1

                    def some(js):
                        for j in js if ahead else ():
                            high(g + 1, 1 - u, j)

                    if attend:
                        exps(a, 0)
                    some((0, 1, 2, 3, 4))
                    act.wait_ge(s_pr, g * (2 + REP) + 2)
                    act.mul(vT[:, :], psP[1][:, :], 1 / WSCALE).then_inc(s_vT, 1)
                    if attend:
                        exps(a, 1)
                    some((5, 6, 7))
                    if attend:
                        turned(a, 0)
                    some((8, 9, 10))
                    if attend:
                        outputs(a, 0)
                        turned(a, 1)
                    some((11,))
                    act.wait_ge(s_tr, 3 * g + 1)
                    act.copy(V[:, u, :, :], psT[:, :, :]).then_inc(s_V, 1)
                    some((12, 13))
                    if attend:
                        outputs(a, 1)
                    some((14, 15))

                for j in range(NBLK):
                    high(0, 0, j)
                head(0, 0, False, True)
                head(1, 1, True, True)
                with act.Fori(1, NKV // 2 - 1) as t:
                    head(2 * t, 0, True, True)
                    head(2 * t + 1, 1, True, True)
                head(NKV - 2, 0, True, True)
                head(NKV - 1, 1, True, False)
                for h in range(2):
                    exps(NKV - 1, h)
                for h in range(2):
                    turned(NKV - 1, h)
                    outputs(NKV - 1, h)

            @block.gpsimd
            def _(pool):
                def low(g, u, j):
                    c, o, w = block_of(j)
                    pool.wait_ge(s_hi, g * NBLK + (j + 1))
                    pool.tensor_tensor(wl[:, u, c, o:o + w], wt[:, j % 2, 0:w], wh[:, u, c, o:o + w],
                                       ALU.subtract).then_inc(s_lo, 1)

                def add(g, u, n, first):
                    if n == 0 and not first:
                        pool.wait_ge(s_S, 2 * g - 2)
                    pool.wait_ge(s_rope, g * ROT + (n + 1))
                    pool.tensor_tensor(kr[:, u, :, :] if n == 0 else qr[:, u, :, n - 1, :], rc[:, n % 2, :, :],
                                       rs[:, n % 2, :, :], ALU.add).then_inc(s_qk, 1)

                def head(g, u, first, ahead):
                    for n, js in enumerate((range(8), (8, 9, 10), (11, 12, 13), (14, 15), ())):
                        add(g, u, n, first)
                        for j in js if ahead else ():
                            low(g + 1, 1 - u, j)

                pool.memset(raw[:, :], 0.0).then_inc(s_zero, 1)
                for j in range(NBLK):
                    low(0, 0, j)
                head(0, 0, True, True)
                head(1, 1, True, True)
                with pool.Fori(1, NKV // 2 - 1) as t:
                    head(2 * t, 0, False, True)
                    head(2 * t + 1, 1, False, True)
                head(NKV - 2, 0, False, True)
                head(NKV - 1, 1, False, False)


def out_projection(k, X, ctxh, ctxl):
    nc = k.nc
    with ExitStack() as ctx:
        sb, ps, sem = placing(k, ctx)
        OCT, W, HALF = 8, 512, NH
        ow = sb("ow", [P, 2, OCT, W], I32)
        raw = sb("raw", [96, N])
        pick = sb("pick", [96, NH, P], BF16)
        sc = sb("sc", [96, 3 * W], BF16)
        zero = sb("zero", [P, W], F16)
        wt = sb("wt", [P, 4, W])
        wh = sb("wh", [P, 4, W], F16)
        wl = sb("wl", [P, 4, W], F16)
        psB = [ps(f"psB{i}", [P, 512]) for i in range(2)]
        psO = [ps(f"psO{i}", [P, 512]) for i in range(TB)]
        s_raw = sem("s_raw")
        s_chain = sem("s_chain")
        s_sc = sem("s_sc")
        s_ow = [sem("s_ow0"), sem("s_ow1")]
        s_bc = sem("s_bc")
        s_deq = sem("s_deq")
        s_hi = sem("s_hi")
        s_lo = sem("s_lo")
        s_mm = sem("s_mm")
        s_half = sem("s_half")
        s_zero = sem("s_zero")
        s_pick = sem("s_pick")
        s_xin = sem("s_xin")
        s_x = sem("s_x")

        AHEAD = 4

        def blocks(eng, each, begin=None, end=None):
            with eng.Fori(0, 2) as hf:
                if begin:
                    begin(hf)
                with eng.Fori(0, 2) as q:
                    for i in range(2 * OCT):
                        each(hf, q, i, hf * HALF + q * (2 * OCT) + i)
                if end:
                    end(hf)

        with nc.Block() as block:
            @block.sync
            def _(sp):
                for p in range(3):
                    sp.dma_start(raw[32 * p:32 * p + NH, :], k.given["so"]).then_inc(s_raw, 16)
                sp.dma_start(pick[:, :, :], k.given["c_pick"]).then_inc(s_pick, 16)
                sp.dma_start(X[:, :, :], k.d_x1.rearrange("(t p) n -> p t n", p=P)).then_inc(s_xin, 16)
                wo = k.given["qw_o"].rearrange("(h p) n -> p h n", p=P)
                for o in range(8):
                    if o >= 2:
                        sp.wait_ge(s_deq, OCT * (o - 1))
                    sp.dma_start(ow[:, o % 2, :, :], wo[:, o % 4 * OCT:o % 4 * OCT + OCT, o // 4 * W:o // 4 * W + W]
                                 ).then_inc(s_ow[o % 2], 16)

            @block.tensor
            def _(pe):
                pickf = pick[:, :, :].rearrange("r h n -> r (h n)")
                cf = [c[:, :, :].rearrange("p h n -> p (h n)") for c in (ctxh, ctxl)]
                pe.sem_inc(s_mm, AHEAD)

                def spread(i, h, col):
                    pe.matmul(psB[i % 2][:, :], pickf[:, bass.ds(h * P, P)], sc[:, bass.ds(col, W)],
                              start=True, stop=True).then_inc(s_bc, 1)

                def clear(start):
                    for b in range(TB):
                        mm = pe.matmul(psO[b][:, :], zero[:, 0:P], zero[:, :], start=start, stop=not start)
                    return mm

                def begin(hf):
                    pe.wait_ge(s_x, hf * TB + 1)
                    clear(True)

                def each(hf, q, i, J):
                    pe.wait_ge(s_deq, J + 1)
                    spread(i, (J + 2) % HALF, (J + 2) // HALF * W)
                    pe.wait_ge(s_lo, J + (AHEAD + 1))
                    h = q * (2 * OCT) + i
                    for b in range(TB):
                        hi, lo = (c[:, bass.ds(h * TOK + P * b, P)] for c in cf)
                        for x, w in ((hi, wh), (lo, wh), (hi, wl)):
                            mm = pe.matmul(psO[b][:, :], x, w[:, i % AHEAD, :], start=False, stop=False)
                    mm.then_inc(s_mm, 1)

                pe.wait_ge(s_zero, 1)
                pe.wait_ge(s_pick, 16)
                pe.wait_ge(s_sc, 1)
                for J in range(2):
                    spread(J, J, 0)
                blocks(pe, each, begin, lambda hf: clear(False).then_inc(s_half, 1))

            @block.vector
            def _(v):
                ch = Counted(v, s_chain)
                v.sem_inc(s_x, 1)
                v.wait_ge(s_zero, 2)
                v.wait_ge(s_raw, 48)
                split_scales(v, ch, sc[:, 0:N], raw[:, :]).then_inc(s_sc, 1)

                def each(hf, q, i, J):
                    if i % OCT == 0:
                        v.wait_ge(s_ow[i // OCT], hf * 32 + q * 16 + 16)
                    v.wait_ge(s_bc, J + 1)
                    v.wait_ge(s_lo, J + 1)
                    v.scalar_tensor_tensor(wt[:, i % AHEAD, :], ow[:, i // OCT, i % OCT, :], 8.0, psB[i % 2][:, :],
                                           ALU.subtract, ALU.mult).then_inc(s_deq, 1)

                def end(hf):
                    v.wait_ge(s_half, hf + 1)
                    for b in range(TB):
                        x = X[:, b, bass.ds(hf * W, W)]
                        v.scalar_tensor_tensor(x, psO[b][:, :], 1 / WSCALE, x, ALU.mult, ALU.add).then_inc(s_x, 1)

                v.wait_ge(s_xin, 16)
                blocks(v, each, end=end)

            @block.scalar
            def _(act):
                def each(hf, q, i, J):
                    act.wait_ge(s_deq, J + 1)
                    act.wait_ge(s_mm, J + 1)
                    act.copy(wh[:, i % AHEAD, :], wt[:, i % AHEAD, :]).then_inc(s_hi, 1)

                blocks(act, each)

            @block.gpsimd
            def _(pool):
                pool.memset(zero[:, :], 0.0).then_inc(s_zero, 1)
                pool.memset(sc[:, :], 0.0).then_inc(s_zero, 1)
                pool.sem_inc(s_lo, AHEAD)

                def each(hf, q, i, J):
                    pool.wait_ge(s_hi, J + 1)
                    pool.tensor_tensor(wl[:, i % AHEAD, :], wt[:, i % AHEAD, :], wh[:, i % AHEAD, :],
                                       ALU.subtract).then_inc(s_lo, 1)

                blocks(pool, each)


NE, RANK = 8, 32


def feed_forward(k, X, xh, xl):
    nc = k.nc
    with ExitStack() as ctx:
        sb, ps, sem = placing(k, ctx)
        WA = N + RANK
        w = sb("w", [P, 2, WA])
        wh = sb("wh", [P, KC, WA], F16)
        wl = sb("wl", [P, KC, WA], F16)
        bias = sb("bias", [P, N])
        bm = sb("bm", [RANK, N])
        lim = sb("lim", [NE, RANK])
        limT = sb("limT", [RANK, NE])
        odd = sb("odd", [P, 1])
        H = sb("H", [P, TB, N])
        zT = sb("zT", [RANK, TOK])
        zp = sb("zp", [RANK, TOK])
        lg = sb("lg", [P, 2, TB, NE])
        e = sb("e", [P, TB, NE])
        g = sb("g", [P, TB, NE])
        best = sb("best", [P, TB, NE])
        one = sb("one", [P, 16])
        mx = sb("mx", [P, 2])
        mxa = sb("mxa", [P, 2])
        gT = sb("gT", [NE, TOK])
        psH = [ps(f"psH{i}", [P, 512]) for i in range(4)]
        psZ = ps("psZ", [RANK, TOK])
        psD = ps("psD", [P, TB, NE])
        psG = ps("psG", [NE, TOK])
        s_c = sem("s_c")
        s_w = [sem("s_w0"), sem("s_w1")]
        s_hi = sem("s_hi")
        s_lo = sem("s_lo")
        s_z = sem("s_z")
        s_zT = sem("s_zT")
        s_h = sem("s_h")
        s_H = sem("s_H")
        s_d = sem("s_d")
        s_mx = sem("s_mx")
        s_all = sem("s_all")
        s_act = sem("s_act")
        s_need = sem("s_need")
        s_chain = sem("s_chain")
        s_g = sem("s_g")
        s_gT = sem("s_gT")
        s_gc = sem("s_gc")
        s_p = sem("s_p")
        s_zp = sem("s_zp")
        s_dl = sem("s_dl")
        s_y = sem("s_y")
        s_out = sem("s_out")
        tiles = [(b, h) for h in range(2) for b in range(TB)]

        with nc.Block() as block:
            @block.sync
            def _(sp):
                sp.dma_start(bias[:, :], k.given["ffn_b"].partition_broadcast(P)).then_inc(s_c, 16)
                sp.dma_start(bm[:, :], k.given["ffn_Bmat"]).then_inc(s_c, 16)
                sp.dma_start(lim[:, :], k.given["ffn_lim"]).then_inc(s_c, 16)
                sp.dma_start(limT[:, :], k.given["ffn_limT"]).then_inc(s_c, 16)
                sp.dma_start(odd[:, :], k.given["c_odd"]).then_inc(s_c, 16)
                for c in range(KC):
                    if c >= 2:
                        sp.wait_ge(s_lo, c - 1)
                    sp.dma_start(w[:, c % 2, 0:N], k.given["ffn_WT"][c * P:(c + 1) * P, :]).then_inc(s_w[c % 2], 16)
                    sp.dma_start(w[:, c % 2, N:WA], k.given["ffn_A"][c * P:(c + 1) * P, :]).then_inc(s_w[c % 2], 16)
                for i, (b, h) in enumerate(tiles):
                    sp.wait_ge(s_y, i + 1)
                    sp.dma_start(k.given["out"][b * P:(b + 1) * P, 512 * h:512 * h + 512], X[:, b, 512 * h:512 * h + 512]
                                 ).then_inc(s_out, 16)
                sp.wait_ge(s_out, 16 * len(tiles))

            @block.scalar
            def _(act):
                for c in range(KC):
                    act.wait_ge(s_w[c % 2], 32 * (c // 2 + 1))
                    act.mul(wh[:, c, :], w[:, c % 2, :], WSCALE).then_inc(s_hi, 1)
                act.wait_ge(s_z, 1)
                act.mul(zT[:, :], psZ[:, :], 1 / WSCALE).then_inc(s_zT, 1)
                act.wait_ge(s_need, 1)
                act.activation(e[:, :, :], e[:, :, :], ACT.Exp).then_inc(s_act, 1)
                act.wait_ge(s_need, 2)
                act.activation(g[:, :, :], g[:, :, :], ACT.Sigmoid, scale=2.0).then_inc(s_act, 1)

            @block.gpsimd
            def _(pool):
                pool.wait_ge(s_mx, 1)
                pool.partition_all_reduce(mxa[:, :], mx[:, :], P, bass.bass_isa.ReduceOp.max).then_inc(s_all, 1)

            @block.tensor
            def _(pe):
                trio = ((xh, wh), (xl, wh), (xh, wl))
                pe.wait_ge(s_lo, KC)
                for c in range(KC):
                    for q, (x, ww) in enumerate(trio):
                        last = pe.matmul(psZ[:, :], ww[:, c, N:WA], x[:, c, :],
                                         start=(c == 0 and q == 0), stop=(c == KC - 1 and q == 2))
                last.then_inc(s_z, 1)
                for i, (b, h) in enumerate(tiles):
                    if i >= 4:
                        pe.wait_ge(s_H, i - 3)
                    for c in range(KC):
                        for q, (x, ww) in enumerate(trio):
                            last = pe.matmul(psH[i % 4][:, :], x[:, c, b * P:(b + 1) * P],
                                             ww[:, c, 512 * h:512 * h + 512],
                                             start=(c == 0 and q == 0), stop=(c == KC - 1 and q == 2))
                    last.then_inc(s_h, 1)
                    if i == 0:
                        pe.wait_ge(s_zT, 1)
                        pe.wait_ge(s_c, 16 * 5)
                        for t in range(TB):
                            last = pe.matmul(psD[:, t, :], zT[:, t * P:(t + 1) * P], limT[:, :], start=True, stop=True)
                        last.then_inc(s_d, 1)
                pe.wait_ge(s_g, 1)
                for t in range(TB):
                    last = pe.transpose(psG[:, t * P:(t + 1) * P], g[:, t, :], k.id32[:, :])
                last.then_inc(s_gT, 1)
                pe.wait_ge(s_gc, 1)
                pe.matmul(psZ[:, :], lim[:, :], gT[:, :], start=True, stop=True).then_inc(s_p, 1)
                pe.wait_ge(s_zp, 1)
                pe.wait_ge(s_H, len(tiles))
                for i, (b, h) in enumerate(tiles):
                    if i >= 4:
                        pe.wait_ge(s_y, i - 3)
                    pe.matmul(psH[i % 4][:, :], zp[:, b * P:(b + 1) * P], bm[:, 512 * h:512 * h + 512],
                              start=True, stop=True).then_inc(s_dl, 1)

            @block.vector
            def _(v):
                ch = Counted(v, s_chain)
                for c in range(KC):
                    v.wait_ge(s_hi, c + 1)
                    v.scalar_tensor_tensor(wl[:, c, :], w[:, c % 2, :], WSCALE, wh[:, c, :],
                                           ALU.mult, ALU.subtract).then_inc(s_lo, 1)
                v.wait_ge(s_c, 16 * 5)

                def hidden(i):
                    b, h = tiles[i]
                    v.wait_ge(s_h, i + 1)
                    v.scalar_tensor_tensor(H[:, b, 512 * h:512 * h + 512], psH[i % 4][:, :], 1 / WSCALE,
                                           bias[:, 512 * h:512 * h + 512], ALU.mult, ALU.add).then_inc(s_H, 1)

                for i in range(TB):
                    hidden(i)
                v.wait_ge(s_H, TB)
                v.wait_ge(s_d, 1)
                ch.inc(v.tensor_copy(lg[:, 0, :, :], H[:, :, 0:NE]))
                ch.then(v.tensor_copy(lg[:, 1, :, :], psD[:, :, :]))
                ch.then(v.tensor_reduce(one[:, 0:2], lg[:, :, :, :].rearrange("p h t e -> p h (t e)"), AX.X, ALU.max,
                                        apply_absolute_value=True))
                v.tensor_scalar(mx[:, :], one[:, 0:2], odd[:, :], None, ALU.mult).then_inc(s_mx, 1)
                v.wait_ge(s_all, 1)
                ch.then(v.tensor_scalar(one[:, 2:4], mxa[:, :], 1e-6, None, ALU.max))
                ch.then(v.reciprocal(one[:, 4:6], one[:, 2:4]))
                ch.then(v.tensor_scalar(e[:, :, :], lg[:, 0, :, :], one[:, 4:5], 0.5, ALU.mult, ALU.mult))
                ch.then(v.tensor_scalar(g[:, :, :], lg[:, 1, :, :], one[:, 5:6], 0.5, ALU.mult, ALU.mult))
                ch.then(v.tensor_tensor(e[:, :, :], e[:, :, :], g[:, :, :], ALU.add))
                ch.then(v.tensor_reduce(one[:, 6:10], e[:, :, :], AX.X, ALU.max))
                v.tensor_tensor(e[:, :, :], e[:, :, :], one[:, 6:10].unsqueeze(2).to_broadcast([P, TB, NE]),
                                ALU.subtract).then_inc(s_need, 1)
                v.wait_ge(s_act, 1)
                ch.then(v.tensor_reduce(one[:, 6:10], e[:, :, :], AX.X, ALU.add))
                ch.then(v.reciprocal(one[:, 10:14], one[:, 6:10]))
                ch.then(v.tensor_tensor(e[:, :, :], e[:, :, :], one[:, 10:14].unsqueeze(2).to_broadcast([P, TB, NE]),
                                        ALU.mult))
                for t in range(TB):
                    ch.inc(v.max(best[:, t, :], e[:, t, :]))
                v.wait_ge(s_chain, ch.n)
                v.tensor_tensor(g[:, :, :], e[:, :, :], best[:, :, 1:2].to_broadcast([P, TB, NE]),
                                ALU.subtract).then_inc(s_need, 1)
                v.wait_ge(s_act, 2)
                ch.then(v.tensor_tensor(g[:, :, :], e[:, :, :], g[:, :, :], ALU.mult))
                ch.then(v.tensor_reduce(one[:, 6:10], g[:, :, :], AX.X, ALU.add))
                ch.then(v.tensor_scalar(one[:, 6:10], one[:, 6:10], 1e-9, None, ALU.add))
                ch.then(v.reciprocal(one[:, 10:14], one[:, 6:10]))
                v.tensor_tensor(g[:, :, :], g[:, :, :], one[:, 10:14].unsqueeze(2).to_broadcast([P, TB, NE]),
                                ALU.mult).then_inc(s_g, 1)
                v.wait_ge(s_gT, 1)
                pairs = psG[:, :].rearrange("e (t o) -> e t o", o=2)[:, :, 1:2]
                v.tensor_copy(gT[:, :].rearrange("e (t o) -> e t o", o=2), pairs.to_broadcast([NE, TOK // 2, 2])
                              ).then_inc(s_gc, 1)
                v.wait_ge(s_p, 1)
                ch.then(v.tensor_tensor(zp[:, :], zT[:, :], psZ[:, :], ALU.mult))
                v.tensor_scalar(zp[:, :], zp[:, :], 0.5, None, ALU.mult).then_inc(s_zp, 1)
                for i in range(TB, 2 * TB):
                    hidden(i)
                v.wait_ge(s_H, 2 * TB)
                for b, h in tiles:
                    x = X[:, b, 512 * h:512 * h + 512]
                    ch.inc(v.tensor_tensor(x, x, H[:, b, 512 * h:512 * h + 512], ALU.add))
                v.wait_ge(s_chain, ch.n)
                for i, (b, h) in enumerate(tiles):
                    v.wait_ge(s_dl, i + 1)
                    x = X[:, b, 512 * h:512 * h + 512]
                    v.tensor_tensor(x, x, psH[i % 4][:, :], ALU.add).then_inc(s_y, 1)


def constants(k):
    with k.nc.semaphore("s_const") as s_const, k.nc.Block() as block:
        @block.sync
        def _(sp):
            pairs = ((k.id32, k.given["c_id32"]), (k.id16, k.given["c_id16"]), (k.ramp, k.given["c_ramp"]))
            for dst, src in pairs:
                sp.dma_start(dst[:, :], src).then_inc(s_const, 16)
            sp.wait_ge(s_const, 16 * len(pairs))


def copy_features(k):
    with k.nc.semaphore("s_cf") as s_cf, k.nc.Block() as block:
        @block.sync
        def _(sp):
            sp.dma_start(k.F[C:P, :, :], k.M2[0:C, :, :]).then_inc(s_cf, 16)
            sp.wait_ge(s_cf, 16)


def build(nc, given):
    k = Kernel(nc, given)
    with ExitStack() as ctx:
        sb, ps, sem = placing(k, ctx)
        k.id32 = sb("id32", [P, P])
        k.id16 = sb("id16", [P, P], F16)
        with ExitStack() as first:
            sb, ps, sem = placing(k, first)
            k.ramp = sb("ramp", [P, N], F16)
            k.F = sb("F", [P, B, N])
            k.M2 = sb("M2", [P, B, N])
            k.rank = sb("rank", [P, B * M, NB])
            mv = sb("mv", [P, B, 2])
            outputs = (C, 2 * C)
            wn = [sb(f"wn{i}", [P, 2, 2, O], F16) for i, O in enumerate(outputs)]
            wd = [sb(f"wd{i}", [C, 3, O], F16) for i, O in enumerate(outputs)]
            hb = [sb(f"hb{i}", [P, 1]) for i in range(2)]
            constants(k)
            combine_weights(k, [(given[f"lin{i + 1}"], given[f"win{i + 1}"], given[f"w_conv{i + 1}"],
                                 given[f"b_lin{i + 1}"], O, wn[i], wd[i], hb[i]) for i, O in enumerate(outputs)])
            curve_keys(k)
            curve_ranks(k)
            for i, (O, src) in enumerate(zip(outputs, (k.F, k.M2))):
                with ExitStack() as layer:
                    sb, ps, sem = placing(k, layer)
                    centre = sb("centre", [P, B * NB, 2, O], F16)
                    with ExitStack() as turned:
                        sb, ps, sem = placing(k, turned)
                        k.fT = sb("fT", [P, B, NB, P], F16)
                        split_features(k, src, centre, wd[i], O)
                        gather(k)
                    edge_layer(k, centre, wn[i], O, k.M2[0:O, :, :], mv)
                instance_norm(k, k.M2, mv, hb[i], O)
                if i == 0:
                    copy_features(k)
            points_out(k)
        nc.clear_and_free_semaphores(k.sems)
        nc.all_engine_barrier()
        with ExitStack() as second:
            sb, ps, sem = placing(k, second)
            xh = sb("xh", [P, KC, TOK], F16)
            xl = sb("xl", [P, KC, TOK], F16)
            with ExitStack() as rows:
                sb1, _, _ = placing(k, rows)
                token_norm(k, sb1("X", [P, TB, N]), xh, xl, True)
            ctxh = sb("ctxh", [P, NH, TOK], F16)
            ctxl = sb("ctxl", [P, NH, TOK], F16)
            attention(k, xh, xl, ctxh, ctxl)
            X = sb("X", [P, TB, N])
            out_projection(k, X, ctxh, ctxl)
            token_norm(k, X, xh, xl, False)
            feed_forward(k, X, xh, xl)


def rope_tables():
    inv = 1.0 / np.float32(10000.0) ** (np.arange(0, HD, 2, dtype=np.float32) / np.float32(HD))
    angle = np.arange(C, dtype=np.float32)[:, None] * inv.astype(np.float32)
    cos, sin = np.cos(angle).T.astype(np.float32), np.sin(angle).T.astype(np.float32)
    scale = np.float32(1 / WSCALE)
    return np.concatenate([cos, cos]) * scale, np.concatenate([sin, -sin]) * scale


def kernel(**inputs):
    import concourse.bacc as bacc
    from concourse.bass_utils import run_bass_kernel_spmd

    a = {n: np.asarray(v) for n, v in inputs.items()}
    pick = np.zeros((96, 32, P), np.float32)
    for r in range(96):
        pick[r, r % 32] = WSCALE
    q, s = np.meshgrid(np.arange(P) % C, np.arange(C), indexing="ij")
    mkl, mkr = window_masks()
    cos, sin = rope_tables()
    arrays = {
        "x": a["x"], "coords": a["ctx_4096"][:, 0:3, :],
        "sq": a["L0_attn_scales_q"], "sk": a["L0_attn_scales_k"], "sv": a["L0_attn_scales_v"],
        "so": a["L0_attn_scales_o"], "qw_q": a["L0_attn_qw_q"], "qw_k": a["L0_attn_qw_k"],
        "qw_v": a["L0_attn_qw_v"], "qw_o": a["L0_attn_qw_o"],
        "ffn_WT": a["L0_ffn_W"].T, "ffn_b": a["L0_ffn_b"], "ffn_A": a["L0_ffn_A"], "ffn_Bmat": a["L0_ffn_Bmat"],
        "ffn_lim": a["L0_ffn_LiMEs"], "ffn_limT": a["L0_ffn_LiMEs"].T,
        "w_conv1": a["L0_xattn_W_conv1"].T, "w_conv2": a["L0_xattn_W_conv2"].T, "w_conv3": a["L0_xattn_W_conv3"].T,
        "b_lin1": a["L0_xattn_b_lin1"][:, None], "b_lin2": a["L0_xattn_b_lin2"][:, None],
        "c_id32": np.eye(P, dtype=np.float32), "c_id16": np.eye(P, dtype=np.float16),
        "c_idb": np.eye(P, dtype=np.float32).astype(NP_BF16),
        "c_ramp": np.tile(np.arange(N, dtype=np.float16), (P, 1)),
        "c_pick": pick.astype(NP_BF16), "c_mkl": mkl, "c_mkr": mkr, "c_cos": cos, "c_sin": sin,
        "c_causal": np.where(s > q, -2.0 ** 30, 0.0).astype(np.float32).astype(NP_BF16),
        "c_spread": np.ascontiguousarray(np.kron(np.eye(P, dtype=np.float16), np.ones((1, KNN), np.float16))
                                         .reshape(P, 2, STEP * KNN)),
        "c_odd": (np.arange(P, dtype=np.float32) % 2)[:, None],
    }
    for layer, perm in ((1, [2, 0, 3, 1]), (2, [1, 3, 0, 2])):
        plain, ordered = lin_layouts(a[f"L0_xattn_W_lin{layer}"], perm)
        arrays[f"lin{layer}"], arrays[f"win{layer}"] = plain, ordered
    nc = bacc.Bacc("TRN2", target_bir_lowering=False, num_devices=1)
    arrays = {f"in_{n}": np.ascontiguousarray(v) for n, v in arrays.items()}
    t = {n[3:]: nc.dram_tensor(n, v.shape, mybir.dt.from_np(v.dtype), kind="ExternalInput").ap()
         for n, v in arrays.items()}
    t["out"] = nc.dram_tensor("out", (TOK, N), F32, kind="ExternalOutput").ap()
    build(nc, t)
    got = run_bass_kernel_spmd(nc, [arrays], core_ids=[0])
    return got.results[0]["out"].reshape(B, C, N)
```

```python
from contextlib import ExitStack

import numpy as np
import concourse.bass as bass
from concourse import mybir

ALU = mybir.AluOpType
ACT = mybir.ActivationFunctionType
AX = mybir.AxisListType
F32, F16, BF16, I32 = mybir.dt.float32, mybir.dt.float16, mybir.dt.bfloat16, mybir.dt.int32
NP_BF16 = mybir.dt.np(BF16)

P = 128
B, C, N = 8, 64, 1024
M = 4
KNN = 10
NB = N // P
EPS = 1e-5
WSCALE = 256.0


class Kernel:

    def __init__(self, nc, given):
        self.nc, self.given = nc, given
        self.stage, self.sems = 0, []
        self.d_quant = nc.dram_tensor("d_quant", (3 * B, N), I32).ap()
        self.d_key = nc.dram_tensor("d_key", (2, B, M, N), F32).ap()
        self.d_f = nc.dram_tensor("d_f", (B, C, N), F32).ap()
        self.d_g = nc.dram_tensor("d_g", (B, 8, M, 16, N), F16).ap()
        self.d_x1 = nc.dram_tensor("d_x1", (B * C, N), F32).ap()


class Counted:

    def __init__(self, eng, sem, start=0):
        self.eng, self.sem, self.start, self.n = eng, sem, start, 0

    def inc(self, ins):
        self.n += 1
        ins.then_inc(self.sem, 1)

    def then(self, ins):
        self.inc(ins)
        self.eng.wait_ge(self.sem, self.start + self.n)


def placing(k, ctx):
    k.stage += 1
    nc, tag = k.nc, f"_{k.stage}"

    def sb(name, shape, dt=F32):
        return ctx.enter_context(nc.sbuf_tensor(name + tag, shape, dt))

    def ps(name, shape, dt=F32):
        return ctx.enter_context(nc.psum_tensor(name + tag, shape, dt))

    def sem(name):
        k.sems.append(nc.alloc_semaphore(name + tag))
        return k.sems[-1]

    return sb, ps, sem


def combine_weights(sb, ps, sem, layers):
    s_w, s_comb, s_hi, s_both = sem("s_w"), sem("s_comb"), sem("s_hi"), sem("s_both")
    lin, win, conv, bias, near, both, psN, psD = [], [], [], [], [], [], [], []
    for i, (_, _, _, _, O, _, _, _) in enumerate(layers):
        lin.append(sb(f"lin{i}", [P, 2 * C * M]))
        win.append(sb(f"win{i}", [P, 2, P]))
        conv.append(sb(f"conv{i}", [P, O]))
        bias.append(sb(f"bias{i}", [P, 1]))
        psN.append(ps(f"psN{i}", [P, 2, O]))
        psD.append(ps(f"psD{i}", [P, 2 * O + 1]))
        near.append(sb(f"near{i}", [C, O]))
        both.append(sb(f"both{i}", [C, O]))

    def load(sp):
        for i, (w_lin, w_win, w_conv, b_lin, _, _, _, _) in enumerate(layers):
            sp.dma_start(lin[i][:, :], w_lin).then_inc(s_w, 16)
            sp.dma_start(win[i][:, :, :], w_win.rearrange("c (k r) -> c k r", k=2)).then_inc(s_w, 16)
            sp.dma_start(conv[i][:, :], w_conv).then_inc(s_w, 16)
            sp.dma_start(bias[i][:, :], b_lin).then_inc(s_w, 16)

    def products(pe):
        pe.wait_ge(s_w, 16 * 4 * len(layers))
        for i, (_, _, _, _, O, _, _, _) in enumerate(layers):
            for c in range(2):
                pe.matmul(psN[i][:, c, :], win[i][:, c, :], conv[i][:, :], start=True, stop=True)
            by_curve = lin[i][:, :].rearrange("c (h r m) -> c h m r", h=2, m=M)
            for h in range(2):
                for m in range(M):
                    pe.matmul(psD[i][0:C, h * O:(h + 1) * O], by_curve[:, h, m, :], conv[i][:, :],
                              start=(m == 0), stop=(m == M - 1))
            pe.matmul(psD[i][0:O, 2 * O:2 * O + 1], conv[i][:, :], bias[i][:, :], start=True, stop=True
                      ).then_inc(s_comb, 1)

    def copies(act):
        for i, (_, _, _, _, O, wn, wd, hb) in enumerate(layers):
            act.wait_ge(s_comb, i + 1)
            act.mul(wn[:, 0, :, :], psN[i][:, :, :], WSCALE).then_inc(s_hi, 1)
            act.copy(hb[0:O, :], psD[i][0:O, 2 * O:2 * O + 1])
            act.mul(near[i][:, :], psD[i][0:C, O:2 * O], -WSCALE).then_inc(s_hi, 1)
            act.wait_ge(s_hi, 3 * i + 2)
            act.copy(wd[:, 2, :], near[i][:, :])
            act.wait_ge(s_both, i + 1)
            act.copy(wd[:, 0, :], both[i][:, :]).then_inc(s_hi, 1)

    def rests(v):
        for i, (_, _, _, _, O, wn, wd, hb) in enumerate(layers):
            v.wait_ge(s_hi, 3 * i + 2)
            v.scalar_tensor_tensor(both[i][:, :], psD[i][0:C, 0:O], WSCALE, near[i][:, :], ALU.mult, ALU.add
                                   ).then_inc(s_both, 1)
            v.scalar_tensor_tensor(wn[:, 1, :, :], psN[i][:, :, :], WSCALE, wn[:, 0, :, :],
                                   ALU.mult, ALU.subtract)
            v.wait_ge(s_hi, 3 * i + 3)
            v.wait_ge(s_both, i + 1)
            v.tensor_tensor(wd[:, 1, :], both[i][:, :], wd[:, 0, :], ALU.subtract)

    return load, products, copies, rests


def curve_keys(k, layers):
    nc = k.nc
    with ExitStack() as ctx:
        sb, ps, sem = placing(k, ctx)
        NQ = 3 * B
        xs = sb("xs", [C, B, N], F32)
        xstat = sb("xstat", [C, B, 2, 6], F32)
        xmv = sb("xmv", [C, B, 2], F32)
        xstd = sb("xstd", [C, B], F32)
        xrstd = sb("xrstd", [C, B], F32)
        co = sb("co", [NQ, N], F32)
        cq = sb("cq", [NQ, N], F32)
        cfl = sb("cfl", [NQ, N], F32)
        cint = sb("cint", [NQ, N], I32)
        col = sb("col", [NQ, 16], F32)
        coli = col[:, :].bitcast(I32)
        X = sb("X", [P, 3, M, 64], I32)
        T = sb("T", [P, 3, M, 64], I32)
        mask = sb("mask", [P, 2, 64], I32)
        flip = sb("flip", [P, 2, 64], I32)
        point = sb("point", [P, 64], I32)
        key = sb("key", [P, 2, M, 64], I32)
        keyf = sb("keyf", [P, 2, M, 64], F32)
        epsc = sb("epsc", [P, 1], F32)

        load_weights, products, copies, rests = combine_weights(sb, ps, sem, layers)
        s_const = sem("s_const")
        s_x = sem("s_x")
        s_co = sem("s_co")
        s_chain = sem("s_chain")
        s_var = sem("s_var")
        s_std = sem("s_std")
        s_eps = sem("s_eps")
        s_cint = sem("s_cint")
        s_qout = sem("s_qout")
        s_qin = sem("s_qin")
        s_point = sem("s_point")
        s_keyf = sem("s_keyf")
        s_kout = sem("s_kout")
        s_rstd = sem("s_rstd")

        with nc.Block() as block:
            @block.sync
            def _(sp):
                sp.dma_start(co[:, :], k.given["coords"].rearrange("b a n -> (b a) n")).then_inc(s_co, 16)
                sp.dma_start(xs[:, :, :], k.given["x"].rearrange("b c n -> c b n")).then_inc(s_x, 16)
                load_weights(sp)
                for dst, src in ((k.id32, "c_id32"), (k.id16, "c_id16"), (k.ramp, "c_ramp")):
                    sp.dma_start(dst[:, :], k.given[src]).then_inc(s_const, 16)
                sp.wait_ge(s_cint, 1)
                sp.dma_start(k.d_quant, cint[:, :]).then_inc(s_qout, 16)
                sp.wait_ge(s_qout, 16)
                for b in range(B):
                    for a in range(3):
                        sp.dma_start(X[16 * b:16 * b + 16, a, 0, :],
                                     k.d_quant[3 * b + a].rearrange("(g e) -> g e", e=64)).then_inc(s_qin, 16)
                sp.wait_ge(s_keyf, 1)
                for b in range(B):
                    for h in range(2):
                        sp.dma_start(k.d_key[h, b].rearrange("m (g e) -> g m e", e=64),
                                     keyf[16 * b:16 * b + 16, h, :, :]).then_inc(s_kout, 16)
                sp.wait_ge(s_kout, 16 * 2 * B)
                sp.wait_ge(s_const, 16 * 3)

            @block.tensor
            def _(pe):
                products(pe)

            @block.gpsimd
            def _(pool):
                pool.iota(point[:, :], pattern=[[1, 64]], base=0, channel_multiplier=64).then_inc(s_point, 1)
                pool.memset(epsc[:, :], EPS).then_inc(s_eps, 1)
                pool.wait_ge(s_rstd, 1)
                for b in range(B):
                    pool.tensor_scalar(k.F[0:C, b, :], xs[:, b, :], xmv[:, b, 0:1], xrstd[:, b:b + 1],
                                       ALU.subtract, ALU.mult)

            @block.scalar
            def _(act):
                act.wait_ge(s_var, 1)
                act.wait_ge(s_eps, 1)
                act.activation(xstd[:, :], xmv[:, :, 1], ACT.Sqrt, bias=epsc[0:C, :]).then_inc(s_std, 1)
                copies(act)

            @block.vector
            def _(v):
                ch = Counted(v, s_chain)

                def ts(out, a, s1, s2, o1, o2=ALU.bypass):
                    ch.then(v.tensor_scalar(out, a, s1, s2, o1, o2) if s2 is not None
                            else v.tensor_scalar(out, a, s1, None, o1))

                def tt(out, a, b_, op):
                    ch.then(v.tensor_tensor(out, a, b_, op))

                v.wait_ge(s_co, 16)
                ch.then(v.tensor_reduce(col[:, 0:1], co[:, :], AX.X, ALU.min))
                ch.then(v.tensor_reduce(col[:, 1:2], co[:, :], AX.X, ALU.max))
                tt(col[:, 2:3], col[:, 1:2], col[:, 0:1], ALU.subtract)
                ts(col[:, 3:4], col[:, 2:3], 1e-6, None, ALU.add)
                ch.then(v.reciprocal(col[:, 4:5], col[:, 3:4]))
                ts(col[:, 5:6], col[:, 4:5], 1023.0, None, ALU.mult)
                for src, hi, lo in ((3, 6, 7), (5, 8, 9)):
                    ts(coli[:, hi:hi + 1], coli[:, src:src + 1], -4096, None, ALU.bitwise_and)
                    tt(col[:, lo:lo + 1], col[:, src:src + 1], col[:, hi:hi + 1], ALU.subtract)
                tt(col[:, 10:11], col[:, 6:7], col[:, 8:9], ALU.mult)
                ts(col[:, 11:12], col[:, 10:11], -1.0, 1023.0, ALU.mult, ALU.add)
                for a, b_ in ((6, 9), (7, 8), (7, 9)):
                    tt(col[:, 10:11], col[:, a:a + 1], col[:, b_:b_ + 1], ALU.mult)
                    tt(col[:, 11:12], col[:, 11:12], col[:, 10:11], ALU.subtract)
                tt(col[:, 10:11], col[:, 11:12], col[:, 4:5], ALU.mult)
                tt(col[:, 12:13], col[:, 5:6], col[:, 10:11], ALU.add)
                ts(cq[:, :], co[:, :], col[:, 0:1], col[:, 12:13], ALU.subtract, ALU.mult)
                ch.then(v.tensor_copy(cint[:, :], cq[:, :]))
                ch.then(v.tensor_copy(cfl[:, :], cint[:, :]))
                tt(cq[:, :], cfl[:, :], cq[:, :], ALU.is_gt)
                tt(cfl[:, :], cfl[:, :], cq[:, :], ALU.subtract)
                ts(cfl[:, :], cfl[:, :], 0.0, 1023.0, ALU.max, ALU.min)
                ch.then(v.tensor_copy(cint[:, :], cfl[:, :]))
                v.sem_inc(s_cint, 1)

                v.wait_ge(s_x, 16)
                for b in range(B):
                    for h in range(2):
                        ch.inc(v.bn_stats(xstat[:, b, h, :], xs[:, b, 512 * h:512 * h + 512]))
                v.wait_ge(s_chain, ch.n)
                for b in range(B):
                    ch.inc(v.bn_aggr(xmv[:, b, :], xstat[:, b, :, :]))
                v.wait_ge(s_chain, ch.n)
                v.sem_inc(s_var, 1)

                v.wait_ge(s_std, 1)
                v.reciprocal(xrstd[:, :], xstd[:, :]).then_inc(s_rstd, 1)

                v.wait_ge(s_qin, 16 * 3 * B)
                for a, b_ in ((0, 1), (1, 0), (2, 2)):
                    ch.inc(v.tensor_copy(X[:, b_, 1, :], X[:, a, 0, :]))
                for a in range(3):
                    ch.inc(v.tensor_copy(X[:, a, 2, :], X[:, a, 0, :]))
                for a, b_ in ((0, 1), (1, 0), (2, 2)):
                    ch.inc(v.tensor_copy(X[:, b_, 3, :], X[:, a, 0, :]))
                v.wait_ge(s_chain, ch.n)

                H = [X[:, a, 2:4, :] for a in range(3)]
                t, u = mask[:, :, :], flip[:, :, :]
                for bit in range(9, 0, -1):
                    low = (1 << bit) - 1
                    ts(t, H[0], 31 - bit, 31, ALU.logical_shift_left, ALU.arith_shift_right)
                    ch.then(v.scalar_tensor_tensor(H[0], t, low, H[0], ALU.bitwise_and, ALU.bitwise_xor))
                    for a in (1, 2):
                        ch.inc(v.tensor_scalar(t, H[a], 31 - bit, 31, ALU.logical_shift_left, ALU.arith_shift_right))
                        tt(u, H[0], H[a], ALU.bitwise_xor)
                        tt(u, u, t, ALU.bitwise_or)
                        ch.inc(v.scalar_tensor_tensor(H[0], u, low, H[0], ALU.bitwise_and, ALU.bitwise_xor))
                        tt(t, u, t, ALU.bitwise_xor)
                        ch.then(v.scalar_tensor_tensor(H[a], t, low, H[a], ALU.bitwise_and, ALU.bitwise_xor))
                tt(H[1], H[1], H[0], ALU.bitwise_xor)
                tt(H[2], H[2], H[1], ALU.bitwise_xor)
                ts(u, H[2], 0, None, ALU.bitwise_and)
                for bit in range(9, 0, -1):
                    ts(t, H[2], 31 - bit, 31, ALU.logical_shift_left, ALU.arith_shift_right)
                    ch.then(v.scalar_tensor_tensor(u, t, (1 << bit) - 1, u, ALU.bitwise_and, ALU.bitwise_xor))
                for a in range(3):
                    ch.inc(v.tensor_tensor(H[a], H[a], u, ALU.bitwise_xor))
                v.wait_ge(s_chain, ch.n)

                Xf = X[:, :, :, :].rearrange("p a m e -> p (a m e)")
                Tf = T[:, :, :, :].rearrange("p a m e -> p (a m e)")
                for shift, keep in ((16, 0x030000FF), (8, 0x0300F00F), (4, 0x030C30C3), (2, 0x09249249)):
                    ch.then(v.scalar_tensor_tensor(Tf, Xf, shift, Xf, ALU.logical_shift_left, ALU.bitwise_or))
                    ts(Xf, Tf, keep, None, ALU.bitwise_and)
                S = [X[:, a, :, :] for a in range(3)]
                ch.then(v.scalar_tensor_tensor(T[:, 0, :, :], S[1], 1, S[2], ALU.logical_shift_left, ALU.bitwise_or))
                ch.then(v.scalar_tensor_tensor(T[:, 1, :, :], S[0], 2, T[:, 0, :, :],
                                               ALU.logical_shift_left, ALU.bitwise_or))
                K = T[:, 1, :, :]
                ts(key[:, 0, :, :], K, 6, None, ALU.logical_shift_right)
                ch.then(v.tensor_copy(keyf[:, 0, :, :], key[:, 0, :, :]))
                ts(key[:, 1, :, :], K, 63, 10, ALU.bitwise_and, ALU.logical_shift_left)
                v.wait_ge(s_point, 1)
                ts(point[:, :], point[:, :], N - 1, None, ALU.bitwise_and)
                for m in range(M):
                    ch.inc(v.tensor_tensor(key[:, 1, m, :], key[:, 1, m, :], point[:, :], ALU.bitwise_or))
                v.wait_ge(s_chain, ch.n)
                ch.inc(v.tensor_copy(keyf[:, 1, :, :], key[:, 1, :, :]))
                ts(keyf[:, 0, :, :], keyf[:, 0, :, :], 65536.0, None, ALU.mult)
                v.sem_inc(s_keyf, 1)
                rests(v)


def curve_ranks(k):
    nc = k.nc
    R = B * M
    RING = 4
    with ExitStack() as ctx:
        sb, ps, sem = placing(k, ctx)
        rows = sb("rows", [R, 2, N], F32)
        own = sb("own", [P, 2, R, NB], F32)
        wide = sb("wide", [P, RING, 2, N], F32)
        cmp = sb("cmp", [P, 4, N], F32)
        sign = sb("sign", [P, 2, NB, N], BF16)
        ones = sb("ones", [P, 1], BF16)
        total = sb("total", [P, R, NB], F32)
        psT = ps("psT", [P, 2, NB, R], F32)
        psL = ps("psL", [P, R, NB], F32)
        s_rows = sem("s_rows")
        s_t = sem("s_t")
        s_own = sem("s_own")
        s_wide = [sem(f"s_wide{i}") for i in range(RING)]
        s_cmp = sem("s_cmp")
        s_sign = sem("s_sign")
        s_ones = sem("s_ones")
        s_later = sem("s_later")
        s_tot = sem("s_tot")

        with nc.Block() as block:
            @block.sync
            def _(sp):
                keyw = k.d_key.rearrange("h b m n -> (b m) h n")
                sp.dma_start(rows[:, :, :], keyw).then_inc(s_rows, 16)

                def load(r, i):
                    at = keyw[bass.ds(r, 1), 0:1, 0:1]
                    sp.dma_start(wide[:, i, :, :], bass.AP(tensor=at.tensor, offset=at.offset,
                                                           ap=[[0, P], [R * N, 2], [1, N]])).then_inc(s_wide[i], 16)

                for i in range(RING):
                    load(i, i)
                with sp.Fori(0, R // RING - 1) as t:
                    for i in range(RING):
                        sp.wait_ge(s_cmp, (t * RING + i + 1) * NB)
                        load(t * RING + (RING + i), i)

            @block.gpsimd
            def _(pool):
                pool.memset(ones[:, :], 1.0).then_inc(s_ones, 1)

            @block.tensor
            def _(pe):
                pe.wait_ge(s_rows, 16)
                for h in range(2):
                    for n in range(NB):
                        last = pe.transpose(psT[:, h, n, :], rows[:, h, n * P:(n + 1) * P], k.id32[0:R, 0:R])
                last.then_inc(s_t, 1)
                pe.wait_ge(s_ones, 1)
                pe.sem_inc(s_later, 2)
                later = psL[:, :, :].rearrange("p r n -> p (r n)")
                with pe.Fori(0, R // 2) as t:
                    for u in range(2):
                        r = 2 * t + u
                        pe.wait_ge(s_sign, (r + 1) * NB)
                        for q in range(1, NB):
                            for n in range(q):
                                last = pe.matmul(later[:, bass.ds(r * NB + q, 1)], sign[:, u, n, q * P:(q + 1) * P],
                                                 ones[:, :], start=(n == 0), stop=(n == q - 1))
                        last.then_inc(s_later, 1)

            @block.vector
            def _(v):
                v.wait_ge(s_t, 1)
                v.tensor_copy(own[:, 0, :, :], psT[:, 0, :, :].rearrange("p n r -> p r n")).then_inc(s_own, 1)
                v.tensor_scalar(own[:, 1, :, :], psT[:, 1, :, :].rearrange("p n r -> p r n"), -1.0, None,
                                ALU.mult).then_inc(s_own, 1)
                v.wait_ge(s_own, 2)
                own0 = own[:, 0, :, :].rearrange("p r n -> p (r n)")

                def compare(r, i, n, wait):
                    if wait is not None:
                        v.wait_ge(s_sign, wait)
                    v.scalar_tensor_tensor(cmp[:, n % 4, n * P:N], wide[:, i, 0, n * P:N],
                                           own0[:, bass.ds(r * NB + n, 1)], wide[:, i, 1, n * P:N],
                                           ALU.subtract, ALU.add).then_inc(s_cmp, 1)

                for i in range(RING):
                    v.wait_ge(s_wide[i], 16)
                    for n in range(NB):
                        at = i * NB + n
                        compare(i, i, n, at - 3 if at >= 4 else None)
                with v.Fori(1, R // RING) as t:
                    for i in range(RING):
                        v.wait_ge(s_wide[i], 16 * t + 16)
                        for n in range(NB):
                            compare(t * RING + i, i, n, t * (RING * NB) + (i * NB + n - 3))
                v.wait_ge(s_sign, R * NB)
                v.wait_ge(s_later, R + 2)
                v.tensor_tensor(total[:, :, 1:NB], total[:, :, 1:NB], psL[:, :, 1:NB], ALU.subtract
                                ).then_inc(s_tot, 1)
                v.wait_ge(s_tot, 1)
                v.tensor_scalar(k.rank[:, :, :], total[:, :, :], -0.5, (N - 1) / 2, ALU.mult, ALU.add)

            @block.scalar
            def _(act):
                act.wait_ge(s_own, 2)
                own1 = own[:, 1, :, :].rearrange("p r n -> p (r n)")
                tot = total[:, :, :].rearrange("p r n -> p (r n)")
                with act.Fori(0, R // 2) as t:
                    for u in range(2):
                        r = 2 * t + u
                        act.wait_ge(s_later, r + 1)
                        for n in range(NB):
                            act.wait_ge(s_cmp, r * NB + (n + 1))
                            act.activation(sign[:, u, n, n * P:N], cmp[:, n % 4, n * P:N], ACT.Sign,
                                           bias=own1[:, bass.ds(r * NB + n, 1)],
                                           accum_out=tot[:, bass.ds(r * NB + n, 1)]).then_inc(s_sign, 1)


def split_features(k, src, centre, wd, O, norm):
    nc = k.nc
    with ExitStack() as ctx:
        sb, ps, sem = placing(k, ctx)
        hi = sb("hi", [C, B, N], F16)
        lo = sb("lo", [C, B, N], F16)
        both = sb("both", [C, 2, N], F32)
        psF = [ps(f"psF{i}", [P, NB, P], F16) for i in range(2)]
        psC = [ps(f"psC{i}", [P, NB * O]) for i in range(2)]
        s_hi = sem("s_hi")
        s_lo = sem("s_lo")
        s_both = sem("s_both")
        s_dump = [sem("s_dump0"), sem("s_dump1")]
        s_turn = sem("s_turn")
        s_fT = sem("s_fT")
        s_c = sem("s_c")
        s_chi = sem("s_chi")
        s_clo = sem("s_clo")
        s_join = sem("s_join")

        if norm:
            roots, normalize, s_norm = instance_norm(k, sb, sem, src, *norm, C)

        def part(b, h):
            return centre[:, b * NB:(b + 1) * NB, h, :]

        def sums(b):
            return psC[b % 2][:, :].rearrange("p (n o) -> p n o", o=O)

        with nc.Block() as block:
            @block.scalar
            def _(act):
                def high(b):
                    act.wait_ge(s_c, b + 1)
                    act.mul(part(b, 0), sums(b), 1 / WSCALE).then_inc(s_chi, 1)

                if norm:
                    roots(act)
                for b in range(B):
                    if norm:
                        act.wait_ge(s_norm, b + 1)
                    act.copy(hi[:, b, :], src[0:C, b, :]).then_inc(s_hi, 1)
                    if b >= 2:
                        high(b - 2)
                for b in range(B - 2, B):
                    high(b)

            @block.vector
            def _(v):
                def turned(b):
                    v.wait_ge(s_turn, b + 1)
                    v.tensor_copy(k.fT[:, b, :, :], psF[b % 2][:, :, :]).then_inc(s_fT, 1)

                def rest(b):
                    v.wait_ge(s_chi, b + 1)
                    v.scalar_tensor_tensor(part(b, 1), sums(b), 1 / WSCALE, part(b, 0), ALU.mult, ALU.subtract
                                           ).then_inc(s_clo, 1)

                if norm:
                    normalize(v)
                for b in range(B):
                    v.wait_ge(s_hi, b + 1)
                    v.tensor_tensor(lo[:, b, :], src[0:C, b, :], hi[:, b, :], ALU.subtract).then_inc(s_lo, 1)
                    if b >= 1:
                        turned(b - 1)
                    if b >= 2:
                        rest(b - 2)
                turned(B - 1)
                for b in range(B - 2, B):
                    rest(b)

            @block.gpsimd
            def _(pool):
                for b in range(B):
                    pool.wait_ge(s_lo, b + 1)
                    if b >= 2:
                        pool.wait_ge(s_dump[b % 2], 16 * (b // 2))
                    pool.tensor_tensor(both[:, b % 2, :], hi[:, b, :], lo[:, b, :], ALU.add).then_inc(s_both, 1)

            @block.sync
            def _(sp):
                for b in range(B):
                    sp.wait_ge(s_both, b + 1)
                    sp.dma_start(k.d_f[b], both[:, b % 2, :]).then_inc(s_dump[b % 2], 16)
                if norm:
                    sp.dma_start(k.F[C:P, :, :], src[0:C, :, :]).then_inc(s_join, 16)
                    sp.wait_ge(s_join, 16)
                for u in range(2):
                    sp.wait_ge(s_dump[u], 16 * (B // 2))

            @block.tensor
            def _(pe):
                for b in range(B):
                    pe.wait_ge(s_lo, b + 1)
                    if b >= 2:
                        pe.wait_ge(s_fT, b - 1)
                    for n in range(NB):
                        for h, x in enumerate((hi, lo)):
                            last = pe.transpose(psF[b % 2][:, n, C * h:C * h + C], x[:, b, n * P:(n + 1) * P],
                                                k.id16[0:C, 0:C])
                    last.then_inc(s_turn, 1)
                    if b >= 2:
                        pe.wait_ge(s_clo, b - 1)
                    for n in range(NB):
                        for q, x in enumerate((hi, hi, lo)):
                            last = pe.matmul(psC[b % 2][:, n * O:(n + 1) * O], x[:, b, n * P:(n + 1) * P],
                                             wd[:, q, :], start=(q == 0), stop=(q == 2))
                    last.then_inc(s_c, 1)


def gather(k, sem, psG, s_copied):
    free = k.M2[:, :, :].rearrange("p b n -> p (b n)").bitcast(F16).rearrange("p (r n) -> p r n", n=N)
    hot, out = free[:, 0:8, :], free[:, 8:8 + M, :]
    s_hot = sem("s_hot")
    s_sent = [sem(f"s_sent{m}") for m in range(M)]
    s_freehot = sem("s_freehot")
    rank = k.rank[:, :, :].rearrange("p r n -> p (r n)")

    def one_hots(v):
        with v.Fori(0, B) as b:
            for j in range(M * NB):
                v.wait_ge(s_freehot, b * (M * NB) + (j + 1))
                v.tensor_scalar(hot[:, j % 8, :], k.ramp[:, :], rank[:, bass.ds(b * (M * NB) + j, 1)], None,
                                ALU.is_equal).then_inc(s_hot, 1)

    def products(pe):
        pe.sem_inc(s_freehot, 8)
        fT = k.fT[:, :, :, :].rearrange("p b n c -> p (b n c)")
        with pe.Fori(0, B) as b:
            for m in range(M):
                pe.wait_ge(s_copied, b * M + (m + 1))
                for n in range(NB):
                    pe.wait_ge(s_hot, b * (M * NB) + (m * NB + n + 1))
                    for h in range(2):
                        last = pe.matmul(psG[m % 2][:, h, :], fT[:, bass.ds(b * (NB * P) + n * P, P)],
                                         hot[:, (m * NB + n) % 8, 512 * h:512 * h + 512],
                                         start=(n == 0), stop=(n == NB - 1))
                    last.then_inc(s_freehot, 1)

    def sends(act):
        act.sem_inc(s_copied, 2)
        for m in range(M):
            act.sem_inc(s_sent[m], 16)
        with act.Fori(0, B) as b:
            for m in range(M):
                act.wait_ge(s_freehot, b * (M * NB) + ((m + 1) * NB + 8))
                act.wait_ge(s_sent[m], b * 16 + 16)
                act.copy(out[:, m, :].rearrange("p (h n) -> p h n", h=2), psG[m % 2][:, :, :]).then_inc(s_copied, 1)
                act.wait_ge(s_copied, b * M + (m + 3))
                act.dma_start(k.d_g[bass.ds(b, 1), :, m, :, :].rearrange("o q c n -> (o q) c n"),
                              out[:, m, :]).then_inc(s_sent[m], 16)
        for m in range(M):
            act.wait_ge(s_sent[m], 16 * B + 16)

    return one_hots, products, sends


G = 6
GP = 11
ROWS = GP * KNN
STEP = 64
WIN = 20
AW = 2 * (P + 2 * GP)
SPAN = STEP + 12
PAD = KNN // 2
GW = N + 16
STEPS = B * N // STEP
HALVES = ((0, 4 * GP), (4 * GP, STEP - 4 * GP))
PER = N // STEP


def edge_layer(k, centre, wn, O, maxh, mv):
    nc = k.nc
    with ExitStack() as ctx:
        sb, ps, sem = placing(k, ctx)
        Gs = sb("Gs", [P, 2, 2, 2, GW], F16)
        none = sb("none", [P, 4], F32)
        fr = sb("fr", [P, 2, 2, N + 2], F32)
        sth = sb("sth", [P, 2, 2, 2, SPAN, 2], F16)
        stu = sb("stu", [P, 2, 2, SPAN], F32)
        d16 = sb("d16", [P, 2, 2, G * GP, KNN], F16)
        mkl = sb("mkl", [3 * GP, ROWS], BF16)
        mkr = sb("mkr", [3 * GP, PER // 2 + 1, G * 2 * WIN], BF16)
        E = sb("E", [ROWS, 2, G * 2, WIN, 2], F32)
        top = sb("top", [ROWS, 2, G * 4], F32)
        tot = sb("tot", [ROWS, 2, G * 4], F32)
        inv = sb("inv", [ROWS, 2, G * 4], F32)
        A = sb("A", [ROWS, 2, 3, AW], F32)
        AT = sb("AT", [P, 2, G * ROWS], F32)
        GWs = sb("GWs", [P, 2, 3, O], F32)
        stat = sb("stat", [O, STEPS, 2, 6], F32)
        psS = [ps(f"psS{i}", [P, 512]) for i in range(2)]
        psW = ps("psW", [P, 512])
        psA = ps("psA", [P, 2, 512])
        psY = ps("psY", [P, 2, 512])

        s_copied = sem("s_copied")
        one_hots, products, sends = gather(k, sem, (psA, psY), s_copied)
        s_w = sem("s_w")
        s_load = [sem("s_load0"), sem("s_load1")]
        s_zero = sem("s_zero")
        s_pool = sem("s_pool")
        s_S = sem("s_S")
        s_sth = sem("s_sth")
        s_dve = sem("s_dve")
        s_sub = sem("s_sub")
        s_exp = sem("s_exp")
        s_A = sem("s_A")
        s_T = sem("s_T")
        s_AT = sem("s_AT")
        s_W = sem("s_W")
        s_GW = sem("s_GW")
        s_Y = sem("s_Y")
        s_Y0 = sem("s_Y0")
        s_done = sem("s_done")
        NLOAD = 4 + 4

        PADS, EDGE, EACH = 1, 5, 3
        BATCH = PADS + EDGE + EACH * PER

        def staged(n):
            return n // PER * BATCH + n % PER * EACH + (PADS + EDGE + EACH)

        with nc.Block() as block:
            @block.sync
            def _(sp):
                def load(b, u):
                    for hl in range(2):
                        for c in range(2):
                            at = 4 * hl + 2 * c
                            sp.dma_start(Gs[:, u, hl, c, PAD:PAD + N],
                                         k.d_g[bass.ds(b, 1), at:at + 2].rearrange("o h m c n -> (o h m c) n")
                                         ).then_inc(s_load[u], 16)
                    flat = k.d_f.rearrange("b c n -> (b c) n")
                    for c in range(2):
                        for h in range(2):
                            at = flat[bass.ds(b * C + (32 * c + 16 * h), 16), :]
                            sp.dma_start(fr[64 * h:64 * h + 64, u, c, 0:N],
                                         bass.AP(tensor=at.tensor, offset=at.offset, ap=[[0, M], [N, 16], [1, N]])
                                         ).then_inc(s_load[u], 16)

                sp.wait_ge(s_zero, 5)
                sp.wait_ge(s_copied, 2 + 2 * M)
                load(0, 0)
                sp.dma_start(mkl[:, :], k.given["c_mkl"]).then_inc(s_w, 16)
                sp.dma_start(mkr[:, :, :], k.given["c_mkr"]).then_inc(s_w, 16)
                sp.wait_ge(s_copied, 2 + 3 * M)
                load(1, 1)
                with sp.Fori(1, B // 2) as t:
                    for u in range(2):
                        sp.wait_ge(s_sth, t * (4 * PER) + (u - 1) * (2 * PER))
                        sp.wait_ge(s_pool, t * (2 * BATCH) + (u - 1) * BATCH)
                        load(2 * t + u, u)

            @block.gpsimd
            def _(pool):
                pool.memset(A[:, :, :, :], 0.0).then_inc(s_zero, 1)
                pool.memset(Gs[:, :, :, :, 0:PAD], 0.0).then_inc(s_zero, 1)
                pool.memset(sth[:, :, :, :, :, :], 0.0).then_inc(s_zero, 1)
                pool.memset(none[:, :], 0.0).then_inc(s_zero, 1)
                pool.memset(fr[:, :, :, N:N + 2], 0.0).then_inc(s_zero, 1)
                pool.wait_ge(s_zero, 5)

                def stage(b, par, s, u, first):
                    n = b * PER + s
                    ch = Counted(pool, s_pool, b * BATCH + s * EACH + (PADS if first else PADS + EDGE))
                    w = s * STEP
                    at = bass.ds(w, SPAN)
                    ch.then(pool.tensor_tensor(stu[:, u, :, :], Gs[:, par, 0, :, at], Gs[:, par, 1, :, at], ALU.add))
                    pool.wait_ge(s_S, n + 1)
                    for c in range(2):
                        g = stu[:, u, c, :]
                        win = bass.AP(tensor=g.tensor, offset=g.offset, ap=[list(g.ap[0]), [1, G * GP], [1, KNN]])
                        ch.inc(pool.tensor_tensor(
                            d16[:, u, c, :, :], win,
                            fr[:, par, c, bass.ds(w, G * GP)].unsqueeze(2).to_broadcast([P, G * GP, KNN]),
                            ALU.subtract))
                    if first:
                        pool.wait_ge(s_pool, ch.start + ch.n)
                        for i in range(EDGE):
                            ch.inc(pool.tensor_tensor(
                                d16[:, u, :, i, 0:PAD - i],
                                stu[:, u, :, i + 2 * PAD:i + 2 * PAD + 1].to_broadcast([P, 2, PAD - i]),
                                fr[:, par, :, i:i + 1].to_broadcast([P, 2, PAD - i]), ALU.subtract))

                with pool.Fori(0, B // 2) as t:
                    for par in range(2):
                        b = 2 * t + par
                        pool.wait_ge(s_load[par], t * (16 * NLOAD) + 16 * NLOAD)
                        edge = Gs[:, par, :, :, :].rearrange("p q c n -> p (q c) n")
                        pool.tensor_tensor(edge[:, :, PAD + N:GW],
                                           edge[:, :, PAD + N - 1:PAD + N].to_broadcast([P, 4, GW - PAD - N]),
                                           none[:, :].unsqueeze(2).to_broadcast([P, 4, GW - PAD - N]),
                                           ALU.add).then_inc(s_pool, 1)
                        pool.wait_ge(s_pool, b * BATCH + PADS)
                        stage(b, par, 0, 0, True)
                        stage(b, par, 1, 1, False)
                        with pool.Fori(1, PER // 2) as q:
                            for u in range(2):
                                stage(b, par, 2 * q + u, u, False)

            @block.tensor
            def _(pe):
                pe.sem_inc(s_S, 2)
                products(pe)
                pe.wait_ge(s_copied, B * M + 2)
                pe.wait_ge(s_w, 16 * 2)
                pe.sem_inc(s_W, 2)
                pe.sem_inc(s_Y, 2)

                mk = mkr[:, :, :].rearrange("k v n -> k (v n)")
                cf = centre[:, :, :, :].rearrange("p b h o -> p (b h o)")
                NS = G * 2 * WIN

                def scores(n, u, first):
                    pe.wait_ge(s_pool, staged(n))
                    pe.wait_ge(s_sth, 2 * (n + 1))
                    if not first:
                        pe.wait_ge(s_sub, n - 1)
                    at = (n // 2) % (PER // 2) * NS + u * NS
                    pe.matmul(psS[u][0:ROWS, 0:2 * NS].rearrange("p (g c n) -> p g c n", g=G, c=2), mkl[:, :],
                              mk[:, bass.ds(at, NS)].rearrange("k (g n) -> k g n", g=G).unsqueeze(2)
                              .to_broadcast([3 * GP, G, 2, 2 * WIN]), start=True, stop=False)
                    for g in range(G):
                        for c in range(2):
                            for hl in range(2):
                                last = pe.matmul(psS[u][0:ROWS, 80 * g + 40 * c:80 * g + 40 * c + 40],
                                                 d16[:, u, c, GP * g:GP * g + GP, :],
                                                 sth[:, u, hl, c, GP * g:GP * g + WIN, :],
                                                 start=False, stop=(g == G - 1 and c == 1 and hl == 1))
                    last.then_inc(s_S, 1)

                def turn(n, u, first):
                    pe.wait_ge(s_A, n + 1)
                    if not first:
                        pe.wait_ge(s_AT, n)
                    for g in range(G):
                        last = pe.transpose(psA[:, g // 3, ROWS * (g % 3):ROWS * (g % 3) + ROWS],
                                            A[:, u, g // 2, P * (g % 2):P * (g % 2) + P], k.id32[0:ROWS, 0:ROWS])
                    last.then_inc(s_T, 1)

                def windows(n, u, first):
                    if not first:
                        pe.wait_ge(s_GW, n)
                    for w in range(3):
                        for c in range(2):
                            for q, (x, y) in enumerate(((0, 0), (0, 1), (1, 0))):
                                last = pe.matmul(psW[64 * c:64 * c + 64, O * w:O * w + O],
                                                 sth[:, u, x, c, 2 * GP * w:2 * GP * w + 32, :],
                                                 wn[:, y, c, :], start=(q == 0), stop=(q == 2))
                    last.then_inc(s_W, 1)

                def sums(n, u, first):
                    pe.wait_ge(s_AT, n + 1)
                    pe.wait_ge(s_GW, n + 1)
                    for j, (p0, pn) in enumerate(HALVES):
                        if not first:
                            pe.wait_ge(s_done, 4 * n + (2 * j - 2))
                        for w in ((0, 1), (2,))[j]:
                            cols = (2 * GP if w < 2 else STEP - 4 * GP) * KNN
                            at = 2 * ROWS * w if w < 2 else 0
                            pe.matmul(psY[0:O, j, at:at + cols], GWs[:, u, w, :],
                                      AT[:, u, 2 * ROWS * w:2 * ROWS * w + cols], start=(w != 1), stop=False)
                        for hl in range(2):
                            last = pe.matmul(psY[0:O, j, 0:pn * KNN], cf[:, bass.ds(n // 2 * (2 * O) + hl * O, O)],
                                             k.id16[:, STEP * u + p0:STEP * u + p0 + pn].unsqueeze(2)
                                             .to_broadcast([P, pn, KNN]), start=False, stop=(hl == 1))
                        last.then_inc((s_Y0, s_Y)[j], 1)

                scores(0, 0, True)
                windows(0, 0, True)
                scores(1, 1, True)
                turn(0, 0, True)
                windows(1, 1, False)
                scores(2, 0, False)
                sums(0, 0, True)
                with pe.Fori(1, STEPS // 2 - 1) as t:
                    for u in range(2):
                        n = 2 * t + u
                        turn(n - 1, 1 - u, False)
                        windows(n, u, False)
                        scores(n + 1, 1 - u, False)
                        sums(n - 1, 1 - u, False)
                turn(STEPS - 3, 1, False)
                windows(STEPS - 2, 0, False)
                scores(STEPS - 1, 1, False)
                sums(STEPS - 3, 1, False)
                turn(STEPS - 2, 0, False)
                windows(STEPS - 1, 1, False)
                sums(STEPS - 2, 0, False)
                turn(STEPS - 1, 1, False)
                sums(STEPS - 1, 1, False)

            @block.scalar
            def _(act):
                sends(act)
                Gf = Gs[:, :, :, :, :].rearrange("p b q c n -> p (b q c) n")
                act.wait_ge(s_zero, 5)

                def windows(n, u):
                    act.wait_ge(s_W, n + 1)
                    act.wait_ge(s_pool, n // PER * BATCH + PADS)
                    for h in range(2):
                        r = slice(64 * h, 64 * h + 64)
                        act.copy(sth[r, u, :, :, :, h].rearrange("p q c n -> p (q c) n"),
                                 Gf[r, bass.ds(n // PER % 2 * 4, 4), bass.ds(n % PER * STEP, SPAN)]
                                 ).then_inc(s_sth, 1)

                def turned(n, u):
                    act.wait_ge(s_T, n + 1)
                    act.wait_ge(s_Y, n + 1)
                    act.copy(AT[:, u, :].rearrange("p (j n) -> p j n", j=2), psA[:, :, 0:3 * ROWS]).then_inc(s_AT, 1)

                def exps(n, u):
                    act.wait_ge(s_sub, n + 1)
                    act.activation(E[:, u, :, :], E[:, u, :, :], ACT.Exp, scale=0.125).then_inc(s_exp, 1)

                def evacuate(n, u):
                    act.wait_ge(s_W, n + 3)
                    act.wait_ge(s_Y, n + 1)
                    act.mul(GWs[:, u, :, :], psW[:, 0:3 * O].rearrange("p (w o) -> p w o", w=3), 1 / WSCALE
                            ).then_inc(s_GW, 1)

                windows(0, 0)
                windows(1, 1)
                exps(0, 0)
                evacuate(0, 0)
                windows(2, 0)
                turned(0, 0)
                exps(1, 1)
                evacuate(1, 1)
                windows(3, 1)
                with act.Fori(1, STEPS // 2 - 1) as t:
                    for u in range(2):
                        n = 2 * t + u
                        turned(n - 1, 1 - u)
                        exps(n, u)
                        evacuate(n, u)
                        windows(n + 2, u)
                for n in (STEPS - 2, STEPS - 1):
                    turned(n - 1, (n - 1) % 2)
                    exps(n, n % 2)
                    evacuate(n, n % 2)
                turned(STEPS - 1, 1)

            @block.vector
            def _(v):
                one_hots(v)
                v.wait_ge(s_zero, 5)
                EV = 3
                mh = maxh.rearrange("o b n -> o (b n)")

                def maxima(n, u):
                    v.wait_ge(s_S, n + 3)
                    m = top[:, u, :].rearrange("p (g h) -> p g h", h=2)
                    v.tensor_reduce(m, score_view(u), AX.X, ALU.max).then_inc(s_dve, 1)

                def subtract(n, u):
                    v.wait_ge(s_dve, n * EV + 1)
                    m = top[:, u, :].rearrange("p (g h) -> p g h", h=2)
                    v.tensor_tensor(E[:, u, :, :, :].rearrange("p g n h -> p g h n"), score_view(u),
                                    m.unsqueeze(3).to_broadcast([ROWS, G * 2, 2, WIN]), ALU.subtract
                                    ).then_inc(s_sub, 1)

                def statistics(n, j):
                    if j == 0:
                        v.wait_ge(s_Y0, n + 1)
                    else:
                        v.wait_ge(s_Y, n + 3)
                    v.bn_stats(stat[:, bass.ds(n, 1), j, :], psY[0:O, j, 0:HALVES[j][1] * KNN]).then_inc(s_done, 1)

                def largest(n, j):
                    p0, pn = HALVES[j]
                    v.tensor_reduce(mh[:, bass.ds(n * STEP + p0, pn)],
                                    psY[0:O, j, 0:pn * KNN].rearrange("o (i a) -> o i a", a=KNN),
                                    AX.X, ALU.max).then_inc(s_done, 1)

                def total(n, u):
                    v.wait_ge(s_exp, n + 1)
                    v.tensor_reduce(tot[:, u, :].rearrange("p (g h) -> p g h", h=2),
                                    E[:, u, :, :, :].rearrange("p g n h -> p g h n"), AX.X, ALU.add).then_inc(s_dve, 1)

                def invert(n, u):
                    v.wait_ge(s_dve, n * EV + 2)
                    v.reciprocal(inv[:, u, :], tot[:, u, :]).then_inc(s_dve, 1)

                def weights(n, u, first):
                    v.wait_ge(s_dve, n * EV + 3)
                    if not first:
                        v.wait_ge(s_T, n - 1)
                    a = A[:, u, :, :]
                    out = bass.AP(tensor=a.tensor, offset=a.offset,
                                  ap=[list(a.ap[0]), [AW // 2, G], [P // 2, 2], [1, 2 * WIN]])
                    r = inv[:, u, :]
                    r = bass.AP(tensor=r.tensor, offset=r.offset,
                                ap=[list(r.ap[0]), [2, G * 2], [0, WIN], [1, 2]])
                    v.tensor_tensor(out, E[:, u, :, :, :].rearrange("p g n h -> p (g n h)"), r,
                                    ALU.mult).then_inc(s_A, 1)

                def score_view(u):
                    return psS[u][0:ROWS, 0:G * 4 * WIN].rearrange("p (g n h) -> p g h n", n=WIN, h=2)

                for n in range(2):
                    maxima(n, n)
                    subtract(n, n)
                    total(n, n)
                    invert(n, n)
                    weights(n, n, True)
                with v.Fori(1, STEPS // 2) as t:
                    for u in range(2):
                        n = 2 * t + u
                        maxima(n, u)
                        statistics(n - 2, 0)
                        subtract(n, u)
                        largest(n - 2, 0)
                        statistics(n - 2, 1)
                        total(n, u)
                        largest(n - 2, 1)
                        invert(n, u)
                        weights(n, u, False)
                for n in range(STEPS - 2, STEPS):
                    for j in range(2):
                        statistics(n, j)
                        largest(n, j)
                v.wait_ge(s_done, 4 * STEPS)
                for b in range(B):
                    v.bn_aggr(mv[0:O, b, :], stat[:, PER * b:PER * b + PER, :, :].rearrange("o n j e -> o (n j e)"))


def instance_norm(k, sb, sem, x, mv, hb, O):
    var = sb("var", [P, B])
    std = sb("std", [P, B])
    r = sb("r", [P, B])
    r2 = sb("r2", [P, B])
    shift = sb("shift", [P, B])
    s_var = sem("s_var")
    s_std = sem("s_std")
    s_nchain = sem("s_nchain")
    s_norm = sem("s_norm")

    def roots(act):
        act.wait_ge(s_var, 1)
        act.activation(std[0:O, :], var[0:O, :], ACT.Sqrt).then_inc(s_std, 1)

    def normalize(v):
        ch = Counted(v, s_nchain)
        v.tensor_scalar(var[0:O, :], mv[0:O, :, 1], EPS, None, ALU.add).then_inc(s_var, 1)
        mean = mv[0:O, :, 0]
        if hb is not None:
            ch.then(v.tensor_scalar(shift[0:O, :], mean, hb[0:O, :], hb[0:O, :], ALU.add, ALU.subtract))
            mean = shift[0:O, :]
        v.wait_ge(s_std, 1)
        v.wait_ge(s_var, 1)
        rsqrt(ch, v, r[0:O, :], r2[0:O, :], std[0:O, :], var[0:O, :])
        start = ch.n
        for b in range(B + 1):
            if b < B:
                ch.inc(v.tensor_scalar(x[0:O, b, :], x[0:O, b, :], mean[:, b:b + 1], r[0:O, b:b + 1],
                                       ALU.subtract, ALU.mult))
            if b >= 1:
                v.wait_ge(s_nchain, start + b)
                v.scalar_tensor_tensor(x[0:O, b - 1, :], x[0:O, b - 1, :], 0.2, x[0:O, b - 1, :], ALU.mult, ALU.max
                                       ).then_inc(s_norm, 1)

    return roots, normalize, s_norm


def rsqrt(ch, v, r, t, std, var):
    ch.then(v.reciprocal(r, std))
    ch.then(v.tensor_tensor(t, r, r, ALU.mult))
    ch.then(v.tensor_tensor(t, t, var, ALU.mult))
    ch.then(v.tensor_scalar(t, t, -0.5, 1.5, ALU.mult, ALU.add))
    ch.then(v.tensor_tensor(r, r, t, ALU.mult))


def neighbour_counts(i):
    start, end = max(0, i - KNN // 2), min(N, i + KNN // 2 + 1)
    pos = [min(start + a, end - 1) for a in range(KNN)]
    return {p: pos.count(p) for p in pos}


def split_bf16(a):
    parts = []
    for _ in range(3):
        part = a.astype(NP_BF16)
        parts.append(part)
        a = a - part.astype(np.float32)
    return parts


def window_masks():
    pick = np.kron(np.eye(GP, dtype=np.float32), np.ones((1, KNN), np.float32))
    bias = np.full((GP, PER // 2 + 1, G, WIN, 2), -2.0 ** 30, np.float32)
    for kind, s in enumerate([0] + [1] * (PER // 2 - 1) + [PER - 1]):
        for g in range(G):
            for r in range(GP):
                i = s * STEP + GP * g + r
                count = neighbour_counts(i) if i < N else {p: 1 for p in range(i - 5, N)}
                for p, c in count.items():
                    bias[r, kind, g, p - (s * STEP + GP * g - PAD), :] = 8 * np.log(np.float32(c))
    bias = bias.reshape(GP, -1)
    return (np.concatenate(split_bf16(pick)[:1] * 3),
            np.concatenate(split_bf16(bias)).reshape(3 * GP, PER // 2 + 1, -1))


def lin_layouts(w, perm):
    w = np.asarray(w)
    cols = [((64 + 32 * c + 16 * h + x) * M + perm.index(m)) for c in range(2) for h in range(2)
            for m in range(M) for x in range(16)]
    return np.ascontiguousarray(w), np.ascontiguousarray(w[:, cols])


def points_out(k, mv, hb):
    nc = k.nc
    with ExitStack() as ctx:
        sb, ps, sem = placing(k, ctx)
        w3 = sb("w3", [P, 2, C])
        x3 = sb("x3", [C, B, N])
        xin = sb("xin", [C, B, N])
        st = sb("st", [C, B, 2, 6])
        mv3 = sb("mv3", [C, B, 2])
        psH = [ps(f"psH{i}", [P, 2, 512]) for i in range(4)]
        s_w3 = sem("s_w3")
        s_xin = sem("s_xin")
        s_h = sem("s_h")
        s_ev = sem("s_ev")
        s_st = sem("s_st")
        s_mv = sem("s_mv")
        s_add = sem("s_add")
        s_x1 = sem("s_x1")
        roots2, normalize2, s_norm2 = instance_norm(k, sb, sem, k.M2, mv, hb, 2 * C)
        sb3, _, sem3 = placing(k, ctx)
        roots3, normalize3, s_norm3 = instance_norm(k, sb3, sem3, x3, mv3, None, C)

        with nc.Block() as block:
            @block.sync
            def _(sp):
                sp.dma_start(w3[:, :, :], k.given["w_conv3"].rearrange("(h p) o -> p h o", p=P)).then_inc(s_w3, 16)
                sp.dma_start(xin[:, :, :], k.given["x"].rearrange("b c n -> c b n")).then_inc(s_xin, 16)
                for b in range(B):
                    sp.wait_ge(s_add, b + 1)
                    sp.dma_start(k.d_x1[C * b:C * b + C, :], x3[:, b, :]).then_inc(s_x1, 16)
                sp.wait_ge(s_x1, 16 * B)

            @block.tensor
            def _(pe):
                pe.wait_ge(s_w3, 16)
                for b in range(B):
                    pe.wait_ge(s_norm2, b + 1)
                    if b >= 4:
                        pe.wait_ge(s_ev, b - 3)
                    for h in range(2):
                        for c, src in enumerate((k.F, k.M2)):
                            last = pe.matmul(psH[b % 4][0:C, h, :], w3[:, c, :], src[:, b, 512 * h:512 * h + 512],
                                             start=(c == 0), stop=(c == 1))
                    last.then_inc(s_h, 1)

            @block.scalar
            def _(act):
                roots2(act)
                for b in range(B):
                    act.wait_ge(s_h, b + 1)
                    act.copy(x3[:, b, :].rearrange("c (h n) -> c h n", h=2), psH[b % 4][0:C, :, :]).then_inc(s_ev, 1)
                roots3(act)

            @block.vector
            def _(v):
                normalize2(v)
                for b in range(B):
                    v.wait_ge(s_ev, b + 1)
                    for h in range(2):
                        v.bn_stats(st[:, b, h, :], x3[:, b, 512 * h:512 * h + 512]).then_inc(s_st, 1)
                v.wait_ge(s_st, 2 * B)
                for b in range(B):
                    v.bn_aggr(mv3[:, b, :], st[:, b, :, :]).then_inc(s_mv, 1)
                v.wait_ge(s_mv, B)
                normalize3(v)
                v.wait_ge(s_xin, 16)
                for b in range(B):
                    v.wait_ge(s_norm3, b + 1)
                    v.tensor_tensor(x3[:, b, :], x3[:, b, :], xin[:, b, :], ALU.add).then_inc(s_add, 1)


TOK = B * C
TB = TOK // P
KC = N // P


def token_norm(k, sb, sem, X, xn, psX, xh, xl):
    st = sb("st", [P, TB, 2, 6])
    mv = sb("mv", [P, TB, 2])
    var = sb("var", [P, TB])
    std = sb("std", [P, TB])
    r = sb("r", [P, TB])
    t = sb("t", [P, TB])
    s_st = sem("s_st")
    s_var = sem("s_var")
    s_std = sem("s_std")
    s_nchain = sem("s_nchain")
    s_xn = sem("s_xn")
    s_xT = sem("s_xT")
    s_xhi = sem("s_xhi")
    s_xlo = sem("s_xlo")

    def normalize(v):
        ch = Counted(v, s_nchain)
        for b in range(TB):
            for h in range(2):
                v.bn_stats(st[:, b, h, :], X[:, b, 512 * h:512 * h + 512]).then_inc(s_st, 1)
        v.wait_ge(s_st, 2 * TB)
        for b in range(TB):
            ch.inc(v.bn_aggr(mv[:, b, :], st[:, b, :, :]))
        v.wait_ge(s_nchain, ch.n)
        v.tensor_scalar(var[:, :], mv[:, :, 1], EPS, None, ALU.add).then_inc(s_var, 1)
        v.wait_ge(s_std, 1)
        v.wait_ge(s_var, 1)
        rsqrt(ch, v, r[:, :], t[:, :], std[:, :], var[:, :])
        for b in range(TB):
            v.tensor_scalar(xn[:, b, :], X[:, b, :], mv[:, b, 0:1], r[:, b:b + 1],
                            ALU.subtract, ALU.mult).then_inc(s_xn, 1)
        for c in range(KC):
            v.wait_ge(s_xhi, c + 1)
            v.tensor_tensor(xl[:, c, :], psX[c % 4], xh[:, c, :], ALU.subtract).then_inc(s_xlo, 1)

    def highs(act):
        act.wait_ge(s_var, 1)
        act.activation(std[:, :], var[:, :], ACT.Sqrt).then_inc(s_std, 1)
        for c in range(KC):
            act.wait_ge(s_xT, c + 1)
            act.copy(xh[:, c, :], psX[c % 4]).then_inc(s_xhi, 1)

    def turns(pe):
        pe.wait_ge(s_xn, TB)
        for c in range(KC):
            if c >= 4:
                pe.wait_ge(s_xlo, c - 3)
            for b in range(TB):
                last = pe.transpose(psX[c % 4][:, b * P:(b + 1) * P], xn[:, b, c * P:(c + 1) * P], k.id32[:, :])
            last.then_inc(s_xT, 1)

    return normalize, highs, turns, s_xlo


NH, NKV, HD = 32, 8, 128
REP = NH // NKV
def split_scales(v, ch, parts, raw):
    ch.then(v.tensor_copy(parts[0:96], raw[0:96]))
    ch.then(v.tensor_tensor(raw[0:96], raw[0:96], parts[0:96], ALU.subtract))
    ch.then(v.tensor_copy(parts[32:64], raw[32:64]))
    ch.then(v.tensor_copy(parts[64:96], raw[64:96]))
    ch.then(v.tensor_tensor(raw[64:96], raw[64:96], parts[64:96], ALU.subtract))
    return v.tensor_copy(parts[64:96], raw[64:96])


def attention(k, xh, xl, ctxh, ctxl):
    nc = k.nc
    with ExitStack() as ctx:
        sb, ps, sem = placing(k, ctx)
        QC, KV = REP * HD, 2 * HD
        NBLK = 2 * KC
        ROT = 1 + REP
        PAIRS = KC // 2
        qw = sb("qw", [P, 2, 2, QC], I32)
        kvw = sb("kvw", [P, 2, 2, KV], I32)
        rows = ctxh[:, :, :].rearrange("p h n -> p (h n)").bitcast(F32).rearrange("p (z t n) -> p z t n", z=2, t=TB)
        SLAB = 1024
        pick = sb("pick", [96, 32, P], BF16)
        raw = sb("raw", [96, SLAB])
        sc = sb("sc", [96, 2, SLAB], BF16)
        wt = sb("wt", [P, 2, QC])
        wh = sb("wh", [P, 2, KC, QC + KV], F16)
        wl = sb("wl", [P, 2, KC, QC + KV], F16)
        cos = sb("cos", [P, C])
        sin = sb("sin", [P, C])
        rc = sb("rc", [P, 2, B, C])
        rs = sb("rs", [P, 2, B, C])
        kr = sb("kr", [P, 2, B, C])
        qr = sb("qr", [P, 2, B, REP, C])
        vT = sb("vT", [P, TOK])
        V = sb("V", [P, 2, TB, HD])
        mask = sb("mask", [P, C], BF16)
        idb = sb("idb", [P, P], BF16)
        Pr = sb("Pr", [P, 2, B, C])
        top = sb("top", [P, 2, B])
        tot = sb("tot", [P, 2, B])
        inv = sb("inv", [P, 2, B])
        PT = sb("PT", [P, 2, TB, P])
        psB = [ps(f"psB{i}", [P, 512]) for i in range(2)]
        psP = [ps(f"psP{i}", [P, 512]) for i in range(2)]
        psS = ps("psS", [P, B, C])
        psT = ps("psT", [P, TB, P])
        psC = ps("psC", [P, 2, TB, 2, C])
        flat = (psS[:, :, :].rearrange("p b s -> p (b s)"), psT[:, :, :].rearrange("p b s -> p (b s)"),
                *(psC[:, i, :, :, :].rearrange("p t x s -> p (t x s)") for i in range(2)))
        normalize, highs, turns, s_xlo = token_norm(k, sb, sem, rows[:, 0], rows[:, 1], flat, xh, xl)
        s_x = sem("s_x")
        s_c = sem("s_c")
        s_pick = sem("s_pick")
        s_raw = sem("s_raw")
        s_zero = sem("s_zero")
        s_chain = sem("s_chain")
        s_sc = sem("s_sc")
        s_wq = [sem("s_wq0"), sem("s_wq1")]
        s_bc = sem("s_bc")
        s_deq = sem("s_deq")
        s_hi = sem("s_hi")
        s_lo = sem("s_lo")
        s_pr = sem("s_pr")
        s_rope = sem("s_rope")
        s_qk = sem("s_qk")
        s_vT = sem("s_vT")
        s_tr = sem("s_tr")
        s_V = sem("s_V")
        s_S = sem("s_S")
        s_soft = sem("s_soft")
        s_sub = sem("s_sub")
        s_exp = sem("s_exp")
        s_prob = sem("s_prob")
        s_PT = sem("s_PT")
        s_ctx = sem("s_ctx")
        s_ch = sem("s_ch")
        s_cl = sem("s_cl")

        def block_of(j):
            pair, r = divmod(j, 4)
            return (2 * pair + r % 2, 0, QC) if r < 2 else (2 * pair + r % 2, QC, KV)

        with nc.Block() as block:
            @block.sync
            def _(sp):
                def load(g, pair):
                    c, u = slice(2 * pair, 2 * pair + 2), pair % 2
                    sp.dma_start(qw[:, u, :, :], k.given["qw_q"].rearrange("(c p) n -> p c n", p=P)
                                 [:, c, bass.ds(g * QC, QC)]).then_inc(s_wq[u], 16)
                    for i, w in enumerate((k.given["qw_k"], k.given["qw_v"])):
                        sp.dma_start(kvw[:, u, :, HD * i:HD * i + HD], w.rearrange("(c p) n -> p c n", p=P)
                                     [:, c, bass.ds(g * HD, HD)]).then_inc(s_wq[u], 16)

                def reload(g, pair):
                    sp.wait_ge(s_deq, g * NBLK + 4 * (pair - 1))
                    load(g, pair)

                def scales(slabs):
                    for p in range(3):
                        for i, src in enumerate(slabs):
                            at = 32 * p + KC * i
                            sp.dma_start(raw[at:at + KC, :], src).then_inc(s_raw, 16)

                sp.wait_ge(s_zero, 1)
                scales([k.given["sq"][:, SLAB * i:SLAB * i + SLAB] for i in range(4)])
                sp.dma_start(rows[:, 0], k.d_x1.rearrange("(t p) n -> p t n", p=P)).then_inc(s_x, 16)
                sp.dma_start(pick[:, :, :], k.given["c_pick"]).then_inc(s_pick, 16)
                for pair in range(2):
                    load(0, pair)
                sp.wait_ge(s_sc, 1)
                scales((k.given["sk"], k.given["sv"]))
                for dst, src in ((cos, "c_cos"), (sin, "c_sin"), (mask, "c_causal"), (idb, "c_idb")):
                    sp.dma_start(dst[:, :], k.given[src]).then_inc(s_c, 16)
                for pair in range(2, PAIRS):
                    reload(0, pair)
                with sp.Fori(1, NKV) as g:
                    for pair in range(PAIRS):
                        reload(g, pair)

            @block.tensor
            def _(pe):
                pickf = pick[:, :, :].rearrange("r c n -> r (c n)")

                def spread(g, j, first=False):
                    if not first:
                        pe.wait_ge(s_deq, g * NBLK + (j - 1))
                    c, o, w = block_of(j)
                    if o == 0:
                        last = pe.matmul(psB[j % 2][:, 0:w], pickf[:, bass.ds(g // 2 * (KC * P) + c * P, P)],
                                         sc[:, 0, bass.ds(g % 2 * QC, w)], start=True, stop=True)
                    else:
                        for i in range(2):
                            last = pe.matmul(psB[j % 2][:, HD * i:HD * i + HD], pick[:, KC * i + c, :],
                                             sc[:, 1, bass.ds(g * HD, HD)], start=True, stop=True)
                    last.then_inc(s_bc, 1)

                def project(g, u, slot, first, js):
                    js = list(js)
                    if slot == (1 if first else 0):
                        pe.wait_ge(s_lo, (g + 1) * NBLK)
                    if slot == 3:
                        pe.wait_ge(s_vT, g + 1)
                    elif not (first and slot < 2):
                        pe.wait_ge(s_rope, g * ROT + {0: -1, 1: 0, 2: 1, 4: 2, 5: 3}[slot])
                    o = {0: QC, 1: QC + HD}.get(slot, (slot - 2) * HD)
                    for c in range(KC):
                        if first and slot == 0:
                            pe.wait_ge(s_lo, 4 * (c // 2) + c % 2 + 3)
                        for i, (w, x) in enumerate(((wh, xh), (wh, xl), (wl, xh))):
                            last = pe.matmul(psP[slot % 2][:, :], w[:, u, c, o:o + HD], x[:, c, :],
                                             start=(c == 0 and i == 0), stop=(c == KC - 1 and i == 2))
                        if c % 2 == 1 and js:
                            spread(g + 1, js.pop(0))
                    last.then_inc(s_pr, 1)

                def values(g, first):
                    pe.wait_ge(s_vT, g + 1)
                    if not first:
                        pe.wait_ge(s_PT, 2 * g)
                    for b in range(TB):
                        last = pe.transpose(psT[:, b, :], vT[:, b * P:(b + 1) * P], k.id32[:, :])
                    last.then_inc(s_tr, 1)

                def scores(g, u, h, first):
                    if first and h == 0:
                        pe.wait_ge(s_c, 64)
                    if h == 0:
                        pe.wait_ge(s_qk, (g + 1) * ROT)
                    if not (first and h == 0):
                        pe.wait_ge(s_sub, 2 * g + h)
                    pe.matmul(psS[:, :, :], idb[:, :], mask[:, :].unsqueeze(1).to_broadcast([P, B, C]),
                              start=True, stop=False)
                    for b in range(B):
                        last = pe.matmul(psS[:, b, :], qr[:, u, b, 2 * h:2 * h + 2, :], kr[:, u, b, :],
                                         start=False, stop=(b == B - 1))
                    last.then_inc(s_S, 1)

                def turn(g, h):
                    pe.wait_ge(s_prob, 2 * g + (h + 1))
                    if h == 0:
                        pe.wait_ge(s_V, g + 1)
                    else:
                        pe.wait_ge(s_PT, 2 * g + 1)
                    for b in range(TB):
                        last = pe.transpose(psT[:, b, :], Pr[:, h, 2 * b:2 * b + 2, :], k.id32[:, :])
                    last.then_inc(s_tr, 1)

                def context(g, u, h, first):
                    pe.wait_ge(s_PT, 2 * g + (h + 1))
                    if not (first and h == 0):
                        pe.wait_ge(s_cl, 2 * g + h)
                    for b in range(B):
                        r = slice(C * (b % 2), C * (b % 2) + C)
                        last = pe.matmul(psC[:, b % 2, b // 2, :, :], V[r, u, b // 2, :], PT[r, h, b // 2, :],
                                         start=True, stop=True)
                    last.then_inc(s_ctx, 1)

                def head(g, u, attend, ahead):
                    a, w, first = g - 1, 1 - u, attend == "first"
                    js = [range(a, b) if ahead else () for a, b in
                          ((0, 2), (2, 5), (5, 8), (8, 11), (11, 14), (14, 16))]
                    project(g, u, 0, not attend, js[0])
                    if attend:
                        scores(a, w, 0, first)
                    project(g, u, 1, not attend, js[1])
                    if attend:
                        scores(a, w, 1, first)
                    project(g, u, 2, not attend, js[2])
                    if attend:
                        turn(a, 0)
                    project(g, u, 3, not attend, js[3])
                    if attend:
                        context(a, w, 0, first)
                        turn(a, 1)
                    project(g, u, 4, not attend, js[4])
                    values(g, not attend)
                    if attend:
                        context(a, w, 1, first)
                    project(g, u, 5, not attend, js[5])

                turns(pe)
                pe.wait_ge(s_pick, 16)
                pe.wait_ge(s_sc, 2)
                for j in range(NBLK):
                    spread(0, j, j < 2)
                pe.wait_ge(s_xlo, KC)
                head(0, 0, None, True)
                head(1, 1, "first", True)
                with pe.Fori(1, NKV // 2 - 1) as t:
                    head(2 * t, 0, "later", True)
                    head(2 * t + 1, 1, "later", True)
                head(NKV - 2, 0, "later", True)
                head(NKV - 1, 1, "later", False)
                for h in range(2):
                    scores(NKV - 1, 1, h, False)
                for h in range(2):
                    turn(NKV - 1, h)
                    context(NKV - 1, 1, h, False)

            @block.vector
            def _(v):
                def dequant(g, j, first=False):
                    c, o, w = block_of(j)
                    pair = j // 4
                    if j % 4 == 0:
                        v.wait_ge(s_wq[pair % 2], g * 96 + (pair // 2 + 1) * 48)
                    v.wait_ge(s_bc, g * NBLK + (j + 1))
                    if not (first and j < 2):
                        v.wait_ge(s_lo, g * NBLK + (j - 1))
                    v.scalar_tensor_tensor(wt[:, j % 2, 0:w], (qw if o == 0 else kvw)[:, pair % 2, c % 2, :], 8.0,
                                           psB[j % 2][:, 0:w], ALU.subtract, ALU.mult).then_inc(s_deq, 1)

                def rotate(g, n, first):
                    slot = (0, 2, 3, 4, 5)[n]
                    v.wait_ge(s_pr, g * (2 + REP) + (slot + 1))
                    if not (first and n < 2):
                        v.wait_ge(s_qk, g * ROT + max(n - 1, 0))
                    x = psP[slot % 2][:, :].rearrange("p (b s) -> p b s", s=C)
                    cb = cos[:, :].unsqueeze(1).to_broadcast([P, B, C])
                    tb = sin[:, :].unsqueeze(1).to_broadcast([P, B, C])
                    H = HD // 2
                    v.tensor_tensor(rc[:, n % 2, :, :], x, cb, ALU.mult)
                    v.tensor_tensor(rs[0:H, n % 2, :, :], x[H:P], tb[H:P], ALU.mult)
                    v.tensor_tensor(rs[H:P, n % 2, :, :], x[0:H], tb[0:H], ALU.mult).then_inc(s_rope, 1)

                def soften(g, h):
                    v.wait_ge(s_S, 2 * g + (h + 1))
                    v.tensor_reduce(top[:, h, :], psS[:, :, :], AX.X, ALU.max).then_inc(s_soft, 1)
                    v.wait_ge(s_soft, 6 * g + (3 * h + 1))
                    v.tensor_tensor(Pr[:, h, :, :], psS[:, :, :], top[:, h, :].unsqueeze(2).to_broadcast([P, B, C]),
                                    ALU.subtract).then_inc(s_sub, 1)

                def probabilities(g, h):
                    v.wait_ge(s_exp, 2 * g + (h + 1))
                    v.tensor_reduce(tot[:, h, :], Pr[:, h, :, :], AX.X, ALU.add).then_inc(s_soft, 1)
                    v.wait_ge(s_soft, 6 * g + (3 * h + 2))
                    v.reciprocal(inv[:, h, :], tot[:, h, :]).then_inc(s_soft, 1)
                    v.wait_ge(s_soft, 6 * g + (3 * h + 3))
                    v.tensor_tensor(Pr[:, h, :, :], Pr[:, h, :, :], inv[:, h, :].unsqueeze(2).to_broadcast([P, B, C]),
                                    ALU.mult).then_inc(s_prob, 1)

                def rest(g, h):
                    v.wait_ge(s_ch, 2 * g + (h + 1))
                    for r in range(2):
                        hi, lo = (c[:, bass.ds(g * REP + 2 * h, 2), :]
                                  .rearrange("p x (t r s) -> p r x t s", r=2, s=C)[:, r] for c in (ctxh, ctxl))
                        last = v.tensor_tensor(lo, psC[:, r, :, :, :].rearrange("p t x s -> p x t s"), hi,
                                               ALU.subtract)
                    last.then_inc(s_cl, 1)

                def head(g, attend, ahead):
                    a, first = g - 1, not attend

                    def some(js):
                        for j in js if ahead else ():
                            dequant(g + 1, j)

                    rotate(g, 0, first)
                    if attend:
                        soften(a, 0)
                    some((0, 1, 2))
                    if attend:
                        probabilities(a, 0)
                    some((3, 4))
                    if attend:
                        soften(a, 1)
                    some((5,))
                    if attend:
                        probabilities(a, 1)
                    some((6, 7))
                    rotate(g, 1, first)
                    some((8, 9, 10))
                    rotate(g, 2, first)
                    some((11,))
                    if attend:
                        rest(a, 0)
                    some((12, 13))
                    rotate(g, 3, first)
                    if attend:
                        rest(a, 1)
                    some((14, 15))
                    rotate(g, 4, first)

                ch = Counted(v, s_chain)
                for i, loads in enumerate((12, 18)):
                    if i:
                        v.wait_ge(s_x, 16)
                        normalize(v)
                    v.wait_ge(s_raw, 16 * loads)
                    split_scales(v, ch, sc[:, i, :], raw[:, :]).then_inc(s_sc, 1)
                for j in range(NBLK):
                    dequant(0, j, True)
                v.wait_ge(s_c, 64)
                head(0, False, True)
                with v.Fori(1, NKV - 1) as g:
                    head(g, True, True)
                head(NKV - 1, True, False)
                soften(NKV - 1, 0)
                probabilities(NKV - 1, 0)
                soften(NKV - 1, 1)
                probabilities(NKV - 1, 1)
                for h in range(2):
                    rest(NKV - 1, h)

            @block.scalar
            def _(act):
                def high(g, u, j):
                    c, o, w = block_of(j)
                    act.wait_ge(s_deq, g * NBLK + (j + 1))
                    act.copy(wh[:, u, c, o:o + w], wt[:, j % 2, 0:w]).then_inc(s_hi, 1)

                def exps(g, h):
                    act.wait_ge(s_sub, 2 * g + (h + 1))
                    act.activation(Pr[:, h, :, :], Pr[:, h, :, :], ACT.Exp, scale=float(HD) ** -0.5
                                   ).then_inc(s_exp, 1)

                def turned(g, h):
                    act.wait_ge(s_tr, 3 * g + (h + 2))
                    act.copy(PT[:, h, :, :], psT[:, :, :]).then_inc(s_PT, 1)

                def outputs(g, h):
                    act.wait_ge(s_ctx, 2 * g + (h + 1))
                    for r in range(2):
                        hi = (ctxh[:, bass.ds(g * REP + 2 * h, 2), :]
                              .rearrange("p x (t r s) -> p r x t s", r=2, s=C)[:, r])
                        last = act.copy(hi, psC[:, r, :, :, :].rearrange("p t x s -> p x t s"))
                    last.then_inc(s_ch, 1)

                def head(g, u, attend, ahead):
                    a = g - 1

                    def some(js):
                        for j in js if ahead else ():
                            high(g + 1, 1 - u, j)

                    if attend:
                        exps(a, 0)
                    some((0, 1, 2, 3, 4))
                    act.wait_ge(s_pr, g * (2 + REP) + 2)
                    act.mul(vT[:, :], psP[1][:, :], 1 / WSCALE).then_inc(s_vT, 1)
                    if attend:
                        exps(a, 1)
                    some((5, 6, 7))
                    if attend:
                        turned(a, 0)
                    some((8, 9, 10))
                    if attend:
                        outputs(a, 0)
                        turned(a, 1)
                    some((11,))
                    act.wait_ge(s_tr, 3 * g + 1)
                    act.copy(V[:, u, :, :], psT[:, :, :]).then_inc(s_V, 1)
                    some((12, 13))
                    if attend:
                        outputs(a, 1)
                    some((14, 15))

                highs(act)
                for j in range(NBLK):
                    high(0, 0, j)
                head(0, 0, False, True)
                head(1, 1, True, True)
                with act.Fori(1, NKV // 2 - 1) as t:
                    head(2 * t, 0, True, True)
                    head(2 * t + 1, 1, True, True)
                head(NKV - 2, 0, True, True)
                head(NKV - 1, 1, True, False)
                for h in range(2):
                    exps(NKV - 1, h)
                for h in range(2):
                    turned(NKV - 1, h)
                    outputs(NKV - 1, h)

            @block.gpsimd
            def _(pool):
                def low(g, u, j):
                    c, o, w = block_of(j)
                    pool.wait_ge(s_hi, g * NBLK + (j + 1))
                    pool.tensor_tensor(wl[:, u, c, o:o + w], wt[:, j % 2, 0:w], wh[:, u, c, o:o + w],
                                       ALU.subtract).then_inc(s_lo, 1)

                def add(g, u, n, first):
                    if n == 0 and not first:
                        pool.wait_ge(s_S, 2 * g - 2)
                    pool.wait_ge(s_rope, g * ROT + (n + 1))
                    pool.tensor_tensor(kr[:, u, :, :] if n == 0 else qr[:, u, :, n - 1, :], rc[:, n % 2, :, :],
                                       rs[:, n % 2, :, :], ALU.add).then_inc(s_qk, 1)

                def head(g, u, first, ahead):
                    for n, js in enumerate((range(8), (8, 9, 10), (11, 12, 13), (14, 15), ())):
                        add(g, u, n, first)
                        for j in js if ahead else ():
                            low(g + 1, 1 - u, j)

                pool.memset(raw[:, :], 0.0).then_inc(s_zero, 1)
                for j in range(NBLK):
                    low(0, 0, j)
                head(0, 0, True, True)
                head(1, 1, True, True)
                with pool.Fori(1, NKV // 2 - 1) as t:
                    head(2 * t, 0, False, True)
                    head(2 * t + 1, 1, False, True)
                head(NKV - 2, 0, False, True)
                head(NKV - 1, 1, False, False)


NE, RANK = 8, 32
WA = N + RANK


def out_projection(k, X, ctxh, ctxl, fh, fl):
    nc = k.nc
    with ExitStack() as ctx:
        sb, ps, sem = placing(k, ctx)
        OCT, W, HALF = 8, 512, NH
        ow = sb("ow", [P, 2, OCT, W], I32)
        raw = sb("raw", [96, N])
        pick = sb("pick", [96, NH, P], BF16)
        sc = sb("sc", [96, 3 * W], BF16)
        zero = sb("zero", [P, W], F16)
        wt = sb("wt", [P, 4, W])
        wh = sb("wh", [P, 4, W], F16)
        wl = sb("wl", [P, 4, W], F16)
        psB = [ps(f"psB{i}", [P, 512]) for i in range(2)]
        psO = [ps(f"psO{i}", [P, 512]) for i in range(TB)]
        fw = sb("fw", [P, 2, WA])
        s_fw = [sem("s_fw0"), sem("s_fw1")]
        s_fhi = sem("s_fhi")
        s_flo = sem("s_flo")
        s_raw = sem("s_raw")
        s_chain = sem("s_chain")
        s_sc = sem("s_sc")
        s_ow = [sem("s_ow0"), sem("s_ow1")]
        s_bc = sem("s_bc")
        s_deq = sem("s_deq")
        s_hi = sem("s_hi")
        s_lo = sem("s_lo")
        s_mm = sem("s_mm")
        s_half = sem("s_half")
        s_zero = sem("s_zero")
        s_pick = sem("s_pick")
        s_xin = sem("s_xin")
        s_x = sem("s_x")

        AHEAD = 4

        def blocks(eng, each, begin=None, end=None):
            with eng.Fori(0, 2) as hf:
                if begin:
                    begin(hf)
                with eng.Fori(0, 2) as q:
                    for i in range(2 * OCT):
                        each(hf, q, i, hf * HALF + q * (2 * OCT) + i)
                if end:
                    end(hf)

        with nc.Block() as block:
            @block.sync
            def _(sp):
                for p in range(3):
                    sp.dma_start(raw[32 * p:32 * p + NH, :], k.given["so"]).then_inc(s_raw, 16)
                wo = k.given["qw_o"].rearrange("(h p) n -> p h n", p=P)
                for o in range(8):
                    if o >= 2:
                        sp.wait_ge(s_deq, OCT * (o - 1))
                    sp.dma_start(ow[:, o % 2, :, :], wo[:, o % 4 * OCT:o % 4 * OCT + OCT, o // 4 * W:o // 4 * W + W]
                                 ).then_inc(s_ow[o % 2], 16)
                    if o == 0:
                        sp.dma_start(pick[:, :, :], k.given["c_pick"]).then_inc(s_pick, 16)
                    if o == 2:
                        sp.dma_start(X[:, :, :], k.d_x1.rearrange("(t p) n -> p t n", p=P)).then_inc(s_xin, 16)
                    if o >= 2:
                        sp.wait_ge(s_flo, o - 1)
                    for c, src in ((slice(0, N), "ffn_WT"), (slice(N, WA), "ffn_A")):
                        sp.dma_start(fw[:, o % 2, c], k.given[src][o * P:(o + 1) * P, :]).then_inc(s_fw[o % 2], 16)

            @block.tensor
            def _(pe):
                pickf = pick[:, :, :].rearrange("r h n -> r (h n)")
                cf = [c[:, :, :].rearrange("p h n -> p (h n)") for c in (ctxh, ctxl)]
                pe.sem_inc(s_mm, AHEAD)

                def spread(i, h, col):
                    pe.matmul(psB[i % 2][:, :], pickf[:, bass.ds(h * P, P)], sc[:, bass.ds(col, W)],
                              start=True, stop=True).then_inc(s_bc, 1)

                def clear(start):
                    for b in range(TB):
                        mm = pe.matmul(psO[b][:, :], zero[:, 0:P], zero[:, :], start=start, stop=not start)
                    return mm

                def begin(hf):
                    pe.wait_ge(s_x, hf * TB + 1)
                    clear(True)

                def each(hf, q, i, J):
                    pe.wait_ge(s_deq, J + 1)
                    spread(i, (J + 2) % HALF, (J + 2) // HALF * W)
                    pe.wait_ge(s_lo, J + (AHEAD + 1))
                    h = q * (2 * OCT) + i
                    for b in range(TB):
                        hi, lo = (c[:, bass.ds(h * TOK + P * b, P)] for c in cf)
                        for x, w in ((hi, wh), (lo, wh), (hi, wl)):
                            mm = pe.matmul(psO[b][:, :], x, w[:, i % AHEAD, :], start=False, stop=False)
                    mm.then_inc(s_mm, 1)

                pe.wait_ge(s_zero, 1)
                pe.wait_ge(s_pick, 16)
                pe.wait_ge(s_sc, 1)
                for J in range(2):
                    spread(J, J, 0)
                blocks(pe, each, begin, lambda hf: clear(False).then_inc(s_half, 1))

            @block.vector
            def _(v):
                ch = Counted(v, s_chain)
                v.sem_inc(s_x, 1)
                v.wait_ge(s_zero, 2)
                v.wait_ge(s_raw, 48)
                split_scales(v, ch, sc[:, 0:N], raw[:, :]).then_inc(s_sc, 1)

                def each(hf, q, i, J):
                    if i % OCT == 0:
                        v.wait_ge(s_ow[i // OCT], hf * 32 + q * 16 + 16)
                    v.wait_ge(s_bc, J + 1)
                    v.wait_ge(s_lo, J + 1)
                    v.scalar_tensor_tensor(wt[:, i % AHEAD, :], ow[:, i // OCT, i % OCT, :], 8.0, psB[i % 2][:, :],
                                           ALU.subtract, ALU.mult).then_inc(s_deq, 1)
                    if i % OCT == OCT - 1:
                        c = hf * 4 + q * 2 + i // OCT
                        v.wait_ge(s_fhi, c + 1)
                        v.scalar_tensor_tensor(fl[:, bass.ds(c, 1), :].rearrange("p o n -> p (o n)"),
                                               fw[:, i // OCT, :], WSCALE,
                                               fh[:, bass.ds(c, 1), :].rearrange("p o n -> p (o n)"),
                                               ALU.mult, ALU.subtract).then_inc(s_flo, 1)

                def end(hf):
                    v.wait_ge(s_half, hf + 1)
                    v.wait_ge(s_xin, 16)
                    for b in range(TB):
                        x = X[:, b, bass.ds(hf * W, W)]
                        v.scalar_tensor_tensor(x, psO[b][:, :], 1 / WSCALE, x, ALU.mult, ALU.add).then_inc(s_x, 1)

                blocks(v, each, end=end)

            @block.scalar
            def _(act):
                def each(hf, q, i, J):
                    act.wait_ge(s_deq, J + 1)
                    act.wait_ge(s_mm, J + 1)
                    act.copy(wh[:, i % AHEAD, :], wt[:, i % AHEAD, :]).then_inc(s_hi, 1)
                    if i % OCT == OCT // 2:
                        c = hf * 4 + q * 2 + i // OCT
                        act.wait_ge(s_fw[i // OCT], hf * 64 + q * 32 + 32)
                        act.mul(fh[:, bass.ds(c, 1), :].rearrange("p o n -> p (o n)"), fw[:, i // OCT, :], WSCALE
                                ).then_inc(s_fhi, 1)

                blocks(act, each)

            @block.gpsimd
            def _(pool):
                pool.memset(zero[:, :], 0.0).then_inc(s_zero, 1)
                pool.memset(sc[:, :], 0.0).then_inc(s_zero, 1)
                pool.sem_inc(s_lo, AHEAD)

                def each(hf, q, i, J):
                    pool.wait_ge(s_hi, J + 1)
                    pool.tensor_tensor(wl[:, i % AHEAD, :], wt[:, i % AHEAD, :], wh[:, i % AHEAD, :],
                                       ALU.subtract).then_inc(s_lo, 1)

                blocks(pool, each)


def feed_forward(k, X, xh, xl, wh, wl):
    nc = k.nc
    with ExitStack() as ctx:
        sb, ps, sem = placing(k, ctx)
        bias = sb("bias", [P, N])
        bm = sb("bm", [RANK, N])
        lim = sb("lim", [NE, RANK])
        limT = sb("limT", [RANK, NE])
        odd = sb("odd", [P, 1])
        H = sb("H", [P, TB, N])
        zT = sb("zT", [RANK, TOK])
        zp = sb("zp", [RANK, TOK])
        lg = sb("lg", [P, 2, TB, NE])
        e = sb("e", [P, TB, NE])
        g = sb("g", [P, TB, NE])
        best = sb("best", [P, TB, NE])
        one = sb("one", [P, 16])
        mx = sb("mx", [P, 2])
        mxa = sb("mxa", [P, 2])
        gT = sb("gT", [NE, TOK])
        psH = [ps(f"psH{i}", [P, 512]) for i in range(4)]
        psZ = ps("psZ", [RANK, TOK])
        psD = ps("psD", [P, TB, NE])
        psG = ps("psG", [NE, TOK])
        xn = sb("xn", [P, TB, N])
        normalize, highs, turns, s_xlo = token_norm(k, sb, sem, X, xn, [h[:, :] for h in psH], xh, xl)
        s_c = sem("s_c")
        s_z = sem("s_z")
        s_zT = sem("s_zT")
        s_h = sem("s_h")
        s_H = sem("s_H")
        s_d = sem("s_d")
        s_mx = sem("s_mx")
        s_all = sem("s_all")
        s_act = sem("s_act")
        s_need = sem("s_need")
        s_chain = sem("s_chain")
        s_g = sem("s_g")
        s_gT = sem("s_gT")
        s_gc = sem("s_gc")
        s_p = sem("s_p")
        s_zp = sem("s_zp")
        s_dl = sem("s_dl")
        s_y = sem("s_y")
        s_out = sem("s_out")
        tiles = [(b, h) for h in range(2) for b in range(TB)]

        with nc.Block() as block:
            @block.sync
            def _(sp):
                sp.dma_start(bias[:, :], k.given["ffn_b"].partition_broadcast(P)).then_inc(s_c, 16)
                sp.dma_start(bm[:, :], k.given["ffn_Bmat"]).then_inc(s_c, 16)
                sp.dma_start(lim[:, :], k.given["ffn_lim"]).then_inc(s_c, 16)
                sp.dma_start(limT[:, :], k.given["ffn_limT"]).then_inc(s_c, 16)
                sp.dma_start(odd[:, :], k.given["c_odd"]).then_inc(s_c, 16)
                for i, (b, h) in enumerate(tiles):
                    sp.wait_ge(s_y, i + 1)
                    sp.dma_start(k.given["out"][b * P:(b + 1) * P, 512 * h:512 * h + 512],
                                 X[:, b, 512 * h:512 * h + 512]).then_inc(s_out, 16)
                sp.wait_ge(s_out, 16 * len(tiles))

            @block.scalar
            def _(act):
                highs(act)
                act.wait_ge(s_z, 1)
                act.mul(zT[:, :], psZ[:, :], 1 / WSCALE).then_inc(s_zT, 1)
                act.wait_ge(s_need, 1)
                act.activation(e[:, :, :], e[:, :, :], ACT.Exp).then_inc(s_act, 1)
                act.wait_ge(s_need, 2)
                act.activation(g[:, :, :], g[:, :, :], ACT.Sigmoid, scale=2.0).then_inc(s_act, 1)

            @block.gpsimd
            def _(pool):
                pool.wait_ge(s_mx, 1)
                pool.partition_all_reduce(mxa[:, :], mx[:, :], P, bass.bass_isa.ReduceOp.max).then_inc(s_all, 1)

            @block.tensor
            def _(pe):
                turns(pe)
                pe.wait_ge(s_xlo, KC)
                trio = ((xh, wh), (xl, wh), (xh, wl))
                for c in range(KC):
                    for q, (x, ww) in enumerate(trio):
                        last = pe.matmul(psZ[:, :], ww[:, c, N:WA], x[:, c, :],
                                         start=(c == 0 and q == 0), stop=(c == KC - 1 and q == 2))
                last.then_inc(s_z, 1)
                for i, (b, h) in enumerate(tiles):
                    if i >= 4:
                        pe.wait_ge(s_H, i - 3)
                    for c in range(KC):
                        for q, (x, ww) in enumerate(trio):
                            last = pe.matmul(psH[i % 4][:, :], x[:, c, b * P:(b + 1) * P],
                                             ww[:, c, 512 * h:512 * h + 512],
                                             start=(c == 0 and q == 0), stop=(c == KC - 1 and q == 2))
                    last.then_inc(s_h, 1)
                    if i == 0:
                        pe.wait_ge(s_zT, 1)
                        pe.wait_ge(s_c, 16 * 5)
                        for t in range(TB):
                            last = pe.matmul(psD[:, t, :], zT[:, t * P:(t + 1) * P], limT[:, :], start=True, stop=True)
                        last.then_inc(s_d, 1)
                pe.wait_ge(s_g, 1)
                for t in range(TB):
                    last = pe.transpose(psG[:, t * P:(t + 1) * P], g[:, t, :], k.id32[:, :])
                last.then_inc(s_gT, 1)
                pe.wait_ge(s_gc, 1)
                pe.matmul(psZ[:, :], lim[:, :], gT[:, :], start=True, stop=True).then_inc(s_p, 1)
                pe.wait_ge(s_zp, 1)
                pe.wait_ge(s_H, len(tiles))
                for i, (b, h) in enumerate(tiles):
                    if i >= 4:
                        pe.wait_ge(s_y, i - 3)
                    pe.matmul(psH[i % 4][:, :], zp[:, b * P:(b + 1) * P], bm[:, 512 * h:512 * h + 512],
                              start=True, stop=True).then_inc(s_dl, 1)

            @block.vector
            def _(v):
                ch = Counted(v, s_chain)
                normalize(v)
                v.wait_ge(s_c, 16 * 5)

                def hidden(i):
                    b, h = tiles[i]
                    v.wait_ge(s_h, i + 1)
                    v.scalar_tensor_tensor(H[:, b, 512 * h:512 * h + 512], psH[i % 4][:, :], 1 / WSCALE,
                                           bias[:, 512 * h:512 * h + 512], ALU.mult, ALU.add).then_inc(s_H, 1)

                for i in range(TB):
                    hidden(i)
                v.wait_ge(s_H, TB)
                v.wait_ge(s_d, 1)
                ch.inc(v.tensor_copy(lg[:, 0, :, :], H[:, :, 0:NE]))
                ch.then(v.tensor_copy(lg[:, 1, :, :], psD[:, :, :]))
                ch.then(v.tensor_reduce(one[:, 0:2], lg[:, :, :, :].rearrange("p h t e -> p h (t e)"), AX.X, ALU.max,
                                        apply_absolute_value=True))
                v.tensor_scalar(mx[:, :], one[:, 0:2], odd[:, :], None, ALU.mult).then_inc(s_mx, 1)
                v.wait_ge(s_all, 1)
                ch.then(v.tensor_scalar(one[:, 2:4], mxa[:, :], 1e-6, None, ALU.max))
                ch.then(v.reciprocal(one[:, 4:6], one[:, 2:4]))
                ch.then(v.tensor_scalar(e[:, :, :], lg[:, 0, :, :], one[:, 4:5], 0.5, ALU.mult, ALU.mult))
                ch.then(v.tensor_scalar(g[:, :, :], lg[:, 1, :, :], one[:, 5:6], 0.5, ALU.mult, ALU.mult))
                ch.then(v.tensor_tensor(e[:, :, :], e[:, :, :], g[:, :, :], ALU.add))
                ch.then(v.tensor_reduce(one[:, 6:10], e[:, :, :], AX.X, ALU.max))
                v.tensor_tensor(e[:, :, :], e[:, :, :], one[:, 6:10].unsqueeze(2).to_broadcast([P, TB, NE]),
                                ALU.subtract).then_inc(s_need, 1)
                v.wait_ge(s_act, 1)
                ch.then(v.tensor_reduce(one[:, 6:10], e[:, :, :], AX.X, ALU.add))
                ch.then(v.reciprocal(one[:, 10:14], one[:, 6:10]))
                ch.then(v.tensor_tensor(e[:, :, :], e[:, :, :], one[:, 10:14].unsqueeze(2).to_broadcast([P, TB, NE]),
                                        ALU.mult))
                for t in range(TB):
                    ch.inc(v.max(best[:, t, :], e[:, t, :]))
                v.wait_ge(s_chain, ch.n)
                v.tensor_tensor(g[:, :, :], e[:, :, :], best[:, :, 1:2].to_broadcast([P, TB, NE]),
                                ALU.subtract).then_inc(s_need, 1)
                v.wait_ge(s_act, 2)
                ch.then(v.tensor_tensor(g[:, :, :], e[:, :, :], g[:, :, :], ALU.mult))
                ch.then(v.tensor_reduce(one[:, 6:10], g[:, :, :], AX.X, ALU.add))
                ch.then(v.tensor_scalar(one[:, 6:10], one[:, 6:10], 1e-9, None, ALU.add))
                ch.then(v.reciprocal(one[:, 10:14], one[:, 6:10]))
                v.tensor_tensor(g[:, :, :], g[:, :, :], one[:, 10:14].unsqueeze(2).to_broadcast([P, TB, NE]),
                                ALU.mult).then_inc(s_g, 1)
                v.wait_ge(s_gT, 1)
                pairs = psG[:, :].rearrange("e (t o) -> e t o", o=2)[:, :, 1:2]
                v.tensor_copy(gT[:, :].rearrange("e (t o) -> e t o", o=2), pairs.to_broadcast([NE, TOK // 2, 2])
                              ).then_inc(s_gc, 1)
                v.wait_ge(s_p, 1)
                ch.then(v.tensor_tensor(zp[:, :], zT[:, :], psZ[:, :], ALU.mult))
                v.tensor_scalar(zp[:, :], zp[:, :], 0.5, None, ALU.mult).then_inc(s_zp, 1)
                for i in range(TB, 2 * TB):
                    hidden(i)
                v.wait_ge(s_H, 2 * TB)
                for b, h in tiles:
                    x = X[:, b, 512 * h:512 * h + 512]
                    ch.inc(v.tensor_tensor(x, x, H[:, b, 512 * h:512 * h + 512], ALU.add))
                v.wait_ge(s_chain, ch.n)
                for i, (b, h) in enumerate(tiles):
                    v.wait_ge(s_dl, i + 1)
                    x = X[:, b, 512 * h:512 * h + 512]
                    v.tensor_tensor(x, x, psH[i % 4][:, :], ALU.add).then_inc(s_y, 1)


def build(nc, given):
    k = Kernel(nc, given)
    with ExitStack() as ctx:
        sb, ps, sem = placing(k, ctx)
        k.id32 = sb("id32", [P, P])
        k.id16 = sb("id16", [P, P], F16)
        with ExitStack() as first:
            sb, ps, sem = placing(k, first)
            k.ramp = sb("ramp", [P, N], F16)
            k.F = sb("F", [P, B, N])
            k.M2 = sb("M2", [P, B, N])
            k.rank = sb("rank", [P, B * M, NB])
            mv = sb("mv", [P, B, 2])
            outputs = (C, 2 * C)
            wn = [sb(f"wn{i}", [P, 2, 2, O], F16) for i, O in enumerate(outputs)]
            wd = [sb(f"wd{i}", [C, 3, O], F16) for i, O in enumerate(outputs)]
            hb = [sb(f"hb{i}", [P, 1]) for i in range(2)]
            curve_keys(k, [(given[f"lin{i + 1}"], given[f"win{i + 1}"], given[f"w_conv{i + 1}"],
                            given[f"b_lin{i + 1}"], O, wn[i], wd[i], hb[i]) for i, O in enumerate(outputs)])
            curve_ranks(k)
            for i, (O, src) in enumerate(zip(outputs, (k.F, k.M2))):
                with ExitStack() as layer:
                    sb, ps, sem = placing(k, layer)
                    centre = sb("centre", [P, B * NB, 2, O], F16)
                    k.fT = sb("fT", [P, B, NB, P], F16)
                    split_features(k, src, centre, wd[i], O, (mv, hb[0]) if i else None)
                    edge_layer(k, centre, wn[i], O, k.M2[0:O, :, :], mv)
            points_out(k, mv, hb[1])
        nc.clear_and_free_semaphores(k.sems)
        nc.all_engine_barrier()
        with ExitStack() as second:
            sb, ps, sem = placing(k, second)
            xh = sb("xh", [P, KC, TOK], F16)
            xl = sb("xl", [P, KC, TOK], F16)
            ctxh = sb("ctxh", [P, NH, TOK], F16)
            ctxl = sb("ctxl", [P, NH, TOK], F16)
            attention(k, xh, xl, ctxh, ctxl)
            X = sb("X", [P, TB, N])
            fh = sb("fh", [P, KC, WA], F16)
            fl = sb("fl", [P, KC, WA], F16)
            out_projection(k, X, ctxh, ctxl, fh, fl)
            feed_forward(k, X, xh, xl, fh, fl)


def rope_tables():
    inv = 1.0 / np.float32(10000.0) ** (np.arange(0, HD, 2, dtype=np.float32) / np.float32(HD))
    angle = np.arange(C, dtype=np.float32)[:, None] * inv.astype(np.float32)
    cos, sin = np.cos(angle).T.astype(np.float32), np.sin(angle).T.astype(np.float32)
    scale = np.float32(1 / WSCALE)
    return np.concatenate([cos, cos]) * scale, np.concatenate([sin, -sin]) * scale


def kernel(**inputs):
    import concourse.bacc as bacc
    from concourse.bass_utils import run_bass_kernel_spmd

    a = {n: np.asarray(v) for n, v in inputs.items()}
    pick = np.zeros((96, 32, P), np.float32)
    for r in range(96):
        pick[r, r % 32] = WSCALE
    q, s = np.meshgrid(np.arange(P) % C, np.arange(C), indexing="ij")
    mkl, mkr = window_masks()
    cos, sin = rope_tables()
    arrays = {
        "x": a["x"], "coords": a["ctx_4096"][:, 0:3, :],
        "sq": a["L0_attn_scales_q"], "sk": a["L0_attn_scales_k"], "sv": a["L0_attn_scales_v"],
        "so": a["L0_attn_scales_o"], "qw_q": a["L0_attn_qw_q"], "qw_k": a["L0_attn_qw_k"],
        "qw_v": a["L0_attn_qw_v"], "qw_o": a["L0_attn_qw_o"],
        "ffn_WT": a["L0_ffn_W"].T, "ffn_b": a["L0_ffn_b"], "ffn_A": a["L0_ffn_A"], "ffn_Bmat": a["L0_ffn_Bmat"],
        "ffn_lim": a["L0_ffn_LiMEs"], "ffn_limT": a["L0_ffn_LiMEs"].T,
        "w_conv1": a["L0_xattn_W_conv1"].T, "w_conv2": a["L0_xattn_W_conv2"].T, "w_conv3": a["L0_xattn_W_conv3"].T,
        "b_lin1": a["L0_xattn_b_lin1"][:, None], "b_lin2": a["L0_xattn_b_lin2"][:, None],
        "c_id32": np.eye(P, dtype=np.float32), "c_id16": np.eye(P, dtype=np.float16),
        "c_idb": np.eye(P, dtype=np.float32).astype(NP_BF16),
        "c_ramp": np.tile(np.arange(N, dtype=np.float16), (P, 1)),
        "c_pick": pick.astype(NP_BF16), "c_mkl": mkl, "c_mkr": mkr, "c_cos": cos, "c_sin": sin,
        "c_causal": np.where(s > q, -2.0 ** 30, 0.0).astype(np.float32).astype(NP_BF16),
        "c_odd": (np.arange(P, dtype=np.float32) % 2)[:, None],
    }
    for layer, perm in ((1, [2, 0, 3, 1]), (2, [1, 3, 0, 2])):
        plain, ordered = lin_layouts(a[f"L0_xattn_W_lin{layer}"], perm)
        arrays[f"lin{layer}"], arrays[f"win{layer}"] = plain, ordered
    nc = bacc.Bacc("TRN2", target_bir_lowering=False, num_devices=1)
    arrays = {f"in_{n}": np.ascontiguousarray(v) for n, v in arrays.items()}
    t = {n[3:]: nc.dram_tensor(n, v.shape, mybir.dt.from_np(v.dtype), kind="ExternalInput").ap()
         for n, v in arrays.items()}
    t["out"] = nc.dram_tensor("out", (TOK, N), F32, kind="ExternalOutput").ap()
    build(nc, t)
    got = run_bass_kernel_spmd(nc, [arrays], core_ids=[0])
    return got.results[0]["out"].reshape(B, C, N)
```
